# Optimizing a Trainium2 kernel written in Bass

```python
import numpy as np
import jax
import jax.numpy as jnp

def _softmax(x, axis=-1):
    return jax.nn.softmax(x, axis=axis)

def _gelu(x):
    return jax.nn.gelu(x, approximate=True)

def _silu(x):
    return jax.nn.silu(x)

def _sigmoid(x):
    return jax.nn.sigmoid(x)

def _layernorm(x, axis=-1, eps=1e-05):
    m = jnp.mean(x, axis=axis, keepdims=True)
    v = jnp.var(x, axis=axis, keepdims=True)
    return (x - m) / jnp.sqrt(v + eps)

def _scatter_add(tgt, idx, src, axis=0):
    return tgt.at[idx].add(src)

def _segment_sum(src, seg, n):
    return jax.ops.segment_sum(src, seg, n)
kernel_name = 'mk_decoder_preln_d1_seqx_r8_967808'

def setup_inputs(seed: int=0):
    np.random.seed(seed)
    _w = jnp.asarray

    def _rec_inputs():
        import jax
        import jax.numpy as jnp
        _rk = jax.random.key(seed)
        x = 7.22e-05 + 1 * jax.random.normal(jax.random.fold_in(_rk, 1), (16, 56, 128), jnp.float32)
        _lenS = 56 - jax.random.randint(jax.random.fold_in(_rk, 7), (16,), 0, max(1, 56 // 4) + 1, jnp.int32)
        _lenS2 = 1500 - jax.random.randint(jax.random.fold_in(_rk, 8), (16,), 0, max(1, 1500 // 4) + 1, jnp.int32)
        _ctx_1024P = jax.random.normal(jax.random.fold_in(_rk, 11), (16, 16, 128), jnp.float32)
        _ctx_1024c = jax.random.dirichlet(jax.random.fold_in(_rk, 511), 0.3 * jnp.ones((16,), jnp.float32), (16, 1500))
        _ctx_1024t = jnp.einsum('bsk,bkd->bsd', _ctx_1024c, _ctx_1024P)
        _ctx_1024t = _ctx_1024t * jax.lax.rsqrt(jnp.mean(jnp.square(_ctx_1024t)) + 1e-12) * 0.953939
        ctx_1024 = 4.13588e-05 + 0.999923 * (_ctx_1024t + 0.3 * jax.random.normal(jax.random.fold_in(_rk, 611), (16, 1500, 128), jnp.float32))
        return (x, ctx_1024)
    x, ctx_1024 = _rec_inputs()

    def _L0_attn_setup():
        import math
        import jax, jax.numpy as jnp
        import numpy as np
        D = 128
        H = 16
        CH = 8
        EPS = 1e-05

        def _layernorm(x, w, b):
            mu = jnp.mean(x, axis=-1, keepdims=True)
            var = jnp.mean((x - mu) ** 2, axis=-1, keepdims=True)
            return (x - mu) * jax.lax.rsqrt(var + EPS) * w + b

        def _token_diffusion(x, Wqk, Wv, Wo, tau):
            b, n, d = x.shape
            dh = d // H
            qk = (x @ Wqk).reshape(b, n, H, dh).transpose(0, 2, 1, 3)
            v = (x @ Wv).reshape(b, n, H, dh).transpose(0, 2, 1, 3)
            dot = jnp.einsum('bhnd,bhmd->bhnm', qk, qk)
            q2 = jnp.sum(qk * qk, axis=-1)
            logits = (2.0 * dot - q2[..., :, None] - q2[..., None, :]) / math.sqrt(dh)
            logits = logits * tau
            attn = jax.nn.softmax(logits, axis=-1)
            out = jnp.einsum('bhnm,bhmd->bhnd', attn, v)
            out = out.transpose(0, 2, 1, 3).reshape(b, n, d)
            return out @ Wo

        def _channel_diffusion(x, Wqk, Wv, Wo, tau):
            b, n, d = x.shape
            dh = d // CH
            qk = (x @ Wqk).transpose(0, 2, 1).reshape(b, CH, dh, n)
            v = (x @ Wv).transpose(0, 2, 1).reshape(b, CH, dh, n)
            dot = jnp.einsum('bhcn,bhdn->bhcd', qk, qk)
            q2 = jnp.sum(qk * qk, axis=-1)
            logits = (2.0 * dot - q2[..., :, None] - q2[..., None, :]) / math.sqrt(n)
            logits = logits * tau
            attn = jax.nn.softmax(logits, axis=-1)
            out = jnp.einsum('bhcd,bhdn->bhcn', attn, v)
            out = out.reshape(b, d, n).transpose(0, 2, 1)
            return out @ Wo
        key = jax.random.key(seed)
        ks = jax.random.split(key, 8)
        s = 1.0 / math.sqrt(D)
        inp = {'x': jax.random.normal(ks[0], (8, 128, D), dtype=jnp.float32), 'Wqk_t': jax.random.normal(ks[1], (D, D), dtype=jnp.float32) * s, 'Wv_t': jax.random.normal(ks[2], (D, D), dtype=jnp.float32) * s, 'Wo_t': jax.random.normal(ks[3], (D, D), dtype=jnp.float32) * s, 'tau_t': jnp.ones((H, 1, 1), dtype=jnp.float32), 'Wqk_c': jax.random.normal(ks[4], (D, D), dtype=jnp.float32) * s, 'Wv_c': jax.random.normal(ks[5], (D, D), dtype=jnp.float32) * s, 'Wo_c': jax.random.normal(ks[6], (D, D), dtype=jnp.float32) * s, 'tau_c': jnp.ones((CH, 1, 1), dtype=jnp.float32), 'ln1_w': jnp.ones((D,), dtype=jnp.float32), 'ln1_b': jnp.zeros((D,), dtype=jnp.float32), 'ln2_w': jnp.ones((D,), dtype=jnp.float32), 'ln2_b': jnp.zeros((D,), dtype=jnp.float32), 'gamma1': 0.0001 * jnp.ones((D,), dtype=jnp.float32), 'gamma2': 0.0001 * jnp.ones((D,), dtype=jnp.float32)}
        return inp
    _L0_attn_all = _L0_attn_setup()
    _L0_attn_in = {k: v for k, v in _L0_attn_all.items() if k in ('Wqk_t', 'Wv_t', 'Wo_t', 'tau_t', 'Wqk_c', 'Wv_c', 'Wo_c', 'tau_c', 'ln1_w', 'ln1_b', 'ln2_w', 'ln2_b', 'gamma1', 'gamma2')}
    del _L0_attn_all

    def _L0_xattn_setup():
        import jax, jax.numpy as jnp
        import numpy as np
        D_MODEL = 128
        NUM_HEADS = 16
        DEPTH = D_MODEL // NUM_HEADS

        def _split_heads(x, B):
            return x.reshape(B, -1, NUM_HEADS, DEPTH).transpose(0, 2, 1, 3)
        key = jax.random.key(seed)
        ks = jax.random.split(key, 10)
        B, LQ, LK = (4, 256, 256)
        bound = float(np.sqrt(6.0 / (D_MODEL + D_MODEL)))

        def w(k):
            return jax.random.uniform(k, (D_MODEL, D_MODEL), jnp.float32, -bound, bound)
        return {'query': jax.random.normal(ks[0], (B, LQ, D_MODEL), jnp.float32), 'value': jax.random.normal(ks[1], (B, LK, D_MODEL), jnp.float32), 'wq': w(ks[2]), 'bq': jnp.zeros((D_MODEL,), jnp.float32), 'wk': w(ks[3]), 'bk': jnp.zeros((D_MODEL,), jnp.float32), 'wv': w(ks[4]), 'bv': jnp.zeros((D_MODEL,), jnp.float32), 'wo': w(ks[5]), 'bo': jnp.zeros((D_MODEL,), jnp.float32)}
    _L0_xattn_all = _L0_xattn_setup()
    _L0_xattn_in = {k: v for k, v in _L0_xattn_all.items() if k in ('wq', 'bq', 'wk', 'bk', 'wv', 'bv', 'wo', 'bo')}
    del _L0_xattn_all

    def _L0_ffn_setup():
        import jax, jax.numpy as jnp
        import numpy as np
        B, S, H = (2, 256, 128)
        E, I, K = (8, 512, 2)

        def _moe_forward(x, gate_w, wg, wu, wd):
            b, s, h = x.shape
            x_flat = x.reshape(-1, h)
            logits = x_flat @ gate_w.T
            top_v, top_i = jax.lax.top_k(logits, K)
            probs = jax.nn.softmax(top_v.astype(jnp.float32), axis=-1).astype(logits.dtype)
            one_hot = jax.nn.one_hot(top_i, E, dtype=probs.dtype)
            combine = jnp.einsum('tk,tke->et', probs, one_hot)

            def body(acc, ws):
                wge, wue, wde, we = ws
                hidden = jax.nn.silu(x_flat @ wge.T) * (x_flat @ wue.T)
                return (acc + we[:, None] * (hidden @ wde.T), None)
            out, _ = jax.lax.scan(body, jnp.zeros_like(x_flat), (wg, wu, wd, combine))
            return out.reshape(b, s, h)
        key = jax.random.key(seed)
        ks = jax.random.split(key, 5)
        scale_h = 1.0 / np.sqrt(H)
        scale_i = 1.0 / np.sqrt(I)
        x = jax.random.normal(ks[0], (B, S, H), dtype=jnp.float32)
        gate_w = jax.random.normal(ks[1], (E, H), dtype=jnp.float32) * scale_h
        wg = jax.random.normal(ks[2], (E, I, H), dtype=jnp.float32) * scale_h
        wu = jax.random.normal(ks[3], (E, I, H), dtype=jnp.float32) * scale_h
        wd = jax.random.normal(ks[4], (E, H, I), dtype=jnp.float32) * scale_i
        return {'x': x, 'gate_w': gate_w, 'wg': wg, 'wu': wu, 'wd': wd}
    _L0_ffn_all = _L0_ffn_setup()
    _L0_ffn_in = {k: v for k, v in _L0_ffn_all.items() if k in ('gate_w', 'wg', 'wu', 'wd')}
    del _L0_ffn_all
    return {'x': x, 'ctx_1024': ctx_1024, 'L0_attn_Wqk_t': _L0_attn_in['Wqk_t'], 'L0_attn_Wv_t': _L0_attn_in['Wv_t'], 'L0_attn_Wo_t': _L0_attn_in['Wo_t'], 'L0_attn_tau_t': _L0_attn_in['tau_t'], 'L0_attn_Wqk_c': _L0_attn_in['Wqk_c'], 'L0_attn_Wv_c': _L0_attn_in['Wv_c'], 'L0_attn_Wo_c': _L0_attn_in['Wo_c'], 'L0_attn_tau_c': _L0_attn_in['tau_c'], 'L0_attn_ln1_w': _L0_attn_in['ln1_w'], 'L0_attn_ln1_b': _L0_attn_in['ln1_b'], 'L0_attn_ln2_w': _L0_attn_in['ln2_w'], 'L0_attn_ln2_b': _L0_attn_in['ln2_b'], 'L0_attn_gamma1': _L0_attn_in['gamma1'], 'L0_attn_gamma2': _L0_attn_in['gamma2'], 'L0_xattn_wq': _L0_xattn_in['wq'], 'L0_xattn_bq': _L0_xattn_in['bq'], 'L0_xattn_wk': _L0_xattn_in['wk'], 'L0_xattn_bk': _L0_xattn_in['bk'], 'L0_xattn_wv': _L0_xattn_in['wv'], 'L0_xattn_bv': _L0_xattn_in['bv'], 'L0_xattn_wo': _L0_xattn_in['wo'], 'L0_xattn_bo': _L0_xattn_in['bo'], 'L0_ffn_gate_w': _L0_ffn_in['gate_w'], 'L0_ffn_wg': _L0_ffn_in['wg'], 'L0_ffn_wu': _L0_ffn_in['wu'], 'L0_ffn_wd': _L0_ffn_in['wd']}

def reference(x, ctx_1024, L0_attn_Wqk_t, L0_attn_Wv_t, L0_attn_Wo_t, L0_attn_tau_t, L0_attn_Wqk_c, L0_attn_Wv_c, L0_attn_Wo_c, L0_attn_tau_c, L0_attn_ln1_w, L0_attn_ln1_b, L0_attn_ln2_w, L0_attn_ln2_b, L0_attn_gamma1, L0_attn_gamma2, L0_xattn_wq, L0_xattn_bq, L0_xattn_wk, L0_xattn_bk, L0_xattn_wv, L0_xattn_bv, L0_xattn_wo, L0_xattn_bo, L0_ffn_gate_w, L0_ffn_wg, L0_ffn_wu, L0_ffn_wd):
    import jax
    import jax.numpy as jnp

    def _L0_attn_ref(x, Wqk_t, Wv_t, Wo_t, tau_t, Wqk_c, Wv_c, Wo_c, tau_c, ln1_w, ln1_b, ln2_w, ln2_b, gamma1, gamma2):
        import math
        import jax, jax.numpy as jnp
        import numpy as np
        D = 128
        H = 16
        CH = 8
        EPS = 1e-05

        def _layernorm(x, w, b):
            mu = jnp.mean(x, axis=-1, keepdims=True)
            var = jnp.mean((x - mu) ** 2, axis=-1, keepdims=True)
            return (x - mu) * jax.lax.rsqrt(var + EPS) * w + b

        def _token_diffusion(x, Wqk, Wv, Wo, tau):
            b, n, d = x.shape
            dh = d // H
            qk = (x @ Wqk).reshape(b, n, H, dh).transpose(0, 2, 1, 3)
            v = (x @ Wv).reshape(b, n, H, dh).transpose(0, 2, 1, 3)
            dot = jnp.einsum('bhnd,bhmd->bhnm', qk, qk)
            q2 = jnp.sum(qk * qk, axis=-1)
            logits = (2.0 * dot - q2[..., :, None] - q2[..., None, :]) / math.sqrt(dh)
            logits = logits * tau
            attn = jax.nn.softmax(logits, axis=-1)
            out = jnp.einsum('bhnm,bhmd->bhnd', attn, v)
            out = out.transpose(0, 2, 1, 3).reshape(b, n, d)
            return out @ Wo

        def _channel_diffusion(x, Wqk, Wv, Wo, tau):
            b, n, d = x.shape
            dh = d // CH
            qk = (x @ Wqk).transpose(0, 2, 1).reshape(b, CH, dh, n)
            v = (x @ Wv).transpose(0, 2, 1).reshape(b, CH, dh, n)
            dot = jnp.einsum('bhcn,bhdn->bhcd', qk, qk)
            q2 = jnp.sum(qk * qk, axis=-1)
            logits = (2.0 * dot - q2[..., :, None] - q2[..., None, :]) / math.sqrt(n)
            logits = logits * tau
            attn = jax.nn.softmax(logits, axis=-1)
            out = jnp.einsum('bhcd,bhdn->bhcn', attn, v)
            out = out.reshape(b, d, n).transpose(0, 2, 1)
            return out @ Wo
        x = x + _token_diffusion(_layernorm(x, ln1_w, ln1_b), Wqk_t, Wv_t, Wo_t, tau_t) * gamma1
        x = x + _channel_diffusion(_layernorm(x, ln2_w, ln2_b), Wqk_c, Wv_c, Wo_c, tau_c) * gamma2
        return x

    def _L0_xattn_ref(query, value, wq, bq, wk, bk, wv, bv, wo, bo):
        import jax, jax.numpy as jnp
        import numpy as np
        D_MODEL = 128
        NUM_HEADS = 16
        DEPTH = D_MODEL // NUM_HEADS

        def _split_heads(x, B):
            return x.reshape(B, -1, NUM_HEADS, DEPTH).transpose(0, 2, 1, 3)
        B = query.shape[0]
        q = _split_heads(query @ wq.T + bq, B)
        k = _split_heads(value @ wk.T + bk, B)
        v = _split_heads(value @ wv.T + bv, B)
        scale = jnp.sqrt(jnp.asarray(DEPTH, dtype=q.dtype))
        scores = jnp.einsum('bhqd,bhkd->bhqk', q, k) / scale
        attn = jax.nn.softmax(scores, axis=-1)
        ctx = jnp.einsum('bhqk,bhkd->bhqd', attn, v)
        ctx = ctx.transpose(0, 2, 1, 3).reshape(B, -1, D_MODEL)
        return ctx @ wo.T + bo

    def _L0_ffn_ref(x, gate_w, wg, wu, wd):
        import jax, jax.numpy as jnp
        import numpy as np
        B, S, H = (2, 256, 128)
        E, I, K = (8, 512, 2)

        def _moe_forward(x, gate_w, wg, wu, wd):
            b, s, h = x.shape
            x_flat = x.reshape(-1, h)
            logits = x_flat @ gate_w.T
            top_v, top_i = jax.lax.top_k(logits, K)
            probs = jax.nn.softmax(top_v.astype(jnp.float32), axis=-1).astype(logits.dtype)
            one_hot = jax.nn.one_hot(top_i, E, dtype=probs.dtype)
            combine = jnp.einsum('tk,tke->et', probs, one_hot)

            def body(acc, ws):
                wge, wue, wde, we = ws
                hidden = jax.nn.silu(x_flat @ wge.T) * (x_flat @ wue.T)
                return (acc + we[:, None] * (hidden @ wde.T), None)
            out, _ = jax.lax.scan(body, jnp.zeros_like(x_flat), (wg, wu, wd, combine))
            return out.reshape(b, s, h)
        return _moe_forward(x, gate_w, wg, wu, wd)
    x = x + _L0_attn_ref(_layernorm(x, axis=-1), L0_attn_Wqk_t, L0_attn_Wv_t, L0_attn_Wo_t, L0_attn_tau_t, L0_attn_Wqk_c, L0_attn_Wv_c, L0_attn_Wo_c, L0_attn_tau_c, L0_attn_ln1_w, L0_attn_ln1_b, L0_attn_ln2_w, L0_attn_ln2_b, L0_attn_gamma1, L0_attn_gamma2)
    x = x + _L0_xattn_ref(_layernorm(x, axis=-1), ctx_1024, L0_xattn_wq, L0_xattn_bq, L0_xattn_wk, L0_xattn_bk, L0_xattn_wv, L0_xattn_bv, L0_xattn_wo, L0_xattn_bo)
    x = x + _L0_ffn_ref(_layernorm(x, axis=-1), L0_ffn_gate_w, L0_ffn_wg, L0_ffn_wu, L0_ffn_wd)
    return x

_drawn_inputs = setup_inputs


def setup_inputs(seed=0):
    import zlib

    import numpy as np

    out = dict(_drawn_inputs(seed))
    spreads = {'L0_attn_tau_t': (1.0, 0.6),
     'L0_attn_tau_c': (1.0, 0.6),
     'L0_attn_ln1_w': (1.0, 0.6),
     'L0_attn_ln1_b': (0.0, 2.0),
     'L0_attn_ln2_w': (1.0, 0.6),
     'L0_attn_ln2_b': (0.0, 2.0),
     'L0_attn_gamma1': (9.999999747378752e-05, 0.6),
     'L0_attn_gamma2': (9.999999747378752e-05, 0.6),
     'L0_xattn_bq': (0.0, 0.415),
     'L0_xattn_bk': (0.0, 2.0),
     'L0_xattn_bv': (0.0, 0.1),
     'L0_xattn_bo': (0.0, 0.1)}
    factors = {'L0_attn_Wqk_t': 64.0,
     'L0_attn_Wv_t': 37.326,
     'L0_attn_Wo_t': 35.196,
     'L0_attn_Wqk_c': 8.0,
     'L0_attn_Wv_c': 39.67,
     'L0_attn_Wo_c': 37.194}
    for name, (base, spread) in spreads.items():
        noise = np.random.default_rng([zlib.crc32(name.encode()), seed]).standard_normal(out[name].shape)
        drawn = base * np.exp(spread * noise) if base else spread * noise
        out[name] = jnp.asarray(drawn.astype(out[name].dtype))
    for name, factor in factors.items():
        out[name] = (out[name] * factor).astype(out[name].dtype)
    return out
```

```python
from contextlib import ExitStack

import numpy as np

import concourse.bass as bass
from concourse import mybir

F32 = mybir.dt.float32
F32R = mybir.dt.float32r
ALU = mybir.AluOpType
ACT = mybir.ActivationFunctionType
AX = mybir.AxisListType

B, N, D, S = 16, 56, 128, 1500
H, DH = 16, 8
CH, CD = 8, 16
E, I = 8, 512
EPS = 1e-5

PAIRS = B // 2
PITCH = 64
HQ = H * N
HALF = HQ // 2
KT, KR = 12, S // 12
KC = 3
KW = S // KC
QT7 = HQ // 128
IT = I // 128
GROUPS = [(0, 3), (3, 3), (6, 2), (8, 3), (11, 3), (14, 2)]
SHIFT_ROW = 3 * DH
OFF_BLOCK = -1e30

MATS = ["Wqk_t", "Wv_t", "Wo_t", "Wqk_c", "Wv_c", "Wo_c", "wq", "wk", "wv", "wo0", "wo1", "wo2", "wo3"]
ROWS = ["gamma1", "gamma2", "bv", "bo"]
COLS = ["ln1_w", "ln1_b", "ln2_w", "ln2_b", "bq", "bk", "tau_t", "tau_c"]


class Steps:

    def __init__(self, engine, sem):
        self.engine, self.sem, self.base, self.n = engine, sem, 0, 0

    def mark(self, instruction):
        instruction.then_inc(self.sem, 1)
        self.n += 1

    def wait(self):
        self.engine.wait_ge(self.sem, self.base + self.n)

    def again(self, engine):
        self.engine = engine
        return self

    def enter(self, i, per):
        self.outer = self.base + self.n
        self.base, self.n = self.outer + i * per, 0

    def leave(self, trips, per):
        assert self.n == per, self.n
        self.base, self.n = self.outer + trips * per, 0


def shape_constants():
    row = np.arange(128)
    ident = np.eye(128)
    head = (row[:, None] // DH == np.arange(H)[None, :]) * 1.0
    place = np.zeros(H, int)
    for h0, n in GROUPS:
        place[h0:h0 + n] = np.arange(n)
    sel = np.zeros((2, 128, 128))
    for h in range(H):
        for d in range(DH):
            for q in range(4):
                sel[q // 2, h * DH + d, 32 * q + place[h] * DH + d] = 1.0
    den = (row[:, None] == 32 * (row[None, :] // 32) + 16) * 1.0
    quarter = (row[:, None] // DH % 4 == np.arange(4)[None, :]) * 1.0
    block = np.where(row[:, None] // CD == row[None, :] // CD, 0.0, OFF_BLOCK)
    before = np.broadcast_to((np.arange(E)[None, :] < np.arange(E)[:, None]) * 1.0, (128, E, E)).reshape(128, -1)
    parts = {"ident": ident, "neg_ident": -ident, "sel_hi": sel[0], "sel_lo": sel[1], "den": den, "block": block,
             "ones": np.ones((128, 128)), "head": head, "quarter": quarter, "before": before}
    at, lots, n = {}, [], 0
    for name, a in parts.items():
        at[name] = (n, a.shape[1])
        lots.append(a.astype(np.float32))
        n += a.shape[1]
    return np.concatenate(lots, axis=1), at


def build(nc, x_in, ctx_in, mats_in, rows_in, cols_in, gate_in, consts_in, const_at, wgu_in, wd_in, out):
    ctx = ExitStack()
    with ctx:
        def sb(name, shape, dt=F32):
            return ctx.enter_context(nc.sbuf_tensor(name, shape, dt))

        def sem(name):
            return ctx.enter_context(nc.semaphore(name))

        PS = ctx.enter_context(nc.psum_tensor("PS", [128, 8, 512], F32))

        X = sb("X", [128, PAIRS, D])
        mats = sb("mats", [128, len(MATS), D])
        rows = sb("rows", [128, len(ROWS), D])
        cols = sb("cols", [128, len(COLS)])
        gate = sb("gate", [128, E])
        consts = sb("consts", [128, consts_in.shape[1]])
        MAT = {n: mats[:, k, :] for k, n in enumerate(MATS)}
        ROW = {n: rows[:, k, :] for k, n in enumerate(ROWS)}
        COL = {n: cols[:, k:k + 1] for k, n in enumerate(COLS)}
        C = {n: consts[:, a:a + w] for n, (a, w) in const_at.items()}
        stats = sb("stats", [128, PAIRS, 6])
        moments = sb("moments", [128, PAIRS, 2])
        rstd = sb("rstd", [128, PAIRS])
        minus_half = sb("minus_half", [128, PAIRS])
        T = sb("T", [128, PAIRS * 128])
        Tb = T[:, :].rearrange("p (b n) -> p b n", n=PITCH)

        x_loaded = sem("x_loaded")
        consts_loaded = sem("consts_loaded")
        weights_loaded = sem("weights_loaded")
        dve_steps = sem("dve_steps")
        act_steps = sem("act_steps")
        pool_steps = sem("pool_steps")
        moments_ready = sem("moments_ready")
        eps_added = sem("eps_added")
        rstd_ready = sem("rstd_ready")

        steps_of = {}

        def layernorm(dve, step, number, src, dst):
            for p in range(PAIRS):
                last = nc.vector.bn_stats(out=stats[:, p, :], in_=src[:, p, :])
            step.mark(last)
            step.wait()
            for p in range(PAIRS):
                last = nc.vector.bn_aggr(out=moments[:, p, :], in_=stats[:, p, :])
            last.then_inc(moments_ready, 1)
            dve.wait_ge(rstd_ready, number + 1)
            for p in range(PAIRS):
                last = nc.vector.tensor_scalar(dst[:, p, :], src[:, p, :], moments[:, p, 0:1], rstd[:, p:p + 1],
                                               ALU.subtract, ALU.mult)
            return last

        def layernorm_power(pool, number):
            pool.wait_ge(moments_ready, number + 1)
            nc.gpsimd.tensor_scalar(rstd[:, :], moments[:, :, 1], EPS, None, ALU.add).then_inc(eps_added, 1)
            pool.wait_ge(eps_added, number + 2)
            nc.gpsimd.tensor_tensor(rstd[:, :], rstd[:, :], minus_half[:, :], ALU.pow).then_inc(rstd_ready, 1)

        def pipelined(engine, body, count):
            body(0, 0, 0)
            with engine.Fori(0, (count - 4) // 2) as i:
                body(2 * i + 1, 1, i)
                body(2 * i + 2, 0, i + 1)
            for n in range(count - 3, count):
                body(n, n % 2, n // 2)

        def exists(n, count):
            return not isinstance(n, int) or n < count

        def later(n, first):
            return not isinstance(n, int) or n >= first

        s1 = ExitStack()

        def sb1(name, shape, dt=F32):
            return s1.enter_context(nc.sbuf_tensor(name, shape, dt))

        with s1:
            Z = sb1("Z", [128, PAIRS, D])
            Y = sb1("Y", [128, PAIRS, D])
            qkT = sb1("qkT", [128, PAIRS * 128])
            v_all = sb1("v_all", [N, B, D])
            coef = sb1("coef", [128, 3])
            scaled = sb1("scaled", [128, PAIRS * 128])
            squared = sb1("squared", [128, PAIRS * 128])
            qk_pair = sb1("qk_pair", [128, 2, 128])
            v_pair = sb1("v_pair", [N, 2, 2, D])
            q_block = sb1("q_block", [128, 2, 2, HQ])
            q_square = sb1("q_square", [128, 2, 2, HQ])
            row_max = sb1("row_max", [128, 2, H])
            row_sum = sb1("row_sum", [128, 2, H])
            probs = sb1("probs", [128, 2, HQ])
            probsT = sb1("probsT", [N, 2, H, 128])
            heads_out = sb1("heads_out", [128, 2, 2, 4 * PITCH])
            wo_quarter = sb1("wo_quarter", [128, 4, D])
            wo_scaled = sb1("wo_scaled", [128, 2, D])
            qk2 = sb1("qk2", [128, PAIRS, D])
            qk_c = sb1("qk_c", [128, PAIRS, D])
            negsq_c = sb1("negsq_c", [128, PAIRS, D])
            gram = sb1("gram", [128, B, D])
            gmax = sb1("gmax", [128, B])
            gsum = sb1("gsum", [128, B])

            y_ready = sem("y_ready")
            y_turned = sem("y_turned")
            y_copied = sem("y_copied")
            coef_ready = sem("coef_ready")
            wo_ready = sem("wo_ready")
            qk_projected = sem("qk_projected")
            qk_read = sem("qk_read")
            v1_projected = sem("v1_projected")
            v_all_ready = sem("v_all_ready")
            scaled_ready = sem("scaled_ready")
            qk_copied = sem("qk_copied")
            v_copied = sem("v_copied")
            blocks_dve = sem("blocks_dve")
            blocks_pool = sem("blocks_pool")
            logits_done = sem("logits_done")
            max_done = sem("max_done")
            shifted_ready = sem("shifted_ready")
            exp_ready = sem("exp_ready")
            sum_done = sem("sum_done")
            inverse_done = sem("inverse_done")
            probs_ready = sem("probs_ready")
            turned = sem("turned")
            turned_copied = [sem("turned_copied_0"), sem("turned_copied_1")]
            pv1_done = sem("pv1_done")
            pv1_copied = sem("pv1_copied")
            out1_done = sem("out1_done")
            out1_added = sem("out1_added")
            qkc_projected = sem("qkc_projected")
            qkc_ready = sem("qkc_ready")
            squares_c = sem("squares_c")
            vc_projected = sem("vc_projected")
            vc_ready = sem("vc_ready")
            gram_done = sem("gram_done")
            gram_shifted = sem("gram_shifted")
            gram_exp = sem("gram_exp")
            gram_ready = sem("gram_ready")
            mixed = sem("mixed")
            mixed_copied = sem("mixed_copied")
            outc_done = sem("outc_done")
            x1_ready = sem("x1_ready")

            TURN = PS[0:N, 4:6, :]
            HEADS = PS[:, 6, :]
            OUT1 = PS[:, 7, 0:D]

            def batch_block(src, p, e):
                v = src[:, :].rearrange("q (b n) -> q b n", n=PITCH)
                return v[:, bass.ds(2 * p + e, 1), 0:N].broadcast_to([128, H, N])

            def by_head(tile):
                return tile.rearrange("p (h n) -> p h n", n=N)

            HEAD_MASK = C["head"].unsqueeze(2).broadcast_to([128, H, N])

            with nc.Block() as block:

                @block.sync
                def _(sp):
                    sp.dma_start(X[:, :, :], x_in).then_inc(x_loaded, 16)
                    sp.dma_start(consts[:, :], consts_in).then_inc(consts_loaded, 16)
                    sp.dma_start(cols[:, :], cols_in).then_inc(consts_loaded, 16)
                    sp.dma_start(rows[:, :, :], rows_in).then_inc(consts_loaded, 16)
                    sp.dma_start(mats[:, :, :], mats_in).then_inc(weights_loaded, 16)
                    sp.dma_start(gate[:, :], gate_in).then_inc(weights_loaded, 16)

                @block.gpsimd
                def _(pool):
                    nc.gpsimd.memset(minus_half[:, :], -0.5).then_inc(eps_added, 1)
                    layernorm_power(pool, 0)
                    layernorm_power(pool, 1)
                    pool.wait_ge(consts_loaded, 48)
                    pool.wait_ge(scaled_ready, 1)

                    def blocks(p, j):
                        if later(p, 2):
                            pool.wait_ge(logits_done, p - 1)
                        nc.gpsimd.tensor_tensor(by_head(q_block[:, j, 0, :]), batch_block(scaled, p, 0), HEAD_MASK, ALU.mult)
                        for e in range(2):
                            last = nc.gpsimd.tensor_tensor(by_head(q_square[:, j, e, :]), batch_block(squared, p, e),
                                                           HEAD_MASK, ALU.mult)
                        last.then_inc(blocks_pool, 1)

                    for p in range(3):
                        blocks(p, p % 2)

                    def turn(p, j, u):
                        if exists(p + 3, PAIRS):
                            blocks(p + 3, 1 - j)

                    pipelined(pool, turn, PAIRS)
                    layernorm_power(pool, 2)

                @block.scalar
                def _(act):
                    act.wait_ge(consts_loaded, 48)
                    for c in range(2):
                        act.wait_ge(y_turned, c + 1)
                        nc.scalar.activation(T[:, c * 512:(c + 1) * 512], PS[:, c, :], ACT.Identity,
                                             bias=COL["ln1_b"], scale=COL["ln1_w"]).then_inc(y_copied, 1)
                    for c in range(2):
                        act.wait_ge(qk_projected, c + 1)
                        nc.scalar.copy(qkT[:, c * 512:(c + 1) * 512], PS[:, 2 + c, :]).then_inc(qk_read, 1)
                    act.wait_ge(qk_read, 2)

                    def copy_qk(p, j):
                        if later(p, 2):
                            act.wait_ge(logits_done, p - 1)
                        nc.scalar.copy(qk_pair[:, j, :], qkT[:, bass.ts(p, 128)]).then_inc(qk_copied, 1)

                    def copy_v(p, j):
                        nc.scalar.copy(v_pair[:, j, :, :], v_all[:, bass.ts(p, 2), :]).then_inc(v_copied, 1)

                    def exp(p, j):
                        act.wait_ge(shifted_ready, p + 1)
                        nc.scalar.activation(probs[:, j, :], probs[:, j, :], ACT.Exp).then_inc(exp_ready, 1)

                    copy_qk(0, 0)
                    copy_qk(1, 1)
                    for c in range(4):
                        act.wait_ge(v1_projected, c + 1)
                        nc.scalar.copy(v_all[:, 4 * c:4 * c + 4, :],
                                       PS[0:N, 4 + c, :].rearrange("p (b d) -> p b d", b=4)).then_inc(v_all_ready, 1)
                    act.wait_ge(v_all_ready, 4)
                    copy_v(0, 0)
                    copy_v(1, 1)
                    exp(0, 0)

                    def turn(p, j, u):
                        if exists(p + 2, PAIRS):
                            copy_qk(p + 2, j)
                        for a in range(2):
                            act.wait_ge(turned, 2 * p + a + 1)
                            nc.scalar.copy(probsT[:, j, 8 * a:8 * a + 8, :], TURN.rearrange("p a (h n) -> p (a h) n", h=4)
                                           ).then_inc(turned_copied[a], 1)
                            if a == 0 and exists(p + 1, PAIRS):
                                exp(p + 1, 1 - j)
                        act.wait_ge(pv1_done, p + 1)
                        nc.scalar.copy(heads_out[:, j, :, :], HEADS.rearrange("p (e n) -> p e n", e=2)
                                       ).then_inc(pv1_copied, 1)
                        if exists(p + 2, PAIRS):
                            copy_v(p + 2, j)

                    pipelined(act, turn, PAIRS)

                    for c in range(2):
                        act.wait_ge(y_turned, c + 3)
                        nc.scalar.activation(T[:, c * 512:(c + 1) * 512], PS[:, c, :], ACT.Identity,
                                             bias=COL["ln2_b"], scale=COL["ln2_w"]).then_inc(y_copied, 1)
                    for c in range(2):
                        act.wait_ge(qkc_projected, c + 1)
                        nc.scalar.copy(qk_c[:, 4 * c:4 * c + 4, :],
                                       PS[:, 2 + c, :].rearrange("p (b d) -> p b d", b=4)).then_inc(qkc_ready, 1)
                    for c in range(2):
                        act.wait_ge(vc_projected, c + 1)
                        nc.scalar.copy(qkT[:, c * 512:(c + 1) * 512], PS[:, 4 + c, :]).then_inc(vc_ready, 1)
                    for c in range(2):
                        act.wait_ge(gram_shifted, c + 1)
                        nc.scalar.activation(gram[:, 8 * c:8 * c + 8, :], gram[:, 8 * c:8 * c + 8, :], ACT.Exp
                                             ).then_inc(gram_exp, 1)
                    for c in range(2):
                        act.wait_ge(mixed, c + 1)
                        nc.scalar.copy(gram[:, 8 * c:8 * c + 8, :],
                                       PS[:, 2 * c:2 * c + 2, :].rearrange("p a (b d) -> p (a b) d", b=4)
                                       ).then_inc(mixed_copied, 1)

                @block.vector
                def _(dve):
                    step = Steps(dve, dve_steps)
                    steps_of["dve"] = step
                    dve.wait_ge(x_loaded, 16)
                    step.mark(layernorm(dve, step, 0, X, Z))
                    step.wait()
                    layernorm(dve, step, 1, Z, Y).then_inc(y_ready, 1)
                    dve.wait_ge(consts_loaded, 48)
                    nc.vector.tensor_scalar(coef[:, 0:1], COL["tau_t"], 2.0 / DH ** 0.5, None, ALU.mult)
                    nc.vector.tensor_scalar(coef[:, 1:2], COL["tau_t"], -1.0 / DH ** 0.5, None, ALU.mult)
                    nc.vector.tensor_scalar(coef[:, 2:3], COL["tau_c"], 1.0 / N ** 0.5, None, ALU.mult
                                            ).then_inc(coef_ready, 1)
                    dve.wait_ge(coef_ready, 1)
                    dve.wait_ge(qk_read, 2)
                    nc.vector.tensor_scalar(scaled[:, :], qkT[:, :], coef[:, 0:1], None, ALU.mult)
                    nc.vector.scalar_tensor_tensor(squared[:, :], qkT[:, :], coef[:, 1:2], qkT[:, :], ALU.mult, ALU.mult
                                                   ).then_inc(scaled_ready, 1)

                    def blocks(p, j):
                        if later(p, 2):
                            dve.wait_ge(logits_done, p - 1)
                        nc.vector.tensor_tensor(by_head(q_block[:, j, 1, :]), batch_block(scaled, p, 1), HEAD_MASK, ALU.mult
                                                ).then_inc(blocks_dve, 1)

                    def logit_half(j, a):
                        return by_head(PS[:, 2 * j + a, 0:HALF])

                    def shift(p, j):
                        dve.wait_ge(logits_done, p + 1)
                        for a in range(2):
                            last = nc.vector.tensor_reduce(out=row_max[:, j, 8 * a:8 * a + 8], in_=logit_half(j, a),
                                                           axis=AX.X, op=ALU.max)
                        last.then_inc(max_done, 1)
                        dve.wait_ge(max_done, p + 1)
                        if later(p, 2):
                            dve.wait_ge(turned, 2 * (p - 1))
                        for a in range(2):
                            last = nc.vector.tensor_tensor(
                                by_head(probs[:, j, a * HALF:(a + 1) * HALF]), logit_half(j, a),
                                row_max[:, j, 8 * a:8 * a + 8].unsqueeze(2).broadcast_to([128, 8, N]), ALU.subtract)
                        last.then_inc(shifted_ready, 1)

                    def normalise(p, j):
                        dve.wait_ge(exp_ready, p + 1)
                        tile = by_head(probs[:, j, :])
                        nc.vector.tensor_reduce(out=row_sum[:, j, :], in_=tile, axis=AX.X, op=ALU.add).then_inc(sum_done, 1)
                        dve.wait_ge(sum_done, p + 1)
                        nc.vector.reciprocal(row_sum[:, j, :], row_sum[:, j, :]).then_inc(inverse_done, 1)
                        dve.wait_ge(inverse_done, p + 1)
                        nc.vector.tensor_tensor(tile, tile, row_sum[:, j, :].unsqueeze(2).broadcast_to([128, H, N]),
                                                ALU.mult).then_inc(probs_ready, 1)

                    dve.wait_ge(scaled_ready, 1)
                    for p in range(3):
                        blocks(p, p % 2)
                        if p == 0:
                            dve.wait_ge(weights_loaded, 32)
                            nc.vector.tensor_tensor(wo_scaled[:, 0, :], MAT["Wo_t"], ROW["gamma1"], ALU.mult)
                            step.mark(nc.vector.tensor_tensor(wo_scaled[:, 1, :], MAT["Wo_c"], ROW["gamma2"], ALU.mult))
                            step.wait()
                            for k in range(4):
                                last = nc.vector.tensor_scalar(wo_quarter[:, k, :], wo_scaled[:, 0, :],
                                                               C["quarter"][:, k:k + 1], None, ALU.mult)
                            last.then_inc(wo_ready, 1)
                    shift(0, 0)
                    normalise(0, 0)

                    def turn(p, j, u):
                        if exists(p + 1, PAIRS):
                            shift(p + 1, 1 - j)
                        if exists(p + 3, PAIRS):
                            blocks(p + 3, 1 - j)
                        if exists(p + 1, PAIRS):
                            normalise(p + 1, 1 - j)
                        dve.wait_ge(out1_done, p + 1)
                        nc.vector.tensor_tensor(Z[:, bass.ds(p, 1), :], Z[:, bass.ds(p, 1), :], OUT1.unsqueeze(1), ALU.add
                                                ).then_inc(out1_added, 1)

                    pipelined(dve, turn, PAIRS)

                    dve.wait_ge(out1_added, PAIRS)
                    layernorm(dve, step, 2, Z, Y).then_inc(y_ready, 1)
                    step.mark(nc.vector.tensor_tensor(X[:, :, :], X[:, :, :], Z[:, :, :], ALU.add))
                    for c in range(2):
                        dve.wait_ge(qkc_ready, c + 1)
                        tiles = slice(4 * c, 4 * c + 4)
                        nc.vector.tensor_scalar(qk2[:, tiles, :], qk_c[:, tiles, :], 2.0, None, ALU.mult)
                        nc.vector.scalar_tensor_tensor(negsq_c[:, tiles, :], qk_c[:, tiles, :], -1.0, qk_c[:, tiles, :],
                                                       ALU.mult, ALU.mult).then_inc(squares_c, 1)
                    mask = C["block"].unsqueeze(1).broadcast_to([128, 8, D])
                    for c in range(2):
                        part = gram[:, 8 * c:8 * c + 8, :]
                        dve.wait_ge(gram_done, c + 1)
                        step.mark(nc.vector.scalar_tensor_tensor(
                            part, PS[:, 2 * c:2 * c + 2, :].rearrange("p a (b d) -> p (a b) d", b=4), coef[:, 2:3], mask,
                            ALU.mult, ALU.add))
                        step.wait()
                        step.mark(nc.vector.tensor_reduce(out=gmax[:, 8 * c:8 * c + 8], in_=part, axis=AX.X, op=ALU.max))
                        step.wait()
                        nc.vector.tensor_tensor(part, part, gmax[:, 8 * c:8 * c + 8].unsqueeze(2).broadcast_to([128, 8, D]),
                                                ALU.subtract).then_inc(gram_shifted, 1)
                    for c in range(2):
                        part, total = gram[:, 8 * c:8 * c + 8, :], gsum[:, 8 * c:8 * c + 8]
                        dve.wait_ge(gram_exp, c + 1)
                        step.mark(nc.vector.tensor_reduce(out=total, in_=part, axis=AX.X, op=ALU.add))
                        step.wait()
                        step.mark(nc.vector.reciprocal(total, total))
                        step.wait()
                        nc.vector.tensor_tensor(part, part, total.unsqueeze(2).broadcast_to([128, 8, D]), ALU.mult
                                                ).then_inc(gram_ready, 1)
                    for c in range(2):
                        dve.wait_ge(outc_done, c + 1)
                        nc.vector.tensor_tensor(X[:, 4 * c:4 * c + 4, :], X[:, 4 * c:4 * c + 4, :],
                                                PS[:, 4 + c, :].rearrange("p (b d) -> p b d", b=4), ALU.add
                                                ).then_inc(x1_ready, 1)
                    dve.wait_ge(x1_ready, 2)

                @block.tensor
                def _(pe):
                    def turn_tokens():
                        for c in range(2):
                            for p in range(4):
                                last = nc.tensor.transpose(PS[:, c, 128 * p:128 * p + 128], Y[:, 4 * c + p, :], C["ident"])
                            last.then_inc(y_turned, 1)

                    pe.wait_ge(consts_loaded, 48)
                    pe.wait_ge(y_ready, 1)
                    turn_tokens()
                    pe.wait_ge(weights_loaded, 32)
                    for c in range(2):
                        pe.wait_ge(y_copied, c + 1)
                        nc.tensor.matmul(PS[:, 2 + c, :], MAT["Wqk_t"], T[:, c * 512:(c + 1) * 512], start=True, stop=True
                                         ).then_inc(qk_projected, 1)
                    for b in range(B):
                        mm = nc.tensor.matmul(PS[0:N, 4 + b // 4, 128 * (b % 4):128 * (b % 4) + 128], Tb[:, b, 0:N],
                                              MAT["Wv_t"], start=True, stop=True)
                        if b % 4 == 3:
                            mm.then_inc(v1_projected, 1)

                    def logits(p, j):
                        pe.wait_ge(blocks_dve, p + 1)
                        pe.wait_ge(blocks_pool, p + 1)
                        pe.wait_ge(qk_copied, p + 1)
                        if later(p, 2):
                            pe.wait_ge(shifted_ready, p - 1)
                        for a in range(2):
                            for e in range(2):
                                nc.tensor.matmul(PS[PITCH * e:PITCH * e + PITCH, 2 * j + a, 0:HALF],
                                                 qk_pair[:, j, PITCH * e:PITCH * e + PITCH],
                                                 q_block[:, j, e, a * HALF:(a + 1) * HALF], start=True, stop=False)
                            for e in range(2):
                                last = nc.tensor.matmul(PS[PITCH * e:PITCH * e + PITCH, 2 * j + a, 0:HALF],
                                                        C["ones"][:, 0:PITCH],
                                                        q_square[:, j, e, a * HALF:(a + 1) * HALF], start=False, stop=True)
                        last.then_inc(logits_done, 1)

                    def turn_probs(p, j, a):
                        pe.wait_ge(consts_loaded, 48)
                        if a == 0:
                            pe.wait_ge(probs_ready, p + 1)
                        else:
                            pe.wait_ge(turned_copied[0], p + 1)
                        for h in range(8):
                            last = nc.tensor.transpose(PS[0:N, 4 + h // 4, 128 * (h % 4):128 * (h % 4) + 128],
                                                       probs[:, j, (8 * a + h) * N:(8 * a + h + 1) * N], C["ident"])
                        last.then_inc(turned, 1)

                    def attend(p, j):
                        pe.wait_ge(v_all_ready, 4)
                        pe.wait_ge(v_copied, p + 1)
                        pe.wait_ge(turned_copied[1], p + 1)
                        for e in range(2):
                            for k in range(4):
                                last = nc.tensor.matmul(
                                    PS[32 * k:32 * k + 32, 6, 256 * e:256 * e + 256], v_pair[:, j, e, 32 * k:32 * k + 32],
                                    probsT[:, j, 4 * k:4 * k + 4, PITCH * e:PITCH * e + PITCH], start=True, stop=True)
                        last.then_inc(pv1_done, 1)

                    def project_heads(p, j):
                        pe.wait_ge(pv1_copied, p + 1)
                        if later(p, 1):
                            pe.wait_ge(out1_added, p)
                        for k in range(4):
                            for e in range(2):
                                last = nc.tensor.matmul(PS[PITCH * e:PITCH * e + PITCH, 7, 0:D],
                                                        heads_out[:, j, e, PITCH * k:PITCH * k + PITCH], wo_quarter[:, k, :],
                                                        start=(k == 0), stop=(k == 3))
                        last.then_inc(out1_done, 1)

                    logits(0, 0)
                    logits(1, 1)
                    pe.wait_ge(v_all_ready, 4)
                    pe.wait_ge(wo_ready, 1)

                    def turn(p, j, u):
                        if exists(p + 2, PAIRS):
                            logits(p + 2, j)
                        turn_probs(p, j, 0)
                        turn_probs(p, j, 1)
                        attend(p, j)
                        project_heads(p, j)

                    pipelined(pe, turn, PAIRS)

                    pe.wait_ge(y_ready, 2)
                    turn_tokens()
                    pe.wait_ge(y_copied, 4)
                    for p in range(PAIRS):
                        mm = nc.tensor.matmul(PS[:, 2 + p // 4, 128 * (p % 4):128 * (p % 4) + 128],
                                              T[:, 128 * p:128 * p + 128], MAT["Wqk_c"], start=True, stop=True)
                        if p % 4 == 3:
                            mm.then_inc(qkc_projected, 1)
                    for c in range(2):
                        nc.tensor.matmul(PS[:, 4 + c, :], MAT["Wv_c"], T[:, c * 512:(c + 1) * 512], start=True, stop=True
                                         ).then_inc(vc_projected, 1)
                    pe.wait_ge(squares_c, 2)
                    for e in range(2):
                        for p in range(PAIRS):
                            r = slice(PITCH * e, PITCH * e + N)
                            o = PS[:, 2 * e + p // 4, 128 * (p % 4):128 * (p % 4) + 128]
                            nc.tensor.matmul(o, qk2[r, p, :], qk_c[r, p, :], start=True, stop=False)
                            last = nc.tensor.matmul(o, C["ones"][r, :], negsq_c[r, p, :], start=False, stop=True)
                        last.then_inc(gram_done, 1)
                    for c in range(2):
                        pe.wait_ge(gram_ready, c + 1)
                        for g in range(8 * c, 8 * c + 8):
                            last = nc.tensor.matmul(PS[:, g // 4, 128 * (g % 4):128 * (g % 4) + 128], gram[:, g, :],
                                                    wo_scaled[:, 1, :], start=True, stop=True)
                        last.then_inc(mixed, 1)
                    pe.wait_ge(mixed_copied, 2)
                    pe.wait_ge(vc_ready, 2)
                    for c in range(2):
                        for p in range(4 * c, 4 * c + 4):
                            for e in range(2):
                                last = nc.tensor.matmul(
                                    PS[PITCH * e:PITCH * e + PITCH, 4 + c, 128 * (p % 4):128 * (p % 4) + 128],
                                    qkT[:, 128 * p + PITCH * e:128 * p + PITCH * e + PITCH], gram[:, 8 * e + p, :], start=True, stop=True)
                        last.then_inc(outc_done, 1)

        s2 = ExitStack()

        def sb2(name, shape, dt=F32):
            return s2.enter_context(nc.sbuf_tensor(name, shape, dt))

        with s2:
            MAX_SLOTS = [3, 3, 3, 3, 3, 2, 2, 2, 0, 0, 0, 0]
            KEY_SLOT, VALUE_SLOT, DEN_SLOT, OUT_SLOT, STACK_SLOT = 0, 3, 6, 7, 9
            assert sum(MAX_SLOTS) == QT7 * KC
            STACK_DMAS = 4 * len(GROUPS)

            q_all = sb2("q_all", [128, B * PITCH])
            Y2 = q_all[:, :].rearrange("p (a d) -> p a d", a=PAIRS)
            q_hi = sb2("q_hi", [128, B * PITCH], F32R)
            q_lo = sb2("q_lo", [128, B * PITCH], F32R)
            sel = sb2("sel", [128, 3, 128], F32R)
            ctxT = sb2("ctxT", [128, 2, S])
            k_full = sb2("k_full", [128, S])
            k_hi = sb2("k_hi", [128, 2, S], F32R)
            k_lo = sb2("k_lo", [128, 2, S], F32R)
            k_stack = sb2("k_stack", [128, 2, len(GROUPS), S], F32R)
            q_block_hi = sb2("q_block_hi", [128, 2, HQ], F32R)
            q_block_lo = sb2("q_block_lo", [128, 2, HQ], F32R)
            q_stack = sb2("q_stack", [128, 2, HQ], F32R)
            chunk_max = sb2("chunk_max", [128, QT7, KC])
            max_col = sb2("max_col", [128, QT7, 128], F32R)
            values = sb2("values", [KR, 2, KT, H // 2, 32])
            P = sb2("P", [KR, 3, HQ])
            ones_row = P[:, :, :].rearrange("p a n -> p (a n)")[0:1, 0:S]
            heads_sum = sb2("heads_sum", [128, 4 * N])
            heads_out2 = sb2("heads_out2", [128, 4 * N])

            y2_ready = sem("y2_ready")
            y2_turned = sem("y2_turned")
            y2_copied = sem("y2_copied")
            q_projected = sem("q_projected")
            q_split = sem("q_split")
            sel_ready = sem("sel_ready")
            cleared = sem("cleared")
            ones_loaded = sem("ones_loaded")
            ctx_loaded = [sem("ctx_loaded_0"), sem("ctx_loaded_1")]
            stack_loaded = [sem("stack_loaded_0"), sem("stack_loaded_1")]
            k_projected = sem("k_projected")
            k_ready = sem("k_ready")
            k_lo_ready = sem("k_lo_ready")
            v_projected = sem("v_projected")
            v_ready = sem("v_ready")
            q_blocks = sem("q_blocks")
            q_selected = sem("q_selected")
            q_stacked = sem("q_stacked")
            max_scored = sem("max_scored")
            max_taken = sem("max_taken")
            max_ready = sem("max_ready")
            s_done = sem("s_done")
            p_ready = sem("p_ready")
            pv_done = sem("pv_done")
            o_copied = sem("o_copied")
            den_done = sem("den_done")
            den_inverted = sem("den_inverted")
            o_scaled = sem("o_scaled")
            out_done = sem("out_done")
            x2_ready = sem("x2_ready")

            OSUM = PS[:, 6, 0:4 * N]
            MISC = PS[:, 7, :]

            with nc.Block() as block:

                @block.sync
                def _(sp):
                    def load_ctx(b, j):
                        sp.dma_start(ctxT[:, j, :], ctx_in[bass.ds(b, 1), :, :].rearrange("a p k -> p (a k)")
                                     ).then_inc(ctx_loaded[j], 16)

                    def load_stack(b, j):
                        sp.wait_ge(cleared, 1)
                        if isinstance(b, int) and b < 2:
                            sp.wait_ge(k_lo_ready, KC * (b + 1))
                        else:
                            sp.wait_ge(s_done, KT * (b - 1))
                        for q in range(4):
                            for g, (h0, n) in enumerate(GROUPS):
                                part = (k_hi, k_lo)[q % 2]
                                sp.dma_start(k_stack[32 * q:32 * q + n * DH, j, g, :].bitcast(F32),
                                             part[h0 * DH:(h0 + n) * DH, j, :].bitcast(F32)).then_inc(stack_loaded[j], 16)

                    load_ctx(0, 0)
                    load_ctx(1, 1)
                    sp.wait_ge(cleared, 1)
                    for j in range(2):
                        for g in range(len(GROUPS)):
                            sp.dma_start(k_stack[SHIFT_ROW:SHIFT_ROW + 1, j, g, :].bitcast(F32), ones_row
                                         ).then_inc(ones_loaded, 16)
                    load_stack(0, 0)

                    def period(b, j, u):
                        if exists(b + 2, B):
                            sp.wait_ge(cleared, 1)
                            sp.wait_ge(v_projected, KC * (b + 1))
                            load_ctx(b + 2, j)
                        if exists(b + 1, B):
                            load_stack(b + 1, 1 - j)

                    pipelined(sp, period, B)

                @block.gpsimd
                def _(pool):
                    layernorm_power(pool, 3)
                    nc.gpsimd.memset(ones_row, 1.0)
                    nc.gpsimd.memset(k_stack[:, :, :, :].bitcast(F32), 0.0).then_inc(cleared, 1)
                    nc.gpsimd.memset(max_col[:, :, :].bitcast(F32), 0.0)
                    nc.gpsimd.memset(values[:, :, :, :, :], 1.0).then_inc(cleared, 1)

                    def blocks(b, j):
                        for part, dst in ((q_hi, q_block_hi), (q_lo, q_block_lo)):
                            q = part[:, :].bitcast(F32).rearrange("p (b n) -> p b n", n=PITCH)[:, bass.ds(b, 1), 0:N]
                            last = nc.gpsimd.tensor_tensor(dst[:, j, :].rearrange("p (h n) -> p h n", h=H),
                                                           q.broadcast_to([128, H, N]),
                                                           C["head"].unsqueeze(2).broadcast_to([128, H, N]), ALU.mult)
                        last.then_inc(q_blocks, 1)

                    def lower(b, j, u):
                        if later(b, 2):
                            pool.wait_ge(stack_loaded[j], 16 * STACK_DMAS * u)
                        for c in range(KC):
                            pool.wait_ge(k_ready, KC * b + c + 1)
                            k = slice(KW * c, KW * c + KW)
                            nc.gpsimd.tensor_tensor(k_lo[:, j, k], k_full[:, k], k_hi[:, j, k].bitcast(F32), ALU.subtract
                                                    ).then_inc(k_lo_ready, 1)

                    pool.wait_ge(q_split, 1)
                    blocks(0, 0)
                    blocks(1, 1)
                    lower(0, 0, 0)
                    lower(1, 1, 0)

                    def period(b, j, u):
                        if exists(b + 2, B):
                            pool.wait_ge(q_selected, 2 * (b + 1))
                            blocks(b + 2, j)
                            lower(b + 2, j, u + 1)

                    pipelined(pool, period, B)

                @block.scalar
                def _(act):
                    for c in range(2):
                        act.wait_ge(y2_turned, c + 1)
                        nc.scalar.copy(T[:, c * 512:(c + 1) * 512], PS[:, c, :]).then_inc(y2_copied, 1)

                    def keys(b, j, u, c):
                        if c == 0:
                            if later(b, 2):
                                act.wait_ge(stack_loaded[j], 16 * STACK_DMAS * u)
                                act.wait_ge(max_scored, QT7 * KC * (b - 1))
                        if later(b, 1):
                            act.wait_ge(k_lo_ready, KC * (b - 1) + c + 1)
                        act.wait_ge(k_projected, KC * b + c + 1)
                        k = slice(KW * c, KW * c + KW)
                        nc.scalar.activation(k_hi[:, j, k], MISC[:, 0:KW], ACT.Identity, bias=COL["bk"])
                        nc.scalar.activation(k_full[:, k], MISC[:, 0:KW], ACT.Identity, bias=COL["bk"]
                                             ).then_inc(k_ready, 1)

                    def stack_queries(b, j, a):
                        if a == 0 and later(b, 2):
                            act.wait_ge(s_done, KT * (b - 1))
                        act.wait_ge(q_selected, 2 * b + a + 1)
                        nc.scalar.copy(q_stack[:, j, a * HALF:(a + 1) * HALF], MISC[:, 0:HALF]).then_inc(q_stacked, 1)

                    def exps(b, t):
                        act.wait_ge(s_done, KT * b + t + 1)
                        if later(b, 1) or t >= 3:
                            act.wait_ge(pv_done, KT * b + t - 2)
                        nc.scalar.activation(P[:, t % 3, :].rearrange("p (a n) -> p a n", a=2),
                                             PS[0:KR, 2 * (t % 2):2 * (t % 2) + 2, 0:HALF], ACT.Exp).then_inc(p_ready, 1)

                    def copy_sums(b):
                        act.wait_ge(pv_done, KT * (b + 1))
                        act.wait_ge(o_scaled, b + 1)
                        nc.scalar.copy(heads_sum[:, :], OSUM).then_inc(o_copied, 1)

                    for b in range(2):
                        for c in range(KC):
                            keys(b, b, 0, c)
                    for a in range(2):
                        stack_queries(0, 0, a)

                    def period(b, j, u):
                        for t in range(KT):
                            exps(b, t)
                            if exists(b + 2, B) and 0 <= t - KEY_SLOT < KC:
                                keys(b + 2, j, u + 1, t - KEY_SLOT)
                            if exists(b + 1, B) and 0 <= t - STACK_SLOT < 2:
                                stack_queries(b + 1, 1 - j, t - STACK_SLOT)
                            if t == 0 and later(b, 1):
                                copy_sums(b - 1)

                    pipelined(act, period, B)
                    copy_sums(B - 1)

                @block.vector
                def _(dve):
                    step = steps_of["dve"].again(dve)
                    layernorm(dve, step, 3, X, Y2).then_inc(y2_ready, 1)
                    dve.wait_ge(y2_ready, 1)
                    nc.vector.tensor_tensor(X[:, :, :], X[:, :, :], ROW["bo"].unsqueeze(1).broadcast_to([128, PAIRS, D]),
                                            ALU.add)
                    nc.vector.tensor_copy(sel[:, 0, :], C["sel_hi"]).then_inc(o_scaled, 1)
                    nc.vector.tensor_copy(sel[:, 1, :], C["sel_lo"])
                    nc.vector.tensor_copy(sel[:, 2, :], C["neg_ident"]).then_inc(sel_ready, 1)
                    dve.wait_ge(q_projected, 2)
                    step.mark(nc.vector.tensor_scalar(q_all[:, :].rearrange("p (a n) -> p a n", a=2), PS[:, 2:4, :],
                                                      COL["bq"], DH ** -0.5, ALU.add, ALU.mult))
                    step.wait()
                    step.mark(nc.vector.tensor_copy(q_hi[:, :], q_all[:, :]))
                    step.wait()
                    nc.vector.tensor_tensor(q_lo[:, :], q_all[:, :], q_hi[:, :].bitcast(F32), ALU.subtract
                                            ).then_inc(q_split, 1)

                    def take_values(b, j, c):
                        dve.wait_ge(v_projected, KC * b + c + 1)
                        if c == 0 and later(b, 2):
                            dve.wait_ge(pv_done, KT * (b - 1))
                        nc.vector.tensor_tensor(
                            values[:, j, 4 * c:4 * c + 4, :, 0:2 * DH],
                            MISC[0:KR, :].rearrange("p (t g d) -> p t g d", t=4, g=H // 2),
                            ROW["bv"][0:KR].rearrange("p (g d) -> p g d", g=H // 2).unsqueeze(1)
                            .broadcast_to([KR, 4, H // 2, 2 * DH]), ALU.add).then_inc(v_ready, 1)

                    def take_max(b, j, n):
                        dve.wait_ge(max_scored, QT7 * KC * b + n + 1)
                        nc.vector.tensor_reduce(out=chunk_max[:, n // KC, n % KC:n % KC + 1],
                                                in_=PS[:, 4 + (j + n) % 2, 0:KW], axis=AX.X, op=ALU.max
                                                ).then_inc(max_taken, 1)

                    def join_max(b):
                        dve.wait_ge(max_taken, QT7 * KC * (b + 1))
                        if later(b, 1):
                            dve.wait_ge(q_selected, 2 * b)
                        nc.vector.tensor_reduce(out=max_col[:, :, SHIFT_ROW], in_=chunk_max[:, :, :], axis=AX.X,
                                                op=ALU.max).then_inc(max_ready, 1)

                    def invert(b):
                        dve.wait_ge(den_done, b + 1)
                        nc.vector.reciprocal(heads_out2[:, :], MISC[:, 0:4 * N]).then_inc(den_inverted, 1)
                        dve.wait_ge(den_inverted, b + 1)
                        nc.vector.tensor_tensor(heads_out2[:, :], heads_out2[:, :], heads_sum[:, :], ALU.mult
                                                ).then_inc(o_scaled, 1)

                    def residual(b, j, u):
                        dve.wait_ge(out_done, b + 1)
                        r = slice(PITCH * j, PITCH * j + N)
                        nc.vector.tensor_tensor(X[r, bass.ds(u, 1), :], X[r, bass.ds(u, 1), :],
                                                MISC[r, 0:D].unsqueeze(1), ALU.add).then_inc(x2_ready, 1)

                    dve.wait_ge(cleared, 2)
                    for c in range(KC):
                        take_values(0, 0, c)
                    for n in range(QT7 * KC):
                        take_max(0, 0, n)
                    join_max(0)

                    def period(b, j, u):
                        n = 0
                        for t in range(KT):
                            if exists(b + 1, B):
                                for _ in range(MAX_SLOTS[t]):
                                    take_max(b + 1, 1 - j, n)
                                    n += 1
                                if t > 0 and MAX_SLOTS[t - 1] and not MAX_SLOTS[t]:
                                    join_max(b + 1)
                                if 0 <= t - VALUE_SLOT < KC:
                                    take_values(b + 1, 1 - j, t - VALUE_SLOT)
                            if later(b, 1):
                                if t == DEN_SLOT:
                                    invert(b - 1)
                                if t == OUT_SLOT:
                                    residual(b - 1, 1 - j, u if j == 1 else u - 1)

                    pipelined(dve, period, B)
                    invert(B - 1)
                    residual(B - 1, 1, PAIRS - 1)

                @block.tensor
                def _(pe):
                    pe.wait_ge(y2_ready, 1)
                    for c in range(2):
                        for p in range(4):
                            last = nc.tensor.transpose(PS[:, c, 128 * p:128 * p + 128], Y2[:, 4 * c + p, :], C["ident"])
                        last.then_inc(y2_turned, 1)
                    for c in range(2):
                        pe.wait_ge(y2_copied, c + 1)
                        nc.tensor.matmul(PS[:, 2 + c, :], MAT["wq"], T[:, c * 512:(c + 1) * 512], start=True, stop=True
                                         ).then_inc(q_projected, 1)

                    released = [None]

                    def shared_bank(after):
                        if released[0]:
                            pe.wait_ge(*released[0])
                        released[0] = after

                    def keys(b, j, u, c):
                        if c == 0:
                            pe.wait_ge(ctx_loaded[j], 16 * (u + 1))
                        shared_bank((k_ready, KC * b + c + 1))
                        nc.tensor.matmul(MISC[:, 0:KW], MAT["wk"], ctxT[:, j, KW * c:KW * c + KW], start=True, stop=True
                                         ).then_inc(k_projected, 1)

                    def project_values(b, j, u, c):
                        if c == 0:
                            pe.wait_ge(ctx_loaded[j], 16 * (u + 1))
                        shared_bank((v_ready, KC * b + c + 1))
                        for t in range(4):
                            k0 = KR * (4 * c + t)
                            last = nc.tensor.matmul(MISC[0:KR, 128 * t:128 * t + 128], ctxT[:, j, k0:k0 + KR], MAT["wv"],
                                                    start=True, stop=True)
                        last.then_inc(v_projected, 1)

                    def max_scores(b, j, n):
                        if n == 0:
                            pe.wait_ge(q_blocks, b + 1)
                            pe.wait_ge(k_ready, KC * (b + 1))
                        if later(b, 1) or n >= 2:
                            pe.wait_ge(max_taken, QT7 * KC * b + n - 1)
                        t, c = n // KC, n % KC
                        nc.tensor.matmul(PS[:, 4 + (j + n) % 2, 0:KW], q_block_hi[:, j, 128 * t:128 * t + 128],
                                         k_hi[:, j, KW * c:KW * c + KW], start=True, stop=True).then_inc(max_scored, 1)

                    def select_queries(b, j, a):
                        pe.wait_ge(max_ready, b + 1)
                        shared_bank((q_stacked, 2 * b + a + 1))
                        cols_ = slice(a * HALF, (a + 1) * HALF)
                        nc.tensor.matmul(MISC[:, 0:HALF], sel[:, 0, :], q_block_hi[:, j, cols_], start=True, stop=False)
                        c0, c1 = a * HALF, (a + 1) * HALF
                        for t in range(QT7):
                            lo, hi = max(c0, 128 * t), min(c1, 128 * t + 128)
                            if lo < hi:
                                nc.tensor.matmul(MISC[:, lo - c0:hi - c0], max_col[:, t, :],
                                                 sel[:, 2, lo - 128 * t:hi - 128 * t], start=False, stop=False)
                        nc.tensor.matmul(MISC[:, 0:HALF], sel[:, 1, :], q_block_lo[:, j, cols_], start=False, stop=True
                                         ).then_inc(q_selected, 1)

                    def scores(b, j, u, t):
                        if t == 0:
                            pe.wait_ge(stack_loaded[j], 16 * STACK_DMAS * (u + 1))
                            pe.wait_ge(q_stacked, 2 * (b + 1))
                        if later(b, 1) or t >= 2:
                            pe.wait_ge(p_ready, KT * b + t - 1)
                        if t == KT - 1 and exists(b + 2, B):
                            pe.wait_ge(k_lo_ready, KC * (b + 3))
                        for g, (h0, n) in enumerate(GROUPS):
                            o = h0 * N % HALF
                            last = nc.tensor.matmul(PS[0:KR, 2 * (t % 2) + h0 * N // HALF, o:o + n * N],
                                                    k_stack[:, j, g, KR * t:KR * t + KR],
                                                    q_stack[:, j, h0 * N:(h0 + n) * N], start=True, stop=True)
                        last.then_inc(s_done, 1)

                    def weigh(b, j, t):
                        pe.wait_ge(p_ready, KT * b + t + 1)
                        if t == 0:
                            if later(b, 1):
                                pe.wait_ge(o_copied, b)
                            pe.wait_ge(v_ready, KC * (b + 1))
                        for r in range(2):
                            for k in range(4):
                                g = 4 * r + k
                                last = nc.tensor.matmul(PS[32 * k:32 * k + 32, 6, 2 * N * r:2 * N * r + 2 * N],
                                                        values[:, j, t, g, :], P[:, t % 3, 2 * N * g:2 * N * g + 2 * N],
                                                        start=(t == 0 and r == 0), stop=(t == KT - 1),
                                                        skip_group_check=True)
                        last.then_inc(pv_done, 1)

                    def denominators(b):
                        pe.wait_ge(o_copied, b + 1)
                        shared_bank((den_inverted, b + 1))
                        nc.tensor.matmul(MISC[:, 0:4 * N], C["den"], heads_sum[:, :], start=True, stop=True
                                         ).then_inc(den_done, 1)

                    def project_out(b, j):
                        pe.wait_ge(o_scaled, b + 2)
                        shared_bank((x2_ready, b + 1))
                        for n in range(4):
                            last = nc.tensor.matmul(MISC[PITCH * j:PITCH * j + N, 0:D], heads_out2[:, N * n:N * n + N],
                                                    MAT[f"wo{n}"], start=(n == 0), stop=(n == 3))
                        last.then_inc(out_done, 1)

                    for b in range(2):
                        for c in range(KC):
                            keys(b, b, 0, c)
                    for c in range(KC):
                        project_values(0, 0, 0, c)
                    for n in range(QT7 * KC):
                        max_scores(0, 0, n)
                    pe.wait_ge(sel_ready, 1)
                    for a in range(2):
                        select_queries(0, 0, a)
                    pe.wait_ge(ones_loaded, 16 * 2 * len(GROUPS))

                    def period(b, j, u):
                        released[0] = (q_stacked, 2 * (b + 1))
                        n = 0
                        for t in range(KT):
                            scores(b, j, u, t)
                            if exists(b + 1, B):
                                for _ in range(MAX_SLOTS[t]):
                                    max_scores(b + 1, 1 - j, n)
                                    n += 1
                            if exists(b + 2, B) and 0 <= t - KEY_SLOT < KC:
                                keys(b + 2, j, u + 1, t - KEY_SLOT)
                            if exists(b + 1, B) and 0 <= t - VALUE_SLOT < KC:
                                project_values(b + 1, 1 - j, u if j == 0 else u + 1, t - VALUE_SLOT)
                            if later(b, 1):
                                if t == DEN_SLOT:
                                    denominators(b - 1)
                                if t == OUT_SLOT:
                                    project_out(b - 1, 1 - j)
                            if exists(b + 1, B) and 0 <= t - STACK_SLOT < 2:
                                select_queries(b + 1, 1 - j, t - STACK_SLOT)
                            if t > 0:
                                weigh(b, j, t - 1)
                            elif later(b, 1):
                                weigh(b - 1, 1 - j, KT - 1)

                    pipelined(pe, period, B)
                    weigh(B - 1, 1, KT - 1)
                    denominators(B - 1)
                    project_out(B - 1, 1)


        s3 = ExitStack()

        def sb3(name, shape, dt=F32):
            return s3.enter_context(nc.sbuf_tensor(name, shape, dt))

        with s3:
            UNITS = 2 * IT
            Y3 = sb3("Y3", [128, PAIRS, D])
            w_gate_up = sb3("w_gate_up", [128, 2, 2 * I])
            w_down = sb3("w_down", [128, 2, IT, D])
            gated = sb3("gated", [128, 2, HALF])
            hidden = sb3("hidden", [128, 2, IT, B * PITCH])
            logit = sb3("logit", [128, PAIRS, E])
            beats = sb3("beats", [128, PAIRS, E, E])
            ties = sb3("ties", [128, PAIRS, E, E])
            rank = sb3("rank", [128, PAIRS, E])
            best = sb3("best", [128, PAIRS])
            weight = sb3("weight", [128, PAIRS, E])
            weight_sum = sb3("weight_sum", [128, PAIRS])
            weight_now = sb3("weight_now", [128, 2, PAIRS])

            y3_ready = sem("y3_ready")
            y3_turned = sem("y3_turned")
            y3_copied = sem("y3_copied")
            routed = sem("routed")
            route_shifted = sem("route_shifted")
            route_exp = sem("route_exp")
            gaps_zero = sem("gaps_zero")
            gate_up_loaded = [sem("gate_up_loaded_0"), sem("gate_up_loaded_1")]
            down_loaded = [sem("down_loaded_0"), sem("down_loaded_1")]
            gate_done = sem("gate_done")
            up_done = sem("up_done")
            gated_ready = sem("gated_ready")
            hidden_ready = sem("hidden_ready")
            down_done = sem("down_done")
            weight_copied = sem("weight_copied")
            summed = sem("summed")
            FREE_BANKS = 4
            stored = sem("stored")

            def experts(engine, body):
                body(0, 0, 0)
                with engine.Fori(0, (E - 2) // 2) as i:
                    body(2 * i + 1, 1, i)
                    body(2 * i + 2, 0, i + 1)
                body(E - 1, 1, E // 2 - 1)

            with nc.Block() as block:

                @block.sync
                def _(sp):
                    def load_gate_up(e, j):
                        sp.dma_start(w_gate_up[:, j, :], wgu_in[bass.ds(e, 1), :, :].rearrange("a p n -> p (a n)")
                                     ).then_inc(gate_up_loaded[j], 16)

                    def load_down(e, j):
                        sp.dma_start(w_down[:, j, :, :], wd_in[bass.ds(e, 1), :, :, :].rearrange("a p t n -> p (a t) n")
                                     ).then_inc(down_loaded[j], 16)

                    sp.wait_ge(y3_ready, 1)
                    for e in range(2):
                        load_gate_up(e, e)
                        load_down(e, e)

                    def period(e, j, u):
                        if not isinstance(e, int) or e + 1 < E:
                            if later(e, 1):
                                sp.wait_ge(y3_ready, 1)
                                sp.wait_ge(up_done, UNITS * e)
                                load_gate_up(e + 1, 1 - j)
                                sp.wait_ge(y3_ready, 1)
                                sp.wait_ge(down_done, 2 * e)
                                load_down(e + 1, 1 - j)

                    experts(sp, period)
                    sp.wait_ge(summed, FREE_BANKS + 2 * E)
                    sp.dma_start(out, X[:, :, :]).then_inc(stored, 16)
                    sp.wait_ge(stored, 16)

                @block.gpsimd
                def _(pool):
                    layernorm_power(pool, 4)
                    pool.wait_ge(y3_ready, 1)
                    nc.gpsimd.memset(hidden[:, :, :, :], 0.0).then_inc(gaps_zero, 1)

                @block.scalar
                def _(act):
                    for c in range(2):
                        act.wait_ge(y3_turned, c + 1)
                        nc.scalar.copy(T[:, c * 512:(c + 1) * 512], PS[:, c, :]).then_inc(y3_copied, 1)
                    act.wait_ge(route_shifted, 1)
                    nc.scalar.activation(weight[:, :, :], weight[:, :, :], ACT.Exp).then_inc(route_exp, 1)

                    def period(e, j, u):
                        for k in range(UNITS):
                            act.wait_ge(gate_done, UNITS * e + k + 1)
                            if later(e, 1) or k >= 2:
                                act.wait_ge(hidden_ready, UNITS * e + k - 1)
                            nc.scalar.activation(gated[:, k % 2, :], PS[:, k % 2, 0:HALF], ACT.Silu
                                                 ).then_inc(gated_ready, 1)

                    experts(act, period)

                @block.vector
                def _(dve):
                    step = steps_of["dve"].again(dve)
                    dve.wait_ge(x2_ready, B)
                    layernorm(dve, step, 4, X, Y3).then_inc(y3_ready, 1)

                    dve.wait_ge(routed, 1)
                    step.mark(nc.vector.tensor_copy(logit[:, :, :], PS[:, 2, 0:PAIRS * E].rearrange("p (a e) -> p a e", e=E)))
                    step.wait()
                    other = logit[:, :, :].unsqueeze(2).broadcast_to([128, PAIRS, E, E])
                    own = logit[:, :, :].unsqueeze(3).broadcast_to([128, PAIRS, E, E])
                    nc.vector.tensor_reduce(out=best[:, :], in_=logit[:, :, :], axis=AX.X, op=ALU.max)
                    nc.vector.tensor_tensor(beats[:, :, :, :], other, own, ALU.is_gt)
                    step.mark(nc.vector.tensor_tensor(ties[:, :, :, :], other, own, ALU.is_equal))
                    step.wait()
                    nc.vector.tensor_tensor(weight[:, :, :], logit[:, :, :], best[:, :].unsqueeze(2).broadcast_to([128, PAIRS, E]),
                                            ALU.subtract).then_inc(route_shifted, 1)
                    before = C["before"].rearrange("p (e f) -> p e f", e=E).unsqueeze(1).broadcast_to([128, PAIRS, E, E])
                    step.mark(nc.vector.tensor_tensor(ties[:, :, :, :], ties[:, :, :, :], before, ALU.mult))
                    step.wait()
                    step.mark(nc.vector.tensor_tensor(beats[:, :, :, :], beats[:, :, :, :], ties[:, :, :, :], ALU.add))
                    step.wait()
                    step.mark(nc.vector.tensor_reduce(out=rank[:, :, :], in_=beats[:, :, :, :], axis=AX.X, op=ALU.add))
                    step.wait()
                    dve.wait_ge(route_exp, 1)
                    step.mark(nc.vector.scalar_tensor_tensor(weight[:, :, :], rank[:, :, :], 2.0, weight[:, :, :],
                                                             ALU.is_lt, ALU.mult))
                    step.wait()
                    step.mark(nc.vector.tensor_reduce(out=weight_sum[:, :], in_=weight[:, :, :], axis=AX.X, op=ALU.add))
                    step.wait()
                    step.mark(nc.vector.reciprocal(weight_sum[:, :], weight_sum[:, :]))
                    step.wait()
                    step.mark(nc.vector.tensor_tensor(weight[:, :, :], weight[:, :, :],
                                                      weight_sum[:, :].unsqueeze(2).broadcast_to([128, PAIRS, E]), ALU.mult))
                    step.wait()
                    dve.wait_ge(gaps_zero, 1)
                    nc.vector.tensor_copy(weight_now[:, 0, :], weight[:, :, 0]).then_inc(summed, FREE_BANKS)

                    def add_outputs(e, j, half):
                        if half == 0:
                            dve.wait_ge(summed, FREE_BANKS + 2 * e)
                            nc.vector.tensor_copy(weight_now[:, j, :], weight[:, :, bass.ds(e, 1)].rearrange("p a e -> p (a e)")
                                                  ).then_inc(weight_copied, 1)
                            dve.wait_ge(weight_copied, e + 1)
                        dve.wait_ge(down_done, 2 * e + half + 1)
                        dve.wait_ge(summed, FREE_BANKS + 2 * e + half - 1)
                        for p in range(4 * half, 4 * half + 4):
                            last = nc.vector.scalar_tensor_tensor(
                                X[:, p, :], PS[:, 4 + 2 * j + half, 128 * (p % 4):128 * (p % 4) + 128],
                                weight_now[:, j, p:p + 1], X[:, p, :], ALU.mult, ALU.add)
                        last.then_inc(summed, 1)

                    def period(e, j, u):
                        for k in range(UNITS):
                            c, t = k // IT, k % IT
                            dve.wait_ge(gated_ready, UNITS * e + k + 1)
                            dve.wait_ge(up_done, UNITS * e + k + 1)
                            nc.vector.tensor_tensor(
                                hidden[:, j, t, :].rearrange("p (b n) -> p b n", n=PITCH)[:, 8 * c:8 * c + 8, 0:N],
                                gated[:, k % 2, :].rearrange("p (b n) -> p b n", n=N),
                                PS[:, 2 + k % 2, 0:HALF].rearrange("p (b n) -> p b n", n=N), ALU.mult
                                ).then_inc(hidden_ready, 1)
                            if later(e, 1) and k % 4 == 3:
                                add_outputs(e - 1, 1 - j, k // 4)

                    experts(dve, period)
                    for half in range(2):
                        add_outputs(E - 1, 1, half)

                @block.tensor
                def _(pe):
                    pe.wait_ge(y3_ready, 1)
                    for c in range(2):
                        for p in range(4):
                            last = nc.tensor.transpose(PS[:, c, 128 * p:128 * p + 128], Y3[:, 4 * c + p, :], C["ident"])
                        last.then_inc(y3_turned, 1)
                    pe.wait_ge(y3_copied, 2)
                    for p in range(PAIRS):
                        last = nc.tensor.matmul(PS[:, 2, E * p:E * p + E], T[:, 128 * p:128 * p + 128], gate[:, :],
                                                start=True, stop=True)
                    last.then_inc(routed, 1)
                    pe.wait_ge(route_shifted, 1)

                    def down(e, j, p):
                        if p % 4 == 0:
                            pe.wait_ge(hidden_ready, UNITS * e + p + 4)
                            pe.wait_ge(summed, 2 * e + p // 4 + 1)
                            if p == 0:
                                pe.wait_ge(down_loaded[j], 16 * (down_turn[0] + 1))
                        for t in range(IT):
                            last = nc.tensor.matmul(PS[:, 4 + 2 * j + p // 4, 128 * (p % 4):128 * (p % 4) + 128],
                                                    hidden[:, j, t, 128 * p:128 * p + 128], w_down[:, j, t, :],
                                                    start=(t == 0), stop=(t == IT - 1))
                        if p % 4 == 3:
                            last.then_inc(down_done, 1)

                    down_turn = [0]

                    def period(e, j, u):
                        pe.wait_ge(gate_up_loaded[j], 16 * (u + 1))
                        down_turn[0] = u if j == 1 else u - 1
                        for k in range(UNITS):
                            c, t = k // IT, k % IT
                            if later(e, 1) or k >= 2:
                                pe.wait_ge(hidden_ready, UNITS * e + k - 1)
                            x = Tb[:, 8 * c:8 * c + 8, 0:N]
                            nc.tensor.matmul(PS[:, k % 2, 0:HALF], w_gate_up[:, j, 128 * t:128 * t + 128], x,
                                             start=True, stop=True).then_inc(gate_done, 1)
                            nc.tensor.matmul(PS[:, 2 + k % 2, 0:HALF], w_gate_up[:, j, I + 128 * t:I + 128 * t + 128], x,
                                             start=True, stop=True).then_inc(up_done, 1)
                            if later(e, 1):
                                down(e - 1, 1 - j, k)

                    experts(pe, period)
                    down_turn[0] = E // 2 - 1
                    for p in range(PAIRS):
                        down(E - 1, 1, p)


def lay_out(a):
    a = {k: np.asarray(v) for k, v in a.items()}
    f = np.float32
    x = np.zeros((128, PAIRS, D), f)
    for e in range(2):
        x[PITCH * e:PITCH * e + N] = a["x"][e::2].transpose(1, 0, 2)
    wo_t = a["L0_xattn_wo"].T.reshape(2, 4, 2, DH, D)
    wo = np.zeros((2, 2, 4, 32, D), f)
    for r in range(2):
        for e in range(2):
            wo[r, e, :, DH * e:DH * e + DH] = wo_t[r, :, e]
    wo = wo.reshape(4, 128, D)
    mats = [a["L0_attn_" + n] for n in MATS[:6]] + [a["L0_xattn_" + n].T for n in MATS[6:9]] + list(wo)
    mats = np.ascontiguousarray(np.stack(mats, axis=1))
    rows = np.stack([a["L0_attn_gamma1"], a["L0_attn_gamma2"], a["L0_xattn_bv"], a["L0_xattn_bo"]])
    rows = np.ascontiguousarray(np.broadcast_to(rows, (128, 4, D)))
    cols = np.stack([a["L0_attn_ln1_w"], a["L0_attn_ln1_b"], a["L0_attn_ln2_w"], a["L0_attn_ln2_b"],
                     a["L0_xattn_bq"], a["L0_xattn_bk"],
                     np.repeat(a["L0_attn_tau_t"].reshape(H), DH), np.repeat(a["L0_attn_tau_c"].reshape(CH), CD)], axis=1)
    wgu = np.concatenate([a["L0_ffn_wg"].transpose(0, 2, 1), a["L0_ffn_wu"].transpose(0, 2, 1)], axis=2)
    wd = a["L0_ffn_wd"].reshape(E, D, IT, 128).transpose(0, 3, 2, 1)
    return {"x_in": x, "ctx_in": np.ascontiguousarray(a["ctx_1024"].transpose(0, 2, 1)), "mats_in": mats, "rows_in": rows,
            "cols_in": np.ascontiguousarray(cols), "gate_in": np.ascontiguousarray(a["L0_ffn_gate_w"].T),
            "consts_in": shape_constants()[0], "wgu_in": np.ascontiguousarray(wgu), "wd_in": np.ascontiguousarray(wd)}


def program(nc, arrays):
    args = {k: nc.dram_tensor(k, v.shape, mybir.dt.from_np(v.dtype), kind="ExternalInput").ap() for k, v in arrays.items()}
    out = nc.dram_tensor("out", (128, PAIRS, D), F32, kind="ExternalOutput").ap()
    build(nc, const_at=shape_constants()[1], out=out, **args)


def kernel(**inputs):
    import concourse.bacc as bacc
    from concourse.bass_utils import run_bass_kernel_spmd

    nc = bacc.Bacc("TRN2", target_bir_lowering=False, num_devices=1)
    arrays = lay_out(inputs)
    program(nc, arrays)
    got = run_bass_kernel_spmd(nc, [arrays], core_ids=[0]).results[0]["out"]
    y = np.empty((B, N, D), got.dtype)
    for e in range(2):
        y[e::2] = got[PITCH * e:PITCH * e + N].transpose(1, 0, 2)
    return y
```

```python
from contextlib import ExitStack

import numpy as np

import concourse.bass as bass
from concourse import mybir

F32 = mybir.dt.float32
F32R = mybir.dt.float32r
ALU = mybir.AluOpType
ACT = mybir.ActivationFunctionType
AX = mybir.AxisListType

B, N, D, S = 16, 56, 128, 1500
H, DH = 16, 8
CH, CD = 8, 16
E, I = 8, 512
EPS = 1e-5

PAIRS = B // 2
PITCH = 64
HQ = H * N
HALF = HQ // 2
KT, KR = 12, S // 12
KC = 3
KW = S // KC
QT7 = HQ // 128
IT = I // 128
GH = 4
GROUPS = H // GH
SHIFT_ROW = 3 * GH * DH
OFF_BLOCK = -1e30

MATS = ["Wqk_t", "Wv_t", "Wo_t", "Wqk_c", "Wv_c", "Wo_c", "wq", "wk", "wv", "wo0", "wo1", "wo2", "wo3"]
ROWS = ["gamma1", "gamma2", "bv", "bo"]
COLS = ["ln1_w", "ln1_b", "ln2_w", "ln2_b", "bq", "bk", "tau_t", "tau_c"]


class Steps:

    def __init__(self, engine, sem):
        self.engine, self.sem, self.base, self.n = engine, sem, 0, 0

    def mark(self, instruction):
        instruction.then_inc(self.sem, 1)
        self.n += 1

    def wait(self):
        self.engine.wait_ge(self.sem, self.base + self.n)

    def again(self, engine):
        self.engine = engine
        return self

    def enter(self, i, per):
        self.outer = self.base + self.n
        self.base, self.n = self.outer + i * per, 0

    def leave(self, trips, per):
        assert self.n == per, self.n
        self.base, self.n = self.outer + trips * per, 0


def shape_constants():
    row = np.arange(128)
    ident = np.eye(128)
    head = (row[:, None] // DH == np.arange(H)[None, :]) * 1.0
    sel = np.zeros((2, 128, 128))
    for q, part in enumerate((0, 0, 1)):
        sel[part, row, 32 * q + row % 32] = 1.0
    den = (row[:, None] == 32 * (row[None, :] // 32) + 16) * 1.0
    quarter = (row[:, None] // DH % 4 == np.arange(4)[None, :]) * 1.0
    block = np.where(row[:, None] // CD == row[None, :] // CD, 0.0, OFF_BLOCK)
    before = np.broadcast_to((np.arange(E)[None, :] < np.arange(E)[:, None]) * 1.0, (128, E, E)).reshape(128, -1)
    parts = {"ident": ident, "neg_ident": -ident, "sel_hi": sel[0], "sel_lo": sel[1], "den": den, "block": block,
             "ones": np.ones((128, 128)), "head": head, "quarter": quarter, "before": before}
    at, lots, n = {}, [], 0
    for name, a in parts.items():
        at[name] = (n, a.shape[1])
        lots.append(a.astype(np.float32))
        n += a.shape[1]
    return np.concatenate(lots, axis=1), at


def build(nc, x_in, ctx_in, mats_in, rows_in, cols_in, gate_in, consts_in, const_at, wgu_in, wd_in, out):
    ctx = ExitStack()
    with ctx:
        def sb(name, shape, dt=F32):
            return ctx.enter_context(nc.sbuf_tensor(name, shape, dt))

        def sem(name):
            return ctx.enter_context(nc.semaphore(name))

        PS = ctx.enter_context(nc.psum_tensor("PS", [128, 8, 512], F32))

        X = sb("X", [128, PAIRS, D])
        mats = sb("mats", [128, len(MATS), D])
        rows = sb("rows", [128, len(ROWS), D])
        cols = sb("cols", [128, len(COLS)])
        gate = sb("gate", [128, E])
        consts = sb("consts", [128, consts_in.shape[1]])
        MAT = {n: mats[:, k, :] for k, n in enumerate(MATS)}
        ROW = {n: rows[:, k, :] for k, n in enumerate(ROWS)}
        COL = {n: cols[:, k:k + 1] for k, n in enumerate(COLS)}
        C = {n: consts[:, a:a + w] for n, (a, w) in const_at.items()}
        stats = sb("stats", [128, PAIRS, 6])
        moments = sb("moments", [128, PAIRS, 2])
        rstd = sb("rstd", [128, PAIRS])
        minus_half = sb("minus_half", [128, PAIRS])
        T = sb("T", [128, PAIRS * 128])
        Tb = T[:, :].rearrange("p (b n) -> p b n", n=PITCH)

        x_loaded = sem("x_loaded")
        consts_loaded = sem("consts_loaded")
        weights_loaded = sem("weights_loaded")
        dve_steps = sem("dve_steps")
        act_steps = sem("act_steps")
        pool_steps = sem("pool_steps")
        moments_ready = sem("moments_ready")
        eps_added = sem("eps_added")
        rstd_ready = sem("rstd_ready")

        steps_of = {}

        def layernorm(dve, step, number, src, dst):
            for p in range(PAIRS):
                last = nc.vector.bn_stats(out=stats[:, p, :], in_=src[:, p, :])
            step.mark(last)
            step.wait()
            for p in range(PAIRS):
                last = nc.vector.bn_aggr(out=moments[:, p, :], in_=stats[:, p, :])
            last.then_inc(moments_ready, 1)
            dve.wait_ge(rstd_ready, number + 1)
            for p in range(PAIRS):
                last = nc.vector.tensor_scalar(dst[:, p, :], src[:, p, :], moments[:, p, 0:1], rstd[:, p:p + 1],
                                               ALU.subtract, ALU.mult)
            return last

        def layernorm_power(pool, number):
            pool.wait_ge(moments_ready, number + 1)
            nc.gpsimd.tensor_scalar(rstd[:, :], moments[:, :, 1], EPS, None, ALU.add).then_inc(eps_added, 1)
            pool.wait_ge(eps_added, number + 2)
            nc.gpsimd.tensor_tensor(rstd[:, :], rstd[:, :], minus_half[:, :], ALU.pow).then_inc(rstd_ready, 1)

        def pipelined(engine, body, count):
            body(0, 0, 0)
            with engine.Fori(0, (count - 4) // 2) as i:
                body(2 * i + 1, 1, i)
                body(2 * i + 2, 0, i + 1)
            for n in range(count - 3, count):
                body(n, n % 2, n // 2)

        def exists(n, count):
            return not isinstance(n, int) or n < count

        def later(n, first):
            return not isinstance(n, int) or n >= first

        sel = sb("sel", [128, 3, 128], F32R)
        ctxT = sb("ctxT", [128, 2, S])
        k_full = sb("k_full", [128, S])
        k_hi = sb("k_hi", [128, 2, S], F32R)
        k_lo = sb("k_lo", [128, 2, S], F32R)
        max_col = sb("max_col", [128, QT7, 128], F32R)
        values = sb("values", [KR, 2, KT, H // 2, 32])

        ctx_loaded = [sem("ctx_loaded_0"), sem("ctx_loaded_1")]
        stack_loaded = [sem("stack_loaded_0"), sem("stack_loaded_1")]
        k_projected = sem("k_projected")
        k_ready = sem("k_ready")
        k_lo_ready = sem("k_lo_ready")
        v_projected = sem("v_projected")
        v_ready = sem("v_ready")
        max_scored = sem("max_scored")
        pv_done = sem("pv_done")
        sel_ready = sem("sel_ready")
        cleared = sem("cleared")

        MISC = PS[:, 7, :]
        SPARE = PS[:, 6, :]

        def load_ctx(sp, b, j):
            sp.dma_start(ctxT[:, j, :], ctx_in[bass.ds(b, 1), :, :].rearrange("a p k -> p (a k)")
                         ).then_inc(ctx_loaded[j], 16)

        def project_keys(pe, b, j, u, c):
            if c == 0:
                pe.wait_ge(ctx_loaded[j], 16 * (u + 1))
            nc.tensor.matmul(MISC[:, 0:KW], MAT["wk"], ctxT[:, j, KW * c:KW * c + KW], start=True, stop=True
                             ).then_inc(k_projected, 1)

        def project_values(pe, b, j, u, c, bank=MISC):
            if c == 0:
                pe.wait_ge(ctx_loaded[j], 16 * (u + 1))
            for t in range(4):
                k0 = KR * (4 * c + t)
                last = nc.tensor.matmul(bank[0:KR, 128 * t:128 * t + 128], ctxT[:, j, k0:k0 + KR], MAT["wv"],
                                        start=True, stop=True)
            last.then_inc(v_projected, 1)

        def read_keys(act, b, j, u, c):
            if c == 0:
                if later(b, 2):
                    act.wait_ge(stack_loaded[j], 16 * STACK_DMAS * u)
                    act.wait_ge(max_scored, QT7 * KC * (b - 1))
            if later(b, 1):
                act.wait_ge(k_lo_ready, KC * (b - 1) + c + 1)
            act.wait_ge(k_projected, KC * b + c + 1)
            k = slice(KW * c, KW * c + KW)
            nc.scalar.activation(k_hi[:, j, k], MISC[:, 0:KW], ACT.Identity, bias=COL["bk"])
            nc.scalar.activation(k_full[:, k], MISC[:, 0:KW], ACT.Identity, bias=COL["bk"]
                                 ).then_inc(k_ready, 1)

        def lower_keys(pool, b, j, u):
            if later(b, 2):
                pool.wait_ge(stack_loaded[j], 16 * STACK_DMAS * u)
            for c in range(KC):
                pool.wait_ge(k_ready, KC * b + c + 1)
                k = slice(KW * c, KW * c + KW)
                nc.gpsimd.tensor_tensor(k_lo[:, j, k], k_full[:, k], k_hi[:, j, k].bitcast(F32), ALU.subtract
                                        ).then_inc(k_lo_ready, 1)

        def read_values(dve, b, j, c, bank=MISC):
            dve.wait_ge(v_projected, KC * b + c + 1)
            if c == 0 and later(b, 2):
                dve.wait_ge(pv_done, KT * (b - 1))
            nc.vector.tensor_tensor(
                values[:, j, 4 * c:4 * c + 4, :, 0:2 * DH],
                bank[0:KR, :].rearrange("p (t g d) -> p t g d", t=4, g=H // 2),
                ROW["bv"][0:KR].rearrange("p (g d) -> p g d", g=H // 2).unsqueeze(1)
                .broadcast_to([KR, 4, H // 2, 2 * DH]), ALU.add).then_inc(v_ready, 1)

        s1 = ExitStack()

        def sb1(name, shape, dt=F32):
            return s1.enter_context(nc.sbuf_tensor(name, shape, dt))

        with s1:
            Z = sb1("Z", [128, PAIRS, D])
            Y = sb1("Y", [128, PAIRS, D])
            qkT = sb1("qkT", [128, PAIRS * 128])
            v_all = sb1("v_all", [N, B, D])
            coef = sb1("coef", [128, 3])
            scaled = sb1("scaled", [128, PAIRS * 128])
            squared = sb1("squared", [128, PAIRS * 128])
            qk_pair = sb1("qk_pair", [128, 2, 128])
            v_pair = sb1("v_pair", [N, 2, 2, D])
            q_block = sb1("q_block", [128, 2, 2, HQ])
            q_square = sb1("q_square", [128, 2, 2, HQ])
            row_max = sb1("row_max", [128, 2, H])
            row_sum = sb1("row_sum", [128, 2, H])
            probs = sb1("probs", [128, 2, HQ])
            probsT = sb1("probsT", [N, 2, H, 128])
            heads_out = sb1("heads_out", [128, 2, 2, 4 * PITCH])
            wo_quarter = sb1("wo_quarter", [128, 4, D])
            wo_scaled = sb1("wo_scaled", [128, 2, D])
            gram_left = sb1("gram_left", [128, B, D])
            gram_right = sb1("gram_right", [128, B, D])
            gram = sb1("gram", [128, B, D])
            gmax = sb1("gmax", [128, B])
            gsum = sb1("gsum", [128, B])

            y_ready = sem("y_ready")
            y_turned = sem("y_turned")
            y_copied = sem("y_copied")
            coef_ready = sem("coef_ready")
            wo_ready = sem("wo_ready")
            qk_projected = sem("qk_projected")
            qk_read = sem("qk_read")
            v1_projected = sem("v1_projected")
            v_all_ready = sem("v_all_ready")
            scaled_ready = sem("scaled_ready")
            qk_copied = sem("qk_copied")
            v_copied = sem("v_copied")
            blocks_dve = sem("blocks_dve")
            blocks_pool = sem("blocks_pool")
            logits_done = sem("logits_done")
            max_done = sem("max_done")
            shifted_ready = sem("shifted_ready")
            exp_ready = sem("exp_ready")
            sum_done = sem("sum_done")
            inverse_done = sem("inverse_done")
            probs_ready = sem("probs_ready")
            turned = sem("turned")
            turned_copied = [sem("turned_copied_0"), sem("turned_copied_1")]
            pv1_done = sem("pv1_done")
            pv1_copied = sem("pv1_copied")
            out1_done = sem("out1_done")
            out1_added = sem("out1_added")
            qkc_projected = sem("qkc_projected")
            squares_ready = sem("squares_ready")
            upper_ready = sem("upper_ready")
            left_filled = sem("left_filled")
            vc_projected = sem("vc_projected")
            vc_ready = sem("vc_ready")
            gram_done = sem("gram_done")
            gram_shifted = sem("gram_shifted")
            gram_exp = sem("gram_exp")
            gram_ready = sem("gram_ready")
            mixed = sem("mixed")
            mixed_copied = sem("mixed_copied")
            outc_done = sem("outc_done")
            x1_ready = sem("x1_ready")

            TURN = PS[0:N, 4:6, :]
            HEADS = PS[:, 6, :]
            OUT1 = PS[:, 7, 0:D]

            def batch_block(src, p, e):
                v = src[:, :].rearrange("q (b n) -> q b n", n=PITCH)
                return v[:, bass.ds(2 * p + e, 1), 0:N].broadcast_to([128, H, N])

            def by_head(tile):
                return tile.rearrange("p (h n) -> p h n", n=N)

            T2 = q_block[:, :, :, :].rearrange("p a e n -> p (a e n)")[:, 0:2 * B * PITCH].rearrange(
                "p (b a n) -> p b a n", b=B, a=2)
            HEAD_MASK = C["head"].unsqueeze(2).broadcast_to([128, H, N])

            with nc.Block() as block:

                @block.sync
                def _(sp):
                    sp.dma_start(X[:, :, :], x_in).then_inc(x_loaded, 16)
                    sp.dma_start(consts[:, :], consts_in).then_inc(consts_loaded, 16)
                    sp.dma_start(cols[:, :], cols_in).then_inc(consts_loaded, 16)
                    sp.dma_start(rows[:, :, :], rows_in).then_inc(consts_loaded, 16)
                    sp.dma_start(mats[:, :, :], mats_in).then_inc(weights_loaded, 16)
                    sp.dma_start(gate[:, :], gate_in).then_inc(weights_loaded, 16)
                    load_ctx(sp, 0, 0)
                    load_ctx(sp, 1, 1)

                @block.gpsimd
                def _(pool):
                    nc.gpsimd.memset(minus_half[:, :], -0.5).then_inc(eps_added, 1)
                    layernorm_power(pool, 0)
                    layernorm_power(pool, 1)
                    pool.wait_ge(consts_loaded, 48)
                    pool.wait_ge(scaled_ready, 1)

                    def blocks(p, j):
                        if later(p, 2):
                            pool.wait_ge(logits_done, p - 1)
                        nc.gpsimd.tensor_tensor(by_head(q_block[:, j, 0, :]), batch_block(scaled, p, 0), HEAD_MASK, ALU.mult)
                        for e in range(2):
                            last = nc.gpsimd.tensor_tensor(by_head(q_square[:, j, e, :]), batch_block(squared, p, e),
                                                           HEAD_MASK, ALU.mult)
                        last.then_inc(blocks_pool, 1)

                    for p in range(3):
                        blocks(p, p % 2)

                    def turn(p, j, u):
                        if exists(p + 3, PAIRS):
                            blocks(p + 3, 1 - j)

                    pipelined(pool, turn, PAIRS)
                    nc.gpsimd.memset(gram_left[:, :, :], -0.5).then_inc(left_filled, 1)
                    layernorm_power(pool, 2)

                    nc.gpsimd.memset(max_col[:, :, :].bitcast(F32), 0.0)
                    lower_keys(pool, 0, 0, 0)
                    nc.gpsimd.memset(values[:, :, :, :, :], 1.0).then_inc(cleared, 1)
                    lower_keys(pool, 1, 1, 0)

                @block.scalar
                def _(act):
                    act.wait_ge(consts_loaded, 48)
                    for c in range(2):
                        act.wait_ge(y_turned, c + 1)
                        nc.scalar.activation(T[:, c * 512:(c + 1) * 512], PS[:, c, :], ACT.Identity,
                                             bias=COL["ln1_b"], scale=COL["ln1_w"]).then_inc(y_copied, 1)
                    for c in range(2):
                        act.wait_ge(qk_projected, c + 1)
                        nc.scalar.copy(qkT[:, c * 512:(c + 1) * 512], PS[:, 2 + c, :]).then_inc(qk_read, 1)
                    act.wait_ge(qk_read, 2)

                    def copy_qk(p, j):
                        if later(p, 2):
                            act.wait_ge(logits_done, p - 1)
                        nc.scalar.copy(qk_pair[:, j, :], qkT[:, bass.ts(p, 128)]).then_inc(qk_copied, 1)

                    def copy_v(p, j):
                        nc.scalar.copy(v_pair[:, j, :, :], v_all[:, bass.ts(p, 2), :]).then_inc(v_copied, 1)

                    def exp(p, j):
                        act.wait_ge(shifted_ready, p + 1)
                        nc.scalar.activation(probs[:, j, :], probs[:, j, :], ACT.Exp).then_inc(exp_ready, 1)

                    copy_qk(0, 0)
                    copy_qk(1, 1)
                    for c in range(4):
                        act.wait_ge(v1_projected, c + 1)
                        nc.scalar.copy(v_all[:, 4 * c:4 * c + 4, :],
                                       PS[0:N, 4 + c, :].rearrange("p (b d) -> p b d", b=4)).then_inc(v_all_ready, 1)
                    act.wait_ge(v_all_ready, 4)
                    copy_v(0, 0)
                    copy_v(1, 1)
                    exp(0, 0)

                    def turn(p, j, u):
                        if exists(p + 2, PAIRS):
                            copy_qk(p + 2, j)
                        for a in range(2):
                            act.wait_ge(turned, 2 * p + a + 1)
                            nc.scalar.copy(probsT[:, j, 8 * a:8 * a + 8, :], TURN.rearrange("p a (h n) -> p (a h) n", h=4)
                                           ).then_inc(turned_copied[a], 1)
                            if a == 0 and exists(p + 1, PAIRS):
                                exp(p + 1, 1 - j)
                        act.wait_ge(pv1_done, p + 1)
                        nc.scalar.copy(heads_out[:, j, :, :], HEADS.rearrange("p (e n) -> p e n", e=2)
                                       ).then_inc(pv1_copied, 1)
                        if exists(p + 2, PAIRS):
                            copy_v(p + 2, j)

                    pipelined(act, turn, PAIRS)
                    for c in range(KC):
                        read_keys(act, 0, 0, 0, c)

                    for c in range(2):
                        act.wait_ge(y_turned, c + 3)
                        once = PS[:, c, :].rearrange("p (b n) -> p b n", n=PITCH).unsqueeze(2)
                        nc.scalar.activation(T2[:, 8 * c:8 * c + 8, :, :], once.broadcast_to([128, B // 2, 2, PITCH]),
                                             ACT.Identity, bias=COL["ln2_b"], scale=COL["ln2_w"]).then_inc(y_copied, 1)
                    for c in range(4):
                        act.wait_ge(qkc_projected, c + 1)
                        r = slice(PITCH, 2 * PITCH)
                        nc.scalar.activation(gram_right[r, 4 * c:4 * c + 4, :],
                                             PS[r, 2 + c, :].rearrange("p (b d) -> p b d", b=4), ACT.Square
                                             ).then_inc(squares_ready, 1)
                    for c in range(2):
                        act.wait_ge(vc_projected, c + 1)
                        nc.scalar.copy(qkT[:, c * 512:(c + 1) * 512], PS[:, 6 + c, :]).then_inc(vc_ready, 1)
                    for c in range(KC):
                        read_keys(act, 1, 1, 0, c)
                        if c < 2:
                            act.wait_ge(gram_shifted, c + 1)
                            nc.scalar.activation(gram[:, 8 * c:8 * c + 8, :], gram[:, 8 * c:8 * c + 8, :], ACT.Exp
                                                 ).then_inc(gram_exp, 1)
                    for c in range(2):
                        act.wait_ge(mixed, c + 1)
                        nc.scalar.copy(gram[:, 8 * c:8 * c + 8, :],
                                       PS[:, 2 * c:2 * c + 2, :].rearrange("p a (b d) -> p (a b) d", b=4)
                                       ).then_inc(mixed_copied, 1)

                @block.vector
                def _(dve):
                    step = Steps(dve, dve_steps)
                    steps_of["dve"] = step
                    dve.wait_ge(x_loaded, 16)
                    step.mark(layernorm(dve, step, 0, X, Z))
                    step.wait()
                    layernorm(dve, step, 1, Z, Y).then_inc(y_ready, 1)
                    dve.wait_ge(consts_loaded, 48)
                    nc.vector.tensor_scalar(coef[:, 0:1], COL["tau_t"], 2.0 / DH ** 0.5, None, ALU.mult)
                    nc.vector.tensor_scalar(coef[:, 1:2], COL["tau_t"], -1.0 / DH ** 0.5, None, ALU.mult)
                    nc.vector.tensor_scalar(coef[:, 2:3], COL["tau_c"], 2.0 / N ** 0.5, None, ALU.mult
                                            ).then_inc(coef_ready, 1)
                    dve.wait_ge(coef_ready, 1)
                    dve.wait_ge(qk_read, 2)
                    nc.vector.tensor_scalar(scaled[:, :], qkT[:, :], coef[:, 0:1], None, ALU.mult)
                    nc.vector.scalar_tensor_tensor(squared[:, :], qkT[:, :], coef[:, 1:2], qkT[:, :], ALU.mult, ALU.mult
                                                   ).then_inc(scaled_ready, 1)

                    def blocks(p, j):
                        if later(p, 2):
                            dve.wait_ge(logits_done, p - 1)
                        nc.vector.tensor_tensor(by_head(q_block[:, j, 1, :]), batch_block(scaled, p, 1), HEAD_MASK, ALU.mult
                                                ).then_inc(blocks_dve, 1)

                    def logit_half(j, a):
                        return by_head(PS[:, 2 * j + a, 0:HALF])

                    def shift(p, j):
                        dve.wait_ge(logits_done, p + 1)
                        for a in range(2):
                            last = nc.vector.tensor_reduce(out=row_max[:, j, 8 * a:8 * a + 8], in_=logit_half(j, a),
                                                           axis=AX.X, op=ALU.max)
                        last.then_inc(max_done, 1)
                        dve.wait_ge(max_done, p + 1)
                        if later(p, 2):
                            dve.wait_ge(turned, 2 * (p - 1))
                        for a in range(2):
                            last = nc.vector.tensor_tensor(
                                by_head(probs[:, j, a * HALF:(a + 1) * HALF]), logit_half(j, a),
                                row_max[:, j, 8 * a:8 * a + 8].unsqueeze(2).broadcast_to([128, 8, N]), ALU.subtract)
                        last.then_inc(shifted_ready, 1)

                    def normalise(p, j):
                        dve.wait_ge(exp_ready, p + 1)
                        tile = by_head(probs[:, j, :])
                        nc.vector.tensor_reduce(out=row_sum[:, j, :], in_=tile, axis=AX.X, op=ALU.add).then_inc(sum_done, 1)
                        dve.wait_ge(sum_done, p + 1)
                        nc.vector.reciprocal(row_sum[:, j, :], row_sum[:, j, :]).then_inc(inverse_done, 1)
                        dve.wait_ge(inverse_done, p + 1)
                        nc.vector.tensor_tensor(tile, tile, row_sum[:, j, :].unsqueeze(2).broadcast_to([128, H, N]),
                                                ALU.mult).then_inc(probs_ready, 1)

                    nc.vector.tensor_copy(sel[:, 0, :], C["sel_hi"]).then_inc(out1_added, 1)
                    nc.vector.tensor_copy(sel[:, 1, :], C["sel_lo"])
                    nc.vector.tensor_copy(sel[:, 2, :], C["neg_ident"]).then_inc(sel_ready, 1)
                    dve.wait_ge(scaled_ready, 1)
                    for p in range(3):
                        blocks(p, p % 2)
                        if p == 0:
                            dve.wait_ge(weights_loaded, 32)
                            nc.vector.tensor_tensor(wo_scaled[:, 0, :], MAT["Wo_t"], ROW["gamma1"], ALU.mult)
                            step.mark(nc.vector.tensor_tensor(wo_scaled[:, 1, :], MAT["Wo_c"], ROW["gamma2"], ALU.mult))
                            step.wait()
                            for k in range(4):
                                last = nc.vector.tensor_scalar(wo_quarter[:, k, :], wo_scaled[:, 0, :],
                                                               C["quarter"][:, k:k + 1], None, ALU.mult)
                            last.then_inc(wo_ready, 1)
                    shift(0, 0)
                    normalise(0, 0)

                    def add_heads(p):
                        dve.wait_ge(out1_done, p + 1)
                        nc.vector.tensor_tensor(Z[:, bass.ds(p, 1), :], Z[:, bass.ds(p, 1), :], OUT1.unsqueeze(1), ALU.add
                                                ).then_inc(out1_added, 1)

                    def turn(p, j, u):
                        if exists(p + 1, PAIRS):
                            shift(p + 1, 1 - j)
                        if exists(p + 3, PAIRS):
                            blocks(p + 3, 1 - j)
                        if later(p, 1):
                            add_heads(p - 1)
                        if exists(p + 1, PAIRS):
                            normalise(p + 1, 1 - j)

                    pipelined(dve, turn, PAIRS)
                    add_heads(PAIRS - 1)

                    dve.wait_ge(out1_added, PAIRS + 1)
                    layernorm(dve, step, 2, Z, Y).then_inc(y_ready, 1)
                    step.mark(nc.vector.tensor_tensor(X[:, :, :], X[:, :, :], Z[:, :, :], ALU.add))
                    dve.wait_ge(left_filled, 1)
                    step.mark(nc.vector.memset(gram_left[PITCH // 2:PITCH, :, :], 0.0))
                    step.wait()
                    for c in range(4):
                        dve.wait_ge(qkc_projected, c + 1)
                        for side, r in ((gram_right, PITCH), (gram_left, N)):
                            last = nc.vector.tensor_copy(side[0:r, 4 * c:4 * c + 4, :],
                                                         PS[0:r, 2 + c, :].rearrange("p (b d) -> p b d", b=4))
                        last.then_inc(upper_ready, 1)
                    mask = C["block"].unsqueeze(1).broadcast_to([128, 8, D])
                    for c in range(2):
                        part = gram[:, 8 * c:8 * c + 8, :]
                        dve.wait_ge(gram_done, c + 1)
                        step.mark(nc.vector.scalar_tensor_tensor(
                            part, PS[:, 2 * c:2 * c + 2, :].rearrange("p a (b d) -> p (a b) d", b=4), coef[:, 2:3], mask,
                            ALU.mult, ALU.add))
                        step.wait()
                        step.mark(nc.vector.tensor_reduce(out=gmax[:, 8 * c:8 * c + 8], in_=part, axis=AX.X, op=ALU.max))
                        step.wait()
                        nc.vector.tensor_tensor(part, part, gmax[:, 8 * c:8 * c + 8].unsqueeze(2).broadcast_to([128, 8, D]),
                                                ALU.subtract).then_inc(gram_shifted, 1)
                    for c in range(2):
                        part, total = gram[:, 8 * c:8 * c + 8, :], gsum[:, 8 * c:8 * c + 8]
                        dve.wait_ge(gram_exp, c + 1)
                        step.mark(nc.vector.tensor_reduce(out=total, in_=part, axis=AX.X, op=ALU.add))
                        step.wait()
                        step.mark(nc.vector.reciprocal(total, total))
                        step.wait()
                        nc.vector.tensor_tensor(part, part, total.unsqueeze(2).broadcast_to([128, 8, D]), ALU.mult
                                                ).then_inc(gram_ready, 1)
                    dve.wait_ge(cleared, 1)
                    for c in range(2):
                        read_values(dve, 0, 0, c, (SPARE, MISC)[c])
                    for c in range(2):
                        dve.wait_ge(outc_done, c + 1)
                        nc.vector.tensor_tensor(X[:, 4 * c:4 * c + 4, :], X[:, 4 * c:4 * c + 4, :],
                                                PS[:, 4 + c, :].rearrange("p (b d) -> p b d", b=4), ALU.add
                                                ).then_inc(x1_ready, 1)
                    read_values(dve, 0, 0, 2, SPARE)
                    dve.wait_ge(x1_ready, 2)

                @block.tensor
                def _(pe):
                    def turn_tokens():
                        for c in range(2):
                            for p in range(4):
                                last = nc.tensor.transpose(PS[:, c, 128 * p:128 * p + 128], Y[:, 4 * c + p, :], C["ident"])
                            last.then_inc(y_turned, 1)

                    pe.wait_ge(consts_loaded, 48)
                    pe.wait_ge(y_ready, 1)
                    turn_tokens()
                    pe.wait_ge(weights_loaded, 32)
                    for c in range(2):
                        pe.wait_ge(y_copied, c + 1)
                        nc.tensor.matmul(PS[:, 2 + c, :], MAT["Wqk_t"], T[:, c * 512:(c + 1) * 512], start=True, stop=True
                                         ).then_inc(qk_projected, 1)
                    for b in range(B):
                        mm = nc.tensor.matmul(PS[0:N, 4 + b // 4, 128 * (b % 4):128 * (b % 4) + 128], Tb[:, b, 0:N],
                                              MAT["Wv_t"], start=True, stop=True)
                        if b % 4 == 3:
                            mm.then_inc(v1_projected, 1)

                    def logits(p, j, a, turned_half=False):
                        if a == 0:
                            pe.wait_ge(blocks_dve, p + 1)
                            pe.wait_ge(blocks_pool, p + 1)
                            pe.wait_ge(qk_copied, p + 1)
                            if later(p, 2):
                                pe.wait_ge(shifted_ready, p - 1)
                        for e in range(2):
                            nc.tensor.matmul(PS[PITCH * e:PITCH * e + PITCH, 2 * j + a, 0:HALF],
                                             qk_pair[:, j, PITCH * e:PITCH * e + PITCH],
                                             q_block[:, j, e, a * HALF:(a + 1) * HALF], start=True, stop=False)
                        if turned_half:
                            pe.wait_ge(turned_copied[0], p - 1)
                        for e in range(2):
                            last = nc.tensor.matmul(PS[PITCH * e:PITCH * e + PITCH, 2 * j + a, 0:HALF],
                                                    C["ones"][:, 0:PITCH],
                                                    q_square[:, j, e, a * HALF:(a + 1) * HALF], start=False, stop=True)
                        if a == 1:
                            last.then_inc(logits_done, 1)

                    def turn_probs(p, j, a):
                        for h in range(8):
                            last = nc.tensor.transpose(PS[0:N, 4 + h // 4, 128 * (h % 4):128 * (h % 4) + 128],
                                                       probs[:, j, (8 * a + h) * N:(8 * a + h + 1) * N], C["ident"])
                        last.then_inc(turned, 1)

                    def attend(p, j):
                        pe.wait_ge(v_all_ready, 4)
                        pe.wait_ge(v_copied, p + 1)
                        pe.wait_ge(turned_copied[1], p + 1)
                        for e in range(2):
                            for k in range(4):
                                last = nc.tensor.matmul(
                                    PS[32 * k:32 * k + 32, 6, 256 * e:256 * e + 256], v_pair[:, j, e, 32 * k:32 * k + 32],
                                    probsT[:, j, 4 * k:4 * k + 4, PITCH * e:PITCH * e + PITCH], start=True, stop=True)
                        last.then_inc(pv1_done, 1)

                    def project_heads(p, j):
                        pe.wait_ge(pv1_copied, p + 1)
                        pe.wait_ge(out1_added, p + 1)
                        if not isinstance(p, int) or p + 1 < PAIRS:
                            pe.wait_ge(probs_ready, p + 2)
                        for k in range(4):
                            for e in range(2):
                                last = nc.tensor.matmul(PS[PITCH * e:PITCH * e + PITCH, 7, 0:D],
                                                        heads_out[:, j, e, PITCH * k:PITCH * k + PITCH], wo_quarter[:, k, :],
                                                        start=(k == 0), stop=(k == 3))
                        last.then_inc(out1_done, 1)

                    for p in range(2):
                        for a in range(2):
                            logits(p, p, a)
                    pe.wait_ge(v_all_ready, 4)
                    pe.wait_ge(wo_ready, 1)
                    pe.wait_ge(probs_ready, 1)

                    def turn(p, j, u):
                        if later(p, 1):
                            project_heads(p - 1, 1 - j)
                        turn_probs(p, j, 0)
                        if exists(p + 2, PAIRS):
                            logits(p + 2, j, 0, turned_half=True)
                        else:
                            pe.wait_ge(turned_copied[0], p + 1)
                        turn_probs(p, j, 1)
                        if exists(p + 2, PAIRS):
                            logits(p + 2, j, 1)
                        attend(p, j)

                    pipelined(pe, turn, PAIRS)
                    project_heads(PAIRS - 1, 1)

                    def first_keys(b):
                        for c in range(KC):
                            if b == 0 and c == 0:
                                pe.wait_ge(out1_added, PAIRS + 1)
                            else:
                                pe.wait_ge(k_ready, KC * b + c)
                            project_keys(pe, b, b, 0, c)

                    first_keys(0)

                    pe.wait_ge(y_ready, 2)
                    turn_tokens()
                    pe.wait_ge(y_copied, 4)
                    for b in range(B):
                        twice = T2[:, b, :, :].rearrange("p a n -> p (a n)")
                        mm = nc.tensor.matmul(PS[:, 2 + b // 4, 128 * (b % 4):128 * (b % 4) + 128], twice, MAT["Wqk_c"],
                                              start=True, stop=True)
                        if b % 4 == 3:
                            mm.then_inc(qkc_projected, 1)
                    pe.wait_ge(k_ready, KC)
                    for c in range(2):
                        nc.tensor.matmul(PS[:, 6 + c, :], MAT["Wv_c"], T2[:, 8 * c:8 * c + 8, 0, :], start=True, stop=True
                                         ).then_inc(vc_projected, 1)
                    for b in range(B):
                        if b % 4 == 0:
                            pe.wait_ge(squares_ready, b // 4 + 1)
                            pe.wait_ge(upper_ready, b // 4 + 1)
                        r = slice(0, PITCH + N)
                        mm = nc.tensor.matmul(PS[:, b // 4, 128 * (b % 4):128 * (b % 4) + 128], gram_left[r, b, :],
                                              gram_right[r, b, :], start=True, stop=True)
                        if b % 8 == 7:
                            mm.then_inc(gram_done, 1)
                    pe.wait_ge(vc_ready, 2)
                    first_keys(1)
                    pe.wait_ge(k_ready, 2 * KC)
                    for c in range(2):
                        project_values(pe, 0, 0, 0, c, (SPARE, MISC)[c])
                    for c in range(2):
                        pe.wait_ge(gram_ready, c + 1)
                        for g in range(8 * c, 8 * c + 8):
                            last = nc.tensor.matmul(PS[:, g // 4, 128 * (g % 4):128 * (g % 4) + 128], gram[:, g, :],
                                                    wo_scaled[:, 1, :], start=True, stop=True)
                        last.then_inc(mixed, 1)
                    pe.wait_ge(mixed_copied, 2)
                    pe.wait_ge(vc_ready, 2)
                    for c in range(2):
                        for p in range(4 * c, 4 * c + 4):
                            for e in range(2):
                                last = nc.tensor.matmul(
                                    PS[PITCH * e:PITCH * e + PITCH, 4 + c, 128 * (p % 4):128 * (p % 4) + 128],
                                    qkT[:, 128 * p + PITCH * e:128 * p + PITCH * e + PITCH], gram[:, 2 * p + e, :],
                                    start=True, stop=True)
                        last.then_inc(outc_done, 1)
                    pe.wait_ge(v_ready, 1)
                    project_values(pe, 0, 0, 0, 2, SPARE)

        s2 = ExitStack()

        def sb2(name, shape, dt=F32):
            return s2.enter_context(nc.sbuf_tensor(name, shape, dt))

        with s2:
            MAX_SLOTS = [3, 2, 2, 2, 2, 2, 2, 2, 2, 2, 0, 0]
            KEY_SLOTS, VALUE_SLOTS, STACK_SLOTS, DEN_SLOT, OUT_SLOT = [0, 2, 4], [1, 3, 5], [8, 10], 6, 9
            HALF_TILES = [slice(0, -(-HALF // 128)), slice(-(-HALF // 128), QT7)]
            assert sum(MAX_SLOTS) == QT7 * KC

            def max_bank(b, j, n):
                return 4 + (j + n) % 2 if later(b, 1) else n % 6

            def max_chunks(t):
                n = list(range(sum(MAX_SLOTS[:t]), sum(MAX_SLOTS[:t + 1])))
                return n[:1], n[1:]
            STACK_DMAS = 3 * GROUPS

            q_all = sb2("q_all", [128, B * PITCH])
            Y2 = q_all[:, :].rearrange("p (a d) -> p a d", a=PAIRS)
            q_hi = sb2("q_hi", [128, B * PITCH], F32R)
            q_lo = sb2("q_lo", [128, B * PITCH], F32R)
            k_stack = sb2("k_stack", [SHIFT_ROW + 1, 2, GROUPS, S], F32R)
            q_block_hi = sb2("q_block_hi", [128, 2, HQ], F32R)
            q_block_lo = sb2("q_block_lo", [128, 2, HQ], F32R)
            q_stack = sb2("q_stack", [128, 2, HQ], F32R)
            chunk_max = sb2("chunk_max", [128, QT7, KC])
            P = sb2("P", [KR, 3, HQ])
            ones_row = P[:, :, :].rearrange("p a n -> p (a n)")[0:1, 0:S]
            heads_sum = sb2("heads_sum", [128, 4 * N])
            heads_out2 = sb2("heads_out2", [128, 4 * N])

            y2_ready = sem("y2_ready")
            y2_turned = sem("y2_turned")
            y2_copied = sem("y2_copied")
            q_projected = sem("q_projected")
            q_split = sem("q_split")
            ones_ready = sem("ones_ready")
            ones_loaded = sem("ones_loaded")
            q_blocks = sem("q_blocks")
            q_selected = sem("q_selected")
            q_stacked = sem("q_stacked")
            max_taken = sem("max_taken")
            max_ready = sem("max_ready")
            s_done = sem("s_done")
            p_ready = sem("p_ready")
            o_copied = sem("o_copied")
            den_done = sem("den_done")
            den_inverted = sem("den_inverted")
            o_scaled = sem("o_scaled")
            out_done = sem("out_done")
            x2_ready = sem("x2_ready")

            OSUM = PS[:, 6, 0:4 * N]

            with nc.Block() as block:

                @block.sync
                def _(sp):
                    def load_stack(b, j):
                        if isinstance(b, int) and b < 2:
                            sp.wait_ge(k_lo_ready, KC * (b + 1))
                        else:
                            sp.wait_ge(s_done, KT * (b - 1))
                        for q, part in enumerate((k_hi, k_lo, k_hi)):
                            for g in range(GROUPS):
                                sp.dma_start(k_stack[32 * q:32 * q + 32, j, g, :].bitcast(F32),
                                             part[32 * g:32 * g + 32, j, :].bitcast(F32)).then_inc(stack_loaded[j], 16)

                    load_stack(0, 0)
                    sp.wait_ge(ones_ready, 1)
                    for j in range(2):
                        for g in range(GROUPS):
                            sp.dma_start(k_stack[SHIFT_ROW:SHIFT_ROW + 1, j, g, :].bitcast(F32), ones_row
                                         ).then_inc(ones_loaded, 16)

                    def period(b, j, u):
                        if exists(b + 2, B):
                            sp.wait_ge(cleared, 1)
                            sp.wait_ge(v_projected, KC * (b + 1))
                            load_ctx(sp, b + 2, j)
                        if exists(b + 1, B):
                            load_stack(b + 1, 1 - j)

                    pipelined(sp, period, B)

                @block.gpsimd
                def _(pool):
                    nc.gpsimd.memset(ones_row, 1.0).then_inc(ones_ready, 1)
                    layernorm_power(pool, 3)

                    def blocks(b, j):
                        for part, dst in ((q_hi, q_block_hi), (q_lo, q_block_lo)):
                            q = part[:, :].bitcast(F32).rearrange("p (b n) -> p b n", n=PITCH)[:, bass.ds(b, 1), 0:N]
                            nc.gpsimd.tensor_tensor(dst[:, j, :].rearrange("p (h n) -> p h n", h=H),
                                                    q.broadcast_to([128, H, N]),
                                                    C["head"].unsqueeze(2).broadcast_to([128, H, N]), ALU.mult
                                                    ).then_inc(q_blocks, 1)

                    pool.wait_ge(q_split, 1)
                    blocks(0, 0)
                    blocks(1, 1)

                    def period(b, j, u):
                        if exists(b + 2, B):
                            pool.wait_ge(q_selected, 2 * (b + 1))
                            blocks(b + 2, j)
                            lower_keys(pool, b + 2, j, u + 1)

                    pipelined(pool, period, B)

                @block.scalar
                def _(act):
                    for c in range(2):
                        act.wait_ge(y2_turned, c + 1)
                        nc.scalar.copy(T[:, c * 512:(c + 1) * 512], PS[:, c, :]).then_inc(y2_copied, 1)

                    def stack_queries(b, j, a):
                        if a == 0 and later(b, 2):
                            act.wait_ge(s_done, KT * (b - 1))
                        act.wait_ge(q_selected, 2 * b + a + 1)
                        nc.scalar.copy(q_stack[:, j, a * HALF:(a + 1) * HALF], MISC[:, 0:HALF]).then_inc(q_stacked, 1)

                    def exps(b, t):
                        act.wait_ge(s_done, KT * b + t + 1)
                        if later(b, 1) or t >= 3:
                            act.wait_ge(pv_done, KT * b + t - 2)
                        nc.scalar.activation(P[:, t % 3, :].rearrange("p (a n) -> p a n", a=2),
                                             PS[0:KR, 2 * (t % 2):2 * (t % 2) + 2, 0:HALF], ACT.Exp).then_inc(p_ready, 1)

                    def copy_sums(b):
                        act.wait_ge(pv_done, KT * (b + 1))
                        act.wait_ge(o_scaled, b + 1)
                        nc.scalar.copy(heads_sum[:, :], OSUM).then_inc(o_copied, 1)

                    for a in range(2):
                        stack_queries(0, 0, a)

                    def period(b, j, u):
                        for t in range(KT):
                            exps(b, t)
                            if exists(b + 2, B) and t in KEY_SLOTS:
                                read_keys(act, b + 2, j, u + 1, KEY_SLOTS.index(t))
                            if exists(b + 1, B) and t in STACK_SLOTS:
                                stack_queries(b + 1, 1 - j, STACK_SLOTS.index(t))
                            if t == 0 and later(b, 1):
                                copy_sums(b - 1)

                    pipelined(act, period, B)
                    copy_sums(B - 1)

                @block.vector
                def _(dve):
                    step = steps_of["dve"].again(dve)
                    layernorm(dve, step, 3, X, Y2).then_inc(y2_ready, 1)
                    dve.wait_ge(y2_ready, 1)
                    nc.vector.tensor_tensor(X[:, :, :], X[:, :, :], ROW["bo"].unsqueeze(1).broadcast_to([128, PAIRS, D]),
                                            ALU.add).then_inc(o_scaled, 1)
                    dve.wait_ge(q_projected, 2)
                    step.mark(nc.vector.tensor_scalar(q_all[:, :].rearrange("p (a n) -> p a n", a=2), PS[:, 2:4, :],
                                                      COL["bq"], DH ** -0.5, ALU.add, ALU.mult))
                    step.wait()
                    step.mark(nc.vector.tensor_copy(q_hi[:, :], q_all[:, :]))
                    step.wait()
                    nc.vector.tensor_tensor(q_lo[:, :], q_all[:, :], q_hi[:, :].bitcast(F32), ALU.subtract
                                            ).then_inc(q_split, 1)

                    def take_max(b, j, n):
                        dve.wait_ge(max_scored, QT7 * KC * b + n + 1)
                        nc.vector.tensor_reduce(out=chunk_max[:, n // KC, n % KC:n % KC + 1],
                                                in_=PS[:, max_bank(b, j, n), 0:KW], axis=AX.X, op=ALU.max
                                                ).then_inc(max_taken, 1)

                    def join_max(b, a):
                        tiles = HALF_TILES[a]
                        dve.wait_ge(max_taken, QT7 * KC * b + tiles.stop * KC)
                        if later(b, 1):
                            dve.wait_ge(q_selected, 2 * b)
                        nc.vector.tensor_reduce(out=max_col[:, tiles, SHIFT_ROW], in_=chunk_max[:, tiles, :], axis=AX.X,
                                                op=ALU.max).then_inc(max_ready, 1)

                    def take_chunks(b, j, chunks):
                        for n in chunks:
                            take_max(b, j, n)
                            for a in range(2):
                                if n == HALF_TILES[a].stop * KC - 1:
                                    join_max(b, a)

                    def invert(b, a):
                        half = slice(2 * N * a, 2 * N * a + 2 * N)
                        dve.wait_ge(den_done, b + 1)
                        nc.vector.reciprocal(heads_out2[:, half], MISC[:, half]).then_inc(den_inverted, 1)

                    def scale_heads(b):
                        dve.wait_ge(den_inverted, 2 * b + 2)
                        nc.vector.tensor_tensor(heads_out2[:, :], heads_out2[:, :], heads_sum[:, :], ALU.mult
                                                ).then_inc(o_scaled, 1)

                    def residual(b, j, u):
                        dve.wait_ge(out_done, b + 1)
                        r = slice(PITCH * j, PITCH * j + N)
                        nc.vector.tensor_tensor(X[r, bass.ds(u, 1), :], X[r, bass.ds(u, 1), :],
                                                MISC[r, 0:D].unsqueeze(1), ALU.add).then_inc(x2_ready, 1)

                    take_chunks(0, 0, range(QT7 * KC))

                    def period(b, j, u):
                        for t in range(KT):
                            first, rest = max_chunks(t)
                            if exists(b + 1, B):
                                take_chunks(b + 1, 1 - j, first)
                                if t in VALUE_SLOTS:
                                    read_values(dve, b + 1, 1 - j, VALUE_SLOTS.index(t))
                            if later(b, 1):
                                if DEN_SLOT <= t < DEN_SLOT + 2:
                                    invert(b - 1, t - DEN_SLOT)
                                if t == DEN_SLOT + 2:
                                    scale_heads(b - 1)
                                if t == OUT_SLOT:
                                    residual(b - 1, 1 - j, u if j == 1 else u - 1)
                            if exists(b + 1, B):
                                take_chunks(b + 1, 1 - j, rest)

                    pipelined(dve, period, B)
                    for a in range(2):
                        invert(B - 1, a)
                    scale_heads(B - 1)
                    residual(B - 1, 1, PAIRS - 1)

                @block.tensor
                def _(pe):
                    pe.wait_ge(y2_ready, 1)
                    for c in range(2):
                        for p in range(4):
                            last = nc.tensor.transpose(PS[:, c, 128 * p:128 * p + 128], Y2[:, 4 * c + p, :], C["ident"])
                        last.then_inc(y2_turned, 1)
                    for c in range(2):
                        pe.wait_ge(y2_copied, c + 1)
                        nc.tensor.matmul(PS[:, 2 + c, :], MAT["wq"], T[:, c * 512:(c + 1) * 512], start=True, stop=True
                                         ).then_inc(q_projected, 1)

                    released = [None]

                    def shared_bank(after):
                        if released[0]:
                            pe.wait_ge(*released[0])
                        released[0] = after

                    def max_scores(b, j, n):
                        if n == 0:
                            pe.wait_ge(q_blocks, 2 * b + 1)
                            pe.wait_ge(k_ready, KC * (b + 1))
                        if later(b, 1):
                            pe.wait_ge(max_taken, QT7 * KC * b + n - 1)
                        elif n >= 6:
                            pe.wait_ge(max_taken, n - 5)
                        t, c = n // KC, n % KC
                        nc.tensor.matmul(PS[:, max_bank(b, j, n), 0:KW], q_block_hi[:, j, 128 * t:128 * t + 128],
                                         k_hi[:, j, KW * c:KW * c + KW], start=True, stop=True).then_inc(max_scored, 1)

                    def select_queries(b, j, a):
                        pe.wait_ge(q_blocks, 2 * b + 2)
                        pe.wait_ge(max_ready, 2 * b + a + 1)
                        shared_bank((q_stacked, 2 * b + a + 1))
                        cols_ = slice(a * HALF, (a + 1) * HALF)
                        nc.tensor.matmul(MISC[:, 0:HALF], sel[:, 0, :], q_block_hi[:, j, cols_], start=True, stop=False)
                        c0, c1 = a * HALF, (a + 1) * HALF
                        for t in range(QT7):
                            lo, hi = max(c0, 128 * t), min(c1, 128 * t + 128)
                            if lo < hi:
                                nc.tensor.matmul(MISC[:, lo - c0:hi - c0], max_col[:, t, :],
                                                 sel[:, 2, lo - 128 * t:hi - 128 * t], start=False, stop=False)
                        nc.tensor.matmul(MISC[:, 0:HALF], sel[:, 1, :], q_block_lo[:, j, cols_], start=False, stop=True
                                         ).then_inc(q_selected, 1)

                    def scores(b, j, u, t):
                        if t == 0:
                            pe.wait_ge(stack_loaded[j], 16 * STACK_DMAS * (u + 1))
                            pe.wait_ge(q_stacked, 2 * (b + 1))
                        if later(b, 1) or t >= 2:
                            pe.wait_ge(p_ready, KT * b + t - 1)
                        if t == KT - 1 and exists(b + 2, B):
                            pe.wait_ge(k_lo_ready, KC * (b + 3))
                        for g in range(GROUPS):
                            o = g % 2 * GH * N
                            last = nc.tensor.matmul(PS[0:KR, 2 * (t % 2) + g // 2, o:o + GH * N],
                                                    k_stack[:, j, g, KR * t:KR * t + KR],
                                                    q_stack[0:SHIFT_ROW + 1, j, g * GH * N:(g + 1) * GH * N],
                                                    start=True, stop=True)
                        last.then_inc(s_done, 1)

                    def weigh(b, j, t):
                        pe.wait_ge(p_ready, KT * b + t + 1)
                        if t == 0:
                            if later(b, 1):
                                pe.wait_ge(o_copied, b)
                            pe.wait_ge(v_ready, KC * (b + 1))
                        for r in range(2):
                            for k in range(4):
                                g = 4 * r + k
                                last = nc.tensor.matmul(PS[32 * k:32 * k + 32, 6, 2 * N * r:2 * N * r + 2 * N],
                                                        values[:, j, t, g, :], P[:, t % 3, 2 * N * g:2 * N * g + 2 * N],
                                                        start=(t == 0 and r == 0), stop=(t == KT - 1),
                                                        skip_group_check=True)
                        last.then_inc(pv_done, 1)

                    def denominators(b):
                        pe.wait_ge(o_copied, b + 1)
                        shared_bank((den_inverted, 2 * b + 2))
                        nc.tensor.matmul(MISC[:, 0:4 * N], C["den"], heads_sum[:, :], start=True, stop=True
                                         ).then_inc(den_done, 1)

                    def project_out(b, j):
                        pe.wait_ge(o_scaled, b + 2)
                        shared_bank((x2_ready, b + 1))
                        for n in range(4):
                            last = nc.tensor.matmul(MISC[PITCH * j:PITCH * j + N, 0:D], heads_out2[:, N * n:N * n + N],
                                                    MAT[f"wo{n}"], start=(n == 0), stop=(n == 3))
                        last.then_inc(out_done, 1)

                    for n in range(QT7 * KC):
                        max_scores(0, 0, n)
                    pe.wait_ge(sel_ready, 1)
                    for a in range(2):
                        select_queries(0, 0, a)
                    pe.wait_ge(ones_loaded, 16 * 2 * GROUPS)

                    def period(b, j, u):
                        released[0] = (q_stacked, 2 * (b + 1))
                        for t in range(KT):
                            first, rest = max_chunks(t)
                            scores(b, j, u, t)
                            if exists(b + 1, B):
                                for n in first:
                                    max_scores(b + 1, 1 - j, n)
                            if exists(b + 2, B) and t in KEY_SLOTS:
                                c = KEY_SLOTS.index(t)
                                shared_bank((k_ready, KC * (b + 2) + c + 1))
                                project_keys(pe, b + 2, j, u + 1, c)
                            if exists(b + 1, B) and t in VALUE_SLOTS:
                                c = VALUE_SLOTS.index(t)
                                shared_bank((v_ready, KC * (b + 1) + c + 1))
                                project_values(pe, b + 1, 1 - j, u if j == 0 else u + 1, c)
                            if later(b, 1):
                                if t == DEN_SLOT:
                                    denominators(b - 1)
                                if t == OUT_SLOT:
                                    project_out(b - 1, 1 - j)
                            if exists(b + 1, B):
                                if t in STACK_SLOTS:
                                    select_queries(b + 1, 1 - j, STACK_SLOTS.index(t))
                                for n in rest:
                                    max_scores(b + 1, 1 - j, n)
                            if t > 0:
                                weigh(b, j, t - 1)
                            elif later(b, 1):
                                weigh(b - 1, 1 - j, KT - 1)

                    pipelined(pe, period, B)
                    weigh(B - 1, 1, KT - 1)
                    denominators(B - 1)
                    project_out(B - 1, 1)


        s3 = ExitStack()

        def sb3(name, shape, dt=F32):
            return s3.enter_context(nc.sbuf_tensor(name, shape, dt))

        with s3:
            UNITS = 2 * IT
            Y3 = sb3("Y3", [128, PAIRS, D])
            w_gate_up = sb3("w_gate_up", [128, 2, 2 * I])
            w_hi = sb3("w_hi", [128, 2, 2 * I], F32R)
            w_lo = sb3("w_lo", [128, 2, 2 * I], F32R)
            T_hi = sb3("T_hi", [128, B, PITCH], F32R)
            T_lo = sb3("T_lo", [128, B, PITCH], F32R)
            w_down = sb3("w_down", [128, 2, IT, D])
            gated = sb3("gated", [128, 2, HALF])
            hidden = sb3("hidden", [128, 2, IT, B * PITCH])
            logit = sb3("logit", [128, PAIRS, E])
            beats = sb3("beats", [128, PAIRS, E, E])
            ties = sb3("ties", [128, PAIRS, E, E])
            rank = sb3("rank", [128, PAIRS, E])
            best = sb3("best", [128, PAIRS])
            weight = sb3("weight", [128, PAIRS, E])
            weight_sum = sb3("weight_sum", [128, PAIRS])
            weight_now = sb3("weight_now", [128, 2, PAIRS])

            y3_ready = sem("y3_ready")
            y3_turned = sem("y3_turned")
            y3_copied = sem("y3_copied")
            t_split = sem("t_split")
            w_rounded = sem("w_rounded")
            w_split = sem("w_split")
            routed = sem("routed")
            route_shifted = sem("route_shifted")
            route_exp = sem("route_exp")
            gaps_zero = sem("gaps_zero")
            gate_up_loaded = [sem("gate_up_loaded_0"), sem("gate_up_loaded_1")]
            down_loaded = [sem("down_loaded_0"), sem("down_loaded_1")]
            gate_done = sem("gate_done")
            up_done = sem("up_done")
            gated_ready = sem("gated_ready")
            hidden_ready = sem("hidden_ready")
            down_done = sem("down_done")
            weight_copied = sem("weight_copied")
            summed = sem("summed")
            FREE_BANKS = 4
            stored = sem("stored")

            def experts(engine, body):
                body(0, 0, 0)
                with engine.Fori(0, (E - 2) // 2) as i:
                    body(2 * i + 1, 1, i)
                    body(2 * i + 2, 0, i + 1)
                body(E - 1, 1, E // 2 - 1)

            with nc.Block() as block:

                @block.sync
                def _(sp):
                    def load_gate_up(e, j):
                        sp.dma_start(w_gate_up[:, j, :], wgu_in[bass.ds(e, 1), :, :].rearrange("a p n -> p (a n)")
                                     ).then_inc(gate_up_loaded[j], 16)

                    def load_down(e, j):
                        sp.dma_start(w_down[:, j, :, :], wd_in[bass.ds(e, 1), :, :, :].rearrange("a p t n -> p (a t) n")
                                     ).then_inc(down_loaded[j], 16)

                    sp.wait_ge(y3_ready, 1)
                    for e in range(2):
                        load_gate_up(e, e)
                        load_down(e, e)

                    def period(e, j, u):
                        if not isinstance(e, int) or e + 1 < E:
                            if later(e, 1):
                                sp.wait_ge(y3_ready, 1)
                                sp.wait_ge(w_split, e)
                                load_gate_up(e + 1, 1 - j)
                                sp.wait_ge(y3_ready, 1)
                                sp.wait_ge(down_done, 2 * e)
                                load_down(e + 1, 1 - j)

                    experts(sp, period)
                    sp.wait_ge(summed, FREE_BANKS + 2 * E)
                    sp.dma_start(out, X[:, :, :]).then_inc(stored, 16)
                    sp.wait_ge(stored, 16)

                @block.gpsimd
                def _(pool):
                    layernorm_power(pool, 4)
                    pool.wait_ge(y3_ready, 1)

                    def split(e, j):
                        pool.wait_ge(w_rounded, e + 1)
                        nc.gpsimd.tensor_tensor(w_lo[:, j, :], w_gate_up[:, j, :], w_hi[:, j, :].bitcast(F32), ALU.subtract
                                                ).then_inc(w_split, 1)

                    split(0, 0)
                    nc.gpsimd.memset(hidden[:, :, :, :], 0.0).then_inc(gaps_zero, 1)

                    def period(e, j, u):
                        if not isinstance(e, int) or e + 1 < E:
                            split(e + 1, 1 - j)

                    experts(pool, period)

                @block.scalar
                def _(act):
                    for c in range(2):
                        act.wait_ge(y3_turned, c + 1)
                        nc.scalar.copy(T_hi[:, 8 * c:8 * c + 8, :], PS[:, c, :].rearrange("p (b n) -> p b n", n=PITCH))
                        nc.scalar.copy(T[:, c * 512:(c + 1) * 512], PS[:, c, :]).then_inc(y3_copied, 1)

                    def round_weights(e, j, u):
                        if later(e, 2):
                            act.wait_ge(up_done, UNITS * (e - 1))
                        act.wait_ge(gate_up_loaded[j], 16 * (u + 1))
                        nc.scalar.copy(w_hi[:, j, :], w_gate_up[:, j, :]).then_inc(w_rounded, 1)

                    round_weights(0, 0, 0)
                    act.wait_ge(route_shifted, 1)
                    nc.scalar.activation(weight[:, :, :], weight[:, :, :], ACT.Exp).then_inc(route_exp, 1)

                    def period(e, j, u):
                        for k in range(UNITS):
                            act.wait_ge(gate_done, UNITS * e + k + 1)
                            if later(e, 1) or k >= 2:
                                act.wait_ge(hidden_ready, UNITS * e + k - 1)
                            nc.scalar.activation(gated[:, k % 2, :], PS[:, k % 2, 0:HALF], ACT.Silu
                                                 ).then_inc(gated_ready, 1)
                            if k == 1 and (not isinstance(e, int) or e + 1 < E):
                                round_weights(e + 1, 1 - j, u if j == 0 else u + 1)

                    experts(act, period)

                @block.vector
                def _(dve):
                    step = steps_of["dve"].again(dve)
                    dve.wait_ge(x2_ready, B)
                    layernorm(dve, step, 4, X, Y3).then_inc(y3_ready, 1)

                    dve.wait_ge(y3_copied, 2)
                    nc.vector.tensor_tensor(T_lo[:, :, :], Tb, T_hi[:, :, :].bitcast(F32), ALU.subtract).then_inc(t_split, 1)

                    dve.wait_ge(routed, 1)
                    step.mark(nc.vector.tensor_copy(logit[:, :, :], PS[:, 2, 0:PAIRS * E].rearrange("p (a e) -> p a e", e=E)))
                    step.wait()
                    other = logit[:, :, :].unsqueeze(2).broadcast_to([128, PAIRS, E, E])
                    own = logit[:, :, :].unsqueeze(3).broadcast_to([128, PAIRS, E, E])
                    nc.vector.tensor_reduce(out=best[:, :], in_=logit[:, :, :], axis=AX.X, op=ALU.max)
                    nc.vector.tensor_tensor(beats[:, :, :, :], other, own, ALU.is_gt)
                    step.mark(nc.vector.tensor_tensor(ties[:, :, :, :], other, own, ALU.is_equal))
                    step.wait()
                    nc.vector.tensor_tensor(weight[:, :, :], logit[:, :, :], best[:, :].unsqueeze(2).broadcast_to([128, PAIRS, E]),
                                            ALU.subtract).then_inc(route_shifted, 1)
                    before = C["before"].rearrange("p (e f) -> p e f", e=E).unsqueeze(1).broadcast_to([128, PAIRS, E, E])
                    step.mark(nc.vector.tensor_tensor(ties[:, :, :, :], ties[:, :, :, :], before, ALU.mult))
                    step.wait()
                    step.mark(nc.vector.tensor_tensor(beats[:, :, :, :], beats[:, :, :, :], ties[:, :, :, :], ALU.add))
                    step.wait()
                    step.mark(nc.vector.tensor_reduce(out=rank[:, :, :], in_=beats[:, :, :, :], axis=AX.X, op=ALU.add))
                    step.wait()
                    dve.wait_ge(route_exp, 1)
                    step.mark(nc.vector.scalar_tensor_tensor(weight[:, :, :], rank[:, :, :], 2.0, weight[:, :, :],
                                                             ALU.is_lt, ALU.mult))
                    step.wait()
                    step.mark(nc.vector.tensor_reduce(out=weight_sum[:, :], in_=weight[:, :, :], axis=AX.X, op=ALU.add))
                    step.wait()
                    step.mark(nc.vector.reciprocal(weight_sum[:, :], weight_sum[:, :]))
                    step.wait()
                    step.mark(nc.vector.tensor_tensor(weight[:, :, :], weight[:, :, :],
                                                      weight_sum[:, :].unsqueeze(2).broadcast_to([128, PAIRS, E]), ALU.mult))
                    step.wait()
                    dve.wait_ge(gaps_zero, 1)
                    nc.vector.tensor_copy(weight_now[:, 0, :], weight[:, :, 0]).then_inc(summed, FREE_BANKS)

                    def add_outputs(e, j, half):
                        if half == 0:
                            dve.wait_ge(summed, FREE_BANKS + 2 * e)
                            nc.vector.tensor_copy(weight_now[:, j, :], weight[:, :, bass.ds(e, 1)].rearrange("p a e -> p (a e)")
                                                  ).then_inc(weight_copied, 1)
                            dve.wait_ge(weight_copied, e + 1)
                        dve.wait_ge(down_done, 2 * e + half + 1)
                        dve.wait_ge(summed, FREE_BANKS + 2 * e + half - 1)
                        for p in range(4 * half, 4 * half + 4):
                            last = nc.vector.scalar_tensor_tensor(
                                X[:, p, :], PS[:, 4 + 2 * j + half, 128 * (p % 4):128 * (p % 4) + 128],
                                weight_now[:, j, p:p + 1], X[:, p, :], ALU.mult, ALU.add)
                        last.then_inc(summed, 1)

                    def period(e, j, u):
                        for k in range(UNITS):
                            c, t = k // IT, k % IT
                            dve.wait_ge(gated_ready, UNITS * e + k + 1)
                            dve.wait_ge(up_done, UNITS * e + k + 1)
                            nc.vector.tensor_tensor(
                                hidden[:, j, t, :].rearrange("p (b n) -> p b n", n=PITCH)[:, 8 * c:8 * c + 8, 0:N],
                                gated[:, k % 2, :].rearrange("p (b n) -> p b n", n=N),
                                PS[:, 2 + k % 2, 0:HALF].rearrange("p (b n) -> p b n", n=N), ALU.mult
                                ).then_inc(hidden_ready, 1)
                            if later(e, 1) and k % 4 == 3:
                                add_outputs(e - 1, 1 - j, k // 4)

                    experts(dve, period)
                    for half in range(2):
                        add_outputs(E - 1, 1, half)

                @block.tensor
                def _(pe):
                    pe.wait_ge(y3_ready, 1)
                    for c in range(2):
                        for p in range(4):
                            last = nc.tensor.transpose(PS[:, c, 128 * p:128 * p + 128], Y3[:, 4 * c + p, :], C["ident"])
                        last.then_inc(y3_turned, 1)
                    pe.wait_ge(y3_copied, 2)
                    for p in range(PAIRS):
                        last = nc.tensor.matmul(PS[:, 2, E * p:E * p + E], T[:, 128 * p:128 * p + 128], gate[:, :],
                                                start=True, stop=True)
                    last.then_inc(routed, 1)
                    pe.wait_ge(route_shifted, 1)
                    pe.wait_ge(t_split, 1)

                    def down(e, j, p):
                        if p % 4 == 0:
                            pe.wait_ge(hidden_ready, UNITS * e + p + 4)
                            pe.wait_ge(summed, 2 * e + p // 4 + 1)
                            if p == 0:
                                pe.wait_ge(down_loaded[j], 16 * (down_turn[0] + 1))
                        for t in range(IT):
                            last = nc.tensor.matmul(PS[:, 4 + 2 * j + p // 4, 128 * (p % 4):128 * (p % 4) + 128],
                                                    hidden[:, j, t, 128 * p:128 * p + 128], w_down[:, j, t, :],
                                                    start=(t == 0), stop=(t == IT - 1))
                        if p % 4 == 3:
                            last.then_inc(down_done, 1)

                    down_turn = [0]

                    def period(e, j, u):
                        down_turn[0] = u if j == 1 else u - 1
                        pe.wait_ge(w_split, e + 1)
                        for k in range(UNITS):
                            c, t = k // IT, k % IT
                            if later(e, 1) or k >= 2:
                                pe.wait_ge(hidden_ready, UNITS * e + k - 1)
                            for side, done in ((0, gate_done), (1, up_done)):
                                w = slice(I * side + 128 * t, I * side + 128 * t + 128)
                                bank = PS[:, 2 * side + k % 2, 0:HALF]
                                hi, lo = (part[:, 8 * c:8 * c + 8, 0:N] for part in (T_hi, T_lo))
                                nc.tensor.matmul(bank, w_hi[:, j, w], hi, start=True, stop=False)
                                nc.tensor.matmul(bank, w_hi[:, j, w], lo, start=False, stop=False)
                                nc.tensor.matmul(bank, w_lo[:, j, w], hi, start=False, stop=True).then_inc(done, 1)
                            if later(e, 1):
                                down(e - 1, 1 - j, k)

                    experts(pe, period)
                    down_turn[0] = E // 2 - 1
                    for p in range(PAIRS):
                        down(E - 1, 1, p)


def lay_out(a):
    a = {k: np.asarray(v) for k, v in a.items()}
    f = np.float32
    x = np.zeros((128, PAIRS, D), f)
    for e in range(2):
        x[PITCH * e:PITCH * e + N] = a["x"][e::2].transpose(1, 0, 2)
    wo_t = a["L0_xattn_wo"].T.reshape(2, 4, 2, DH, D)
    wo = np.zeros((2, 2, 4, 32, D), f)
    for r in range(2):
        for e in range(2):
            wo[r, e, :, DH * e:DH * e + DH] = wo_t[r, :, e]
    wo = wo.reshape(4, 128, D)
    mats = [a["L0_attn_" + n] for n in MATS[:6]] + [a["L0_xattn_" + n].T for n in MATS[6:9]] + list(wo)
    mats = np.ascontiguousarray(np.stack(mats, axis=1))
    rows = np.stack([a["L0_attn_gamma1"], a["L0_attn_gamma2"], a["L0_xattn_bv"], a["L0_xattn_bo"]])
    rows = np.ascontiguousarray(np.broadcast_to(rows, (128, 4, D)))
    cols = np.stack([a["L0_attn_ln1_w"], a["L0_attn_ln1_b"], a["L0_attn_ln2_w"], a["L0_attn_ln2_b"],
                     a["L0_xattn_bq"], a["L0_xattn_bk"],
                     np.repeat(a["L0_attn_tau_t"].reshape(H), DH), np.repeat(a["L0_attn_tau_c"].reshape(CH), CD)], axis=1)
    wgu = np.concatenate([a["L0_ffn_wg"].transpose(0, 2, 1), a["L0_ffn_wu"].transpose(0, 2, 1)], axis=2)
    wd = a["L0_ffn_wd"].reshape(E, D, IT, 128).transpose(0, 3, 2, 1)
    return {"x_in": x, "ctx_in": np.ascontiguousarray(a["ctx_1024"].transpose(0, 2, 1)), "mats_in": mats, "rows_in": rows,
            "cols_in": np.ascontiguousarray(cols), "gate_in": np.ascontiguousarray(a["L0_ffn_gate_w"].T),
            "consts_in": shape_constants()[0], "wgu_in": np.ascontiguousarray(wgu), "wd_in": np.ascontiguousarray(wd)}


def program(nc, arrays):
    args = {k: nc.dram_tensor(k, v.shape, mybir.dt.from_np(v.dtype), kind="ExternalInput").ap() for k, v in arrays.items()}
    out = nc.dram_tensor("out", (128, PAIRS, D), F32, kind="ExternalOutput").ap()
    build(nc, const_at=shape_constants()[1], out=out, **args)


def kernel(**inputs):
    import concourse.bacc as bacc
    from concourse.bass_utils import run_bass_kernel_spmd

    nc = bacc.Bacc("TRN2", target_bir_lowering=False, num_devices=1)
    arrays = lay_out(inputs)
    program(nc, arrays)
    got = run_bass_kernel_spmd(nc, [arrays], core_ids=[0]).results[0]["out"]
    y = np.empty((B, N, D), got.dtype)
    for e in range(2):
        y[e::2] = got[PITCH * e:PITCH * e + N].transpose(1, 0, 2)
    return y
```

```python
from contextlib import ExitStack

import numpy as np

import concourse.bass as bass
from concourse import mybir

F32 = mybir.dt.float32
F32R = mybir.dt.float32r
ALU = mybir.AluOpType
ACT = mybir.ActivationFunctionType
AX = mybir.AxisListType

B, N, D, S = 16, 56, 128, 1500
H, DH = 16, 8
CH, CD = 8, 16
E, I = 8, 512
EPS = 1e-5

PAIRS = B // 2
PITCH = 64
HQ = H * N
HALF = HQ // 2
KT, KR = 12, S // 12
KC = 3
KW = S // KC
QT7 = HQ // 128
IT = I // 128
TT = B * N // 128
GH = 4
GROUPS = H // GH
SHIFT_ROW = 3 * GH * DH
OFF_BLOCK = 1e30

MATS = ["Wqk_t", "Wv_t", "Wo_t", "Wqk_c", "Wv_c", "Wo_c", "wq", "wk", "wv", "wo0", "wo1", "wo2", "wo3"]
ROWS = ["gamma1", "gamma2", "bv", "bo"]
COLS = ["ln1_w", "ln1_b", "ln2_w", "ln2_b", "bq", "bk", "tau_t", "tau_c"]


class Steps:

    def __init__(self, engine, sem):
        self.engine, self.sem, self.n = engine, sem, 0

    def mark(self, instruction):
        instruction.then_inc(self.sem, 1)
        self.n += 1

    def wait(self):
        self.engine.wait_ge(self.sem, self.n)

    def again(self, engine):
        self.engine = engine
        return self


def shape_constants():
    row = np.arange(128)
    ident = np.eye(128)
    head = (row[:, None] // DH == np.arange(H)[None, :]) * 1.0
    sel = np.zeros((2, 128, 128))
    for q, part in enumerate((0, 0, 1)):
        sel[part, row, 32 * q + row % 32] = 1.0
    den = (row[:, None] == 32 * (row[None, :] // 32) + 16) * 1.0
    quarter = (row[:, None] // DH % 4 == np.arange(4)[None, :]) * 1.0
    block = np.where(row[:, None] // CD == row[None, :] // CD, 0.0, OFF_BLOCK)
    before = np.broadcast_to((np.arange(E)[None, :] < np.arange(E)[:, None]) * 1.0, (128, E, E)).reshape(128, -1)
    parts = {"ident": ident, "neg_ident": -ident, "sel_hi": sel[0], "sel_lo": sel[1], "den": den, "block": block,
             "ones": np.ones((128, 128)), "head": head, "quarter": quarter, "before": before}
    at, lots, n = {}, [], 0
    for name, a in parts.items():
        at[name] = (n, a.shape[1])
        lots.append(a.astype(np.float32))
        n += a.shape[1]
    return np.concatenate(lots, axis=1), at


def build(nc, x_in, ctx_in, mats_in, rows_in, cols_in, gate_in, consts_in, const_at, wgu_in, wd_in, out):
    ctx = ExitStack()
    with ctx:
        def sb(name, shape, dt=F32):
            return ctx.enter_context(nc.sbuf_tensor(name, shape, dt))

        def sem(name):
            return ctx.enter_context(nc.semaphore(name))

        PS = ctx.enter_context(nc.psum_tensor("PS", [128, 8, 512], F32))

        X = sb("X", [128, PAIRS, D])
        mats = sb("mats", [128, len(MATS), D])
        rows = sb("rows", [128, len(ROWS), D])
        cols = sb("cols", [128, len(COLS)])
        gate = sb("gate", [128, E])
        consts = sb("consts", [128, consts_in.shape[1]])
        MAT = {n: mats[:, k, :] for k, n in enumerate(MATS)}
        ROW = {n: rows[:, k, :] for k, n in enumerate(ROWS)}
        COL = {n: cols[:, k:k + 1] for k, n in enumerate(COLS)}
        C = {n: consts[:, a:a + w] for n, (a, w) in const_at.items()}
        stats = sb("stats", [128, PAIRS, 6])
        moments = sb("moments", [128, PAIRS, 2])
        rstd = sb("rstd", [128, PAIRS])
        minus_half = sb("minus_half", [128, PAIRS])
        T = sb("T", [128, PAIRS * 128])
        Tb = T[:, :].rearrange("p (b n) -> p b n", n=PITCH)

        x_loaded = sem("x_loaded")
        consts_loaded = sem("consts_loaded")
        weights_loaded = sem("weights_loaded")
        dve_steps = sem("dve_steps")
        moments_ready = sem("moments_ready")
        eps_added = sem("eps_added")
        rstd_ready = sem("rstd_ready")

        steps_of = {}

        def layernorm(dve, step, number, src, dst, ready):
            for p in range(PAIRS):
                last = nc.vector.bn_stats(out=stats[:, p, :], in_=src[:, p, :])
            step.mark(last)
            step.wait()
            for p in range(PAIRS):
                last = nc.vector.bn_aggr(out=moments[:, p, :], in_=stats[:, p, :])
            last.then_inc(moments_ready, 1)
            dve.wait_ge(rstd_ready, number + 1)
            for p in range(PAIRS):
                last = nc.vector.tensor_scalar(dst[:, p, :], src[:, p, :], moments[:, p, 0:1], rstd[:, p:p + 1],
                                               ALU.subtract, ALU.mult)
                if p % (PAIRS // 2) == PAIRS // 2 - 1:
                    last.then_inc(ready, 1)

        def layernorm_power(pool, number):
            pool.wait_ge(moments_ready, number + 1)
            nc.gpsimd.tensor_scalar(rstd[:, :], moments[:, :, 1], EPS, None, ALU.add).then_inc(eps_added, 1)
            pool.wait_ge(eps_added, number + 2)
            nc.gpsimd.tensor_tensor(rstd[:, :], rstd[:, :], minus_half[:, :], ALU.pow).then_inc(rstd_ready, 1)

        def pipelined(engine, body, count):
            body(0, 0, 0)
            with engine.Fori(0, (count - 4) // 2) as i:
                body(2 * i + 1, 1, i)
                body(2 * i + 2, 0, i + 1)
            for n in range(count - 3, count):
                body(n, n % 2, n // 2)

        def exists(n, count):
            return not isinstance(n, int) or n < count

        def later(n, first):
            return not isinstance(n, int) or n >= first

        sel = sb("sel", [128, 3, 128], F32R)
        ctxT = sb("ctxT", [128, 2, S])
        k_full = sb("k_full", [128, S])
        k_hi = sb("k_hi", [128, 2, S], F32R)
        k_lo = sb("k_lo", [128, 2, S], F32R)
        max_col = sb("max_col", [128, QT7, 128], F32R)
        values = sb("values", [KR, 2, KT, H // 2, 32])

        ctx_loaded = [sem("ctx_loaded_0"), sem("ctx_loaded_1")]
        stack_loaded = [sem("stack_loaded_0"), sem("stack_loaded_1")]
        k_projected = sem("k_projected")
        k_ready = sem("k_ready")
        k_lo_ready = sem("k_lo_ready")
        v_projected = sem("v_projected")
        v_ready = sem("v_ready")
        max_scored = sem("max_scored")
        pv_done = sem("pv_done")
        sel_ready = sem("sel_ready")
        cleared = sem("cleared")

        MISC = PS[:, 7, :]
        SPARE = PS[:, 6, :]

        def load_ctx(sp, b, j):
            sp.dma_start(ctxT[:, j, :], ctx_in[bass.ds(b, 1), :, :].rearrange("a p k -> p (a k)")
                         ).then_inc(ctx_loaded[j], 16)

        def project_keys(pe, b, j, u, c):
            if c == 0:
                pe.wait_ge(ctx_loaded[j], 16 * (u + 1))
            nc.tensor.matmul(MISC[:, 0:KW], MAT["wk"], ctxT[:, j, KW * c:KW * c + KW], start=True, stop=True
                             ).then_inc(k_projected, 1)

        def project_values(pe, b, j, u, c, bank=MISC):
            if c == 0:
                pe.wait_ge(ctx_loaded[j], 16 * (u + 1))
            for t in range(4):
                k0 = KR * (4 * c + t)
                last = nc.tensor.matmul(bank[0:KR, 128 * t:128 * t + 128], ctxT[:, j, k0:k0 + KR], MAT["wv"],
                                        start=True, stop=True)
            last.then_inc(v_projected, 1)

        def first_keys(pe, b):
            for c in range(KC):
                if c > 0:
                    pe.wait_ge(k_ready, KC * b + c)
                project_keys(pe, b, b, 0, c)

        def read_keys(act, b, j, u, c):
            if c == 0:
                if later(b, 2):
                    act.wait_ge(stack_loaded[j], 16 * STACK_DMAS * u)
                    act.wait_ge(max_scored, QT7 * KC * (b - 1))
            if later(b, 1):
                act.wait_ge(k_lo_ready, KC * (b - 1) + c + 1)
            act.wait_ge(k_projected, KC * b + c + 1)
            k = slice(KW * c, KW * c + KW)
            nc.scalar.activation(k_hi[:, j, k], MISC[:, 0:KW], ACT.Identity, bias=COL["bk"])
            nc.scalar.activation(k_full[:, k], MISC[:, 0:KW], ACT.Identity, bias=COL["bk"]
                                 ).then_inc(k_ready, 1)

        def lower_keys(pool, b, j, u):
            if later(b, 2):
                pool.wait_ge(stack_loaded[j], 16 * STACK_DMAS * u)
            for c in range(KC):
                pool.wait_ge(k_ready, KC * b + c + 1)
                k = slice(KW * c, KW * c + KW)
                nc.gpsimd.tensor_tensor(k_lo[:, j, k], k_full[:, k], k_hi[:, j, k].bitcast(F32), ALU.subtract
                                        ).then_inc(k_lo_ready, 1)

        def read_values(dve, b, j, c, bank=MISC):
            dve.wait_ge(v_projected, KC * b + c + 1)
            if c == 0 and later(b, 2):
                dve.wait_ge(pv_done, KT * (b - 1))
            nc.vector.tensor_tensor(
                values[:, j, 4 * c:4 * c + 4, :, 0:2 * DH],
                bank[0:KR, :].rearrange("p (t g d) -> p t g d", t=4, g=H // 2),
                ROW["bv"][0:KR].rearrange("p (g d) -> p g d", g=H // 2).unsqueeze(1)
                .broadcast_to([KR, 4, H // 2, 2 * DH]), ALU.add).then_inc(v_ready, 1)

        s1 = ExitStack()

        def sb1(name, shape, dt=F32):
            return s1.enter_context(nc.sbuf_tensor(name, shape, dt))

        with s1:
            Z = sb1("Z", [128, PAIRS, D])
            Y = sb1("Y", [128, PAIRS, D])
            qkT = sb1("qkT", [128, PAIRS * 128])
            v_all = sb1("v_all", [N, B, D])
            coef = sb1("coef", [128, 3])
            scaled = sb1("scaled", [128, PAIRS * 128])
            squared = sb1("squared", [128, PAIRS * 128])
            qk_pair = sb1("qk_pair", [128, 2, 128])
            v_pair = sb1("v_pair", [N, 2, 2, D])
            q_block = sb1("q_block", [128, 2, 2, HQ])
            q_square = sb1("q_square", [128, 2, 2, HQ])
            row_max = sb1("row_max", [128, 2, H])
            row_sum = sb1("row_sum", [128, 2, H])
            probs = sb1("probs", [128, 2, HQ])
            probsT = sb1("probsT", [N, 2, H, 128])
            heads_out = sb1("heads_out", [128, 2, 2, 4 * PITCH])
            wo_quarter = sb1("wo_quarter", [128, 4, D])
            wo_scaled = sb1("wo_scaled", [128, 2, D])
            gram_left = sb1("gram_left", [128, B, D])
            gram_right = sb1("gram_right", [128, B, D])
            gram = sb1("gram", [128, B, D])
            gmin = sb1("gmin", [128, B])
            gsum = sb1("gsum", [128, B])

            z_ready = sem("z_ready")
            y_ready = sem("y_ready")
            y_turned = sem("y_turned")
            y_copied = sem("y_copied")
            coef_ready = sem("coef_ready")
            wo_ready = sem("wo_ready")
            qk_projected = sem("qk_projected")
            qk_read = sem("qk_read")
            v1_projected = sem("v1_projected")
            v_all_ready = sem("v_all_ready")
            scaled_ready = sem("scaled_ready")
            qk_copied = sem("qk_copied")
            v_copied = sem("v_copied")
            blocks_dve = sem("blocks_dve")
            blocks_pool = sem("blocks_pool")
            logits_done = sem("logits_done")
            max_done = sem("max_done")
            shifted_ready = sem("shifted_ready")
            exp_ready = sem("exp_ready")
            sum_done = sem("sum_done")
            inverse_done = sem("inverse_done")
            probs_ready = sem("probs_ready")
            turned = sem("turned")
            turned_copied = [sem("turned_copied_0"), sem("turned_copied_1")]
            pv1_done = sem("pv1_done")
            pv1_copied = sem("pv1_copied")
            out1_done = sem("out1_done")
            out1_added = sem("out1_added")
            qkc_projected = sem("qkc_projected")
            squares_ready = sem("squares_ready")
            upper_ready = sem("upper_ready")
            left_filled = sem("left_filled")
            vc_projected = sem("vc_projected")
            vc_ready = sem("vc_ready")
            gram_done = sem("gram_done")
            gram_shift = sem("gram_shift")
            gram_exp = sem("gram_exp")
            gram_ready = sem("gram_ready")
            mixed = sem("mixed")
            mixed_copied = sem("mixed_copied")
            outc_done = sem("outc_done")
            x1_ready = sem("x1_ready")

            HEADS = PS[:, 6, :]
            OUT1 = PS[:, 7, 0:D]

            def batch_block(src, p, e):
                v = src[:, :].rearrange("q (b n) -> q b n", n=PITCH)
                return v[:, bass.ds(2 * p + e, 1), 0:N].broadcast_to([128, H, N])

            def by_head(tile):
                return tile.rearrange("p (h n) -> p h n", n=N)

            T2 = q_block[:, :, :, :].rearrange("p a e n -> p (a e n)")[:, 0:2 * B * PITCH].rearrange(
                "p (b a n) -> p b a n", b=B, a=2)
            HEAD_MASK = C["head"].unsqueeze(2).broadcast_to([128, H, N])

            with nc.Block() as block:

                @block.sync
                def _(sp):
                    sp.dma_start(X[:, :, :], x_in).then_inc(x_loaded, 16)
                    sp.dma_start(consts[:, :], consts_in).then_inc(consts_loaded, 16)
                    sp.dma_start(cols[:, :], cols_in).then_inc(consts_loaded, 16)
                    sp.dma_start(rows[:, :, :], rows_in).then_inc(consts_loaded, 16)
                    sp.dma_start(mats[:, :, :], mats_in).then_inc(weights_loaded, 16)
                    sp.dma_start(gate[:, :], gate_in).then_inc(weights_loaded, 16)
                    load_ctx(sp, 0, 0)
                    load_ctx(sp, 1, 1)

                @block.gpsimd
                def _(pool):
                    nc.gpsimd.memset(minus_half[:, :], -0.5).then_inc(eps_added, 1)
                    layernorm_power(pool, 0)
                    layernorm_power(pool, 1)
                    pool.wait_ge(consts_loaded, 48)
                    pool.wait_ge(scaled_ready, 1)

                    def blocks(p, j):
                        if later(p, 2):
                            pool.wait_ge(logits_done, p - 1)
                        if later(p, 1):
                            nc.gpsimd.tensor_tensor(by_head(q_block[:, j, 0, :]), batch_block(scaled, p, 0), HEAD_MASK,
                                                    ALU.mult)
                        for e in range(2):
                            last = nc.gpsimd.tensor_tensor(by_head(q_square[:, j, e, :]), batch_block(squared, p, e),
                                                           HEAD_MASK, ALU.mult)
                        last.then_inc(blocks_pool, 1)

                    for p in range(3):
                        blocks(p, p % 2)

                    def turn(p, j, u):
                        if exists(p + 3, PAIRS):
                            blocks(p + 3, 1 - j)

                    pipelined(pool, turn, PAIRS)
                    nc.gpsimd.memset(gram_left[:, :, :], -0.5).then_inc(left_filled, 1)
                    layernorm_power(pool, 2)

                    nc.gpsimd.memset(max_col[:, :, :].bitcast(F32), 0.0)
                    lower_keys(pool, 0, 0, 0)
                    nc.gpsimd.memset(values[:, :, :, :, :], 1.0).then_inc(cleared, 1)

                @block.scalar
                def _(act):
                    act.wait_ge(consts_loaded, 48)
                    for c in range(2):
                        act.wait_ge(y_turned, c + 1)
                        nc.scalar.activation(T[:, c * 512:(c + 1) * 512], PS[:, c, :], ACT.Identity,
                                             bias=COL["ln1_b"], scale=COL["ln1_w"]).then_inc(y_copied, 1)
                    for c in range(2):
                        act.wait_ge(qk_projected, c + 1)
                        nc.scalar.copy(qkT[:, c * 512:(c + 1) * 512], PS[:, 2 + c, :]).then_inc(qk_read, 1)
                    act.wait_ge(qk_read, 2)

                    def copy_qk(p, j):
                        if later(p, 2):
                            act.wait_ge(logits_done, p - 1)
                        nc.scalar.copy(qk_pair[:, j, :], qkT[:, bass.ts(p, 128)]).then_inc(qk_copied, 1)

                    def copy_v(p, j):
                        nc.scalar.copy(v_pair[:, j, :, :], v_all[:, bass.ts(p, 2), :]).then_inc(v_copied, 1)

                    def exp(p, j):
                        act.wait_ge(shifted_ready, p + 1)
                        nc.scalar.activation(probs[:, j, :], probs[:, j, :], ACT.Exp).then_inc(exp_ready, 1)

                    copy_qk(0, 0)
                    copy_qk(1, 1)
                    for c in range(4):
                        act.wait_ge(v1_projected, c + 1)
                        nc.scalar.copy(v_all[:, 4 * c:4 * c + 4, :],
                                       PS[0:N, 4 + c, :].rearrange("p (b d) -> p b d", b=4)).then_inc(v_all_ready, 1)
                    act.wait_ge(v_all_ready, 4)
                    copy_v(0, 0)
                    copy_v(1, 1)
                    exp(0, 0)

                    def turn(p, j, u):
                        if exists(p + 2, PAIRS):
                            copy_qk(p + 2, j)
                        for a in range(2):
                            for c in range(2):
                                act.wait_ge(turned, 4 * p + 2 * a + c + 1)
                                h0 = 8 * a + 4 * c
                                last = nc.scalar.copy(probsT[:, j, h0:h0 + 4, :],
                                                      PS[0:N, 4 + c, :].rearrange("p (h n) -> p h n", h=4))
                            last.then_inc(turned_copied[a], 1)
                            if a == 0 and exists(p + 1, PAIRS):
                                exp(p + 1, 1 - j)
                        act.wait_ge(pv1_done, p + 1)
                        nc.scalar.copy(heads_out[:, j, :, :], HEADS.rearrange("p (e n) -> p e n", e=2)
                                       ).then_inc(pv1_copied, 1)
                        if exists(p + 2, PAIRS):
                            copy_v(p + 2, j)

                    pipelined(act, turn, PAIRS)
                    for c in range(KC):
                        read_keys(act, 0, 0, 0, c)

                    for c in range(2):
                        act.wait_ge(y_turned, c + 3)
                        once = PS[:, c, :].rearrange("p (b n) -> p b n", n=PITCH).unsqueeze(2)
                        nc.scalar.activation(T2[:, 8 * c:8 * c + 8, :, :], once.broadcast_to([128, B // 2, 2, PITCH]),
                                             ACT.Identity, bias=COL["ln2_b"], scale=COL["ln2_w"]).then_inc(y_copied, 1)
                    for c in range(4):
                        act.wait_ge(qkc_projected, c + 1)
                        r = slice(PITCH, 2 * PITCH)
                        nc.scalar.activation(gram_right[r, 4 * c:4 * c + 4, :],
                                             PS[r, 2 + c, :].rearrange("p (b d) -> p b d", b=4), ACT.Square
                                             ).then_inc(squares_ready, 1)
                    for c in range(2):
                        act.wait_ge(vc_projected, c + 1)
                        nc.scalar.copy(qkT[:, c * 512:(c + 1) * 512], PS[:, 6 + c, :]).then_inc(vc_ready, 1)
                    for c in range(2):
                        act.wait_ge(gram_shift, c + 1)
                        for g in range(8 * c, 8 * c + 8):
                            last = nc.scalar.activation(gram[:, g, :], gram[:, g, :], ACT.Exp, bias=gmin[:, g:g + 1],
                                                        scale=-1.0, accum_out=gsum[:, g:g + 1])
                        last.then_inc(gram_exp, 1)
                    for c in range(2):
                        act.wait_ge(mixed, c + 1)
                        nc.scalar.copy(gram[:, 8 * c:8 * c + 8, :],
                                       PS[:, 2 * c:2 * c + 2, :].rearrange("p a (b d) -> p (a b) d", b=4)
                                       ).then_inc(mixed_copied, 1)

                @block.vector
                def _(dve):
                    step = Steps(dve, dve_steps)
                    steps_of["dve"] = step
                    dve.wait_ge(x_loaded, 16)
                    layernorm(dve, step, 0, X, Z, z_ready)
                    dve.wait_ge(z_ready, 2)
                    layernorm(dve, step, 1, Z, Y, y_ready)
                    dve.wait_ge(consts_loaded, 48)
                    nc.vector.tensor_scalar(coef[:, 0:1], COL["tau_t"], 2.0 / DH ** 0.5, None, ALU.mult)
                    nc.vector.tensor_scalar(coef[:, 1:2], COL["tau_t"], -1.0 / DH ** 0.5, None, ALU.mult)
                    nc.vector.tensor_scalar(coef[:, 2:3], COL["tau_c"], -2.0 / N ** 0.5, None, ALU.mult
                                            ).then_inc(coef_ready, 1)
                    dve.wait_ge(coef_ready, 1)
                    dve.wait_ge(qk_read, 2)
                    nc.vector.tensor_scalar(scaled[:, :], qkT[:, :], coef[:, 0:1], None, ALU.mult)
                    nc.vector.scalar_tensor_tensor(squared[:, :], qkT[:, :], coef[:, 1:2], qkT[:, :], ALU.mult, ALU.mult
                                                   ).then_inc(scaled_ready, 1)

                    def blocks(p, j):
                        if later(p, 2):
                            dve.wait_ge(logits_done, p - 1)
                        for e in range(1 if later(p, 1) else 0, 2):
                            last = nc.vector.tensor_tensor(by_head(q_block[:, j, e, :]), batch_block(scaled, p, e),
                                                           HEAD_MASK, ALU.mult)
                        last.then_inc(blocks_dve, 1)

                    def logit_half(j, a):
                        return by_head(PS[:, 2 * j + a, 0:HALF])

                    def shift(p, j):
                        dve.wait_ge(logits_done, p + 1)
                        for a in range(2):
                            last = nc.vector.tensor_reduce(out=row_max[:, j, 8 * a:8 * a + 8], in_=logit_half(j, a),
                                                           axis=AX.X, op=ALU.max)
                        last.then_inc(max_done, 1)
                        dve.wait_ge(max_done, p + 1)
                        if later(p, 2):
                            dve.wait_ge(turned, 4 * (p - 1))
                        for a in range(2):
                            last = nc.vector.tensor_tensor(
                                by_head(probs[:, j, a * HALF:(a + 1) * HALF]), logit_half(j, a),
                                row_max[:, j, 8 * a:8 * a + 8].unsqueeze(2).broadcast_to([128, 8, N]), ALU.subtract)
                        last.then_inc(shifted_ready, 1)

                    def normalise(p, j):
                        dve.wait_ge(exp_ready, p + 1)
                        tile = by_head(probs[:, j, :])
                        nc.vector.tensor_reduce(out=row_sum[:, j, :], in_=tile, axis=AX.X, op=ALU.add).then_inc(sum_done, 1)
                        dve.wait_ge(sum_done, p + 1)
                        nc.vector.reciprocal(row_sum[:, j, :], row_sum[:, j, :]).then_inc(inverse_done, 1)
                        dve.wait_ge(inverse_done, p + 1)
                        nc.vector.tensor_tensor(tile, tile, row_sum[:, j, :].unsqueeze(2).broadcast_to([128, H, N]),
                                                ALU.mult).then_inc(probs_ready, 1)

                    nc.vector.tensor_copy(sel[:, 0, :], C["sel_hi"]).then_inc(out1_added, 1)
                    nc.vector.tensor_copy(sel[:, 1, :], C["sel_lo"])
                    nc.vector.tensor_copy(sel[:, 2, :], C["neg_ident"]).then_inc(sel_ready, 1)
                    dve.wait_ge(scaled_ready, 1)
                    for p in range(3):
                        blocks(p, p % 2)
                        if p == 1:
                            dve.wait_ge(weights_loaded, 32)
                            nc.vector.tensor_tensor(wo_scaled[:, 0, :], MAT["Wo_t"], ROW["gamma1"], ALU.mult)
                            step.mark(nc.vector.tensor_tensor(wo_scaled[:, 1, :], MAT["Wo_c"], ROW["gamma2"], ALU.mult))
                            step.wait()
                            for k in range(4):
                                last = nc.vector.tensor_scalar(wo_quarter[:, k, :], wo_scaled[:, 0, :],
                                                               C["quarter"][:, k:k + 1], None, ALU.mult)
                            last.then_inc(wo_ready, 1)
                    shift(0, 0)
                    normalise(0, 0)

                    def add_heads(p):
                        dve.wait_ge(out1_done, p + 1)
                        nc.vector.tensor_tensor(Z[:, bass.ds(p, 1), :], Z[:, bass.ds(p, 1), :], OUT1.unsqueeze(1), ALU.add
                                                ).then_inc(out1_added, 1)

                    def turn(p, j, u):
                        if exists(p + 1, PAIRS):
                            shift(p + 1, 1 - j)
                        if exists(p + 3, PAIRS):
                            blocks(p + 3, 1 - j)
                        if later(p, 1):
                            add_heads(p - 1)
                        if exists(p + 1, PAIRS):
                            normalise(p + 1, 1 - j)

                    pipelined(dve, turn, PAIRS)
                    add_heads(PAIRS - 1)

                    dve.wait_ge(out1_added, PAIRS + 1)
                    layernorm(dve, step, 2, Z, Y, y_ready)
                    step.mark(nc.vector.tensor_tensor(X[:, :, :], X[:, :, :], Z[:, :, :], ALU.add))
                    dve.wait_ge(left_filled, 1)
                    step.mark(nc.vector.memset(gram_left[PITCH // 2:PITCH, :, :], 0.0))
                    step.wait()
                    for c in range(4):
                        dve.wait_ge(qkc_projected, c + 1)
                        for side, r in ((gram_right, PITCH), (gram_left, N)):
                            last = nc.vector.tensor_copy(side[0:r, 4 * c:4 * c + 4, :],
                                                         PS[0:r, 2 + c, :].rearrange("p (b d) -> p b d", b=4))
                        last.then_inc(upper_ready, 1)
                    mask = C["block"].unsqueeze(1).broadcast_to([128, 8, D])
                    for c in range(2):
                        part = gram[:, 8 * c:8 * c + 8, :]
                        dve.wait_ge(gram_done, c + 1)
                        step.mark(nc.vector.scalar_tensor_tensor(
                            part, PS[:, 2 * c:2 * c + 2, :].rearrange("p a (b d) -> p (a b) d", b=4), coef[:, 2:3], mask,
                            ALU.mult, ALU.add))
                        step.wait()
                        nc.vector.tensor_reduce(out=gmin[:, 8 * c:8 * c + 8], in_=part, axis=AX.X, op=ALU.min
                                                ).then_inc(gram_shift, 1)
                    for c in range(2):
                        part, total = gram[:, 8 * c:8 * c + 8, :], gsum[:, 8 * c:8 * c + 8]
                        dve.wait_ge(gram_exp, c + 1)
                        step.mark(nc.vector.reciprocal(total, total))
                        step.wait()
                        nc.vector.tensor_tensor(part, part, total.unsqueeze(2).broadcast_to([128, 8, D]), ALU.mult
                                                ).then_inc(gram_ready, 1)
                    dve.wait_ge(cleared, 1)
                    for c in range(2):
                        read_values(dve, 0, 0, c, (SPARE, MISC)[c])
                    for c in range(2):
                        dve.wait_ge(outc_done, c + 1)
                        nc.vector.tensor_tensor(X[:, 4 * c:4 * c + 4, :], X[:, 4 * c:4 * c + 4, :],
                                                PS[:, 4 + c, :].rearrange("p (b d) -> p b d", b=4), ALU.add
                                                ).then_inc(x1_ready, 1)
                    read_values(dve, 0, 0, 2, SPARE)
                    dve.wait_ge(x1_ready, 2)

                @block.tensor
                def _(pe):
                    def turn_tokens(number):
                        for c in range(2):
                            pe.wait_ge(y_ready, 2 * number + c + 1)
                            for p in range(4):
                                last = nc.tensor.transpose(PS[:, c, 128 * p:128 * p + 128], Y[:, 4 * c + p, :], C["ident"])
                            last.then_inc(y_turned, 1)

                    pe.wait_ge(consts_loaded, 48)
                    turn_tokens(0)
                    pe.wait_ge(weights_loaded, 32)
                    for c in range(2):
                        pe.wait_ge(y_copied, c + 1)
                        nc.tensor.matmul(PS[:, 2 + c, :], MAT["Wqk_t"], T[:, c * 512:(c + 1) * 512], start=True, stop=True
                                         ).then_inc(qk_projected, 1)
                    for b in range(B):
                        mm = nc.tensor.matmul(PS[0:N, 4 + b // 4, 128 * (b % 4):128 * (b % 4) + 128], Tb[:, b, 0:N],
                                              MAT["Wv_t"], start=True, stop=True)
                        if b % 4 == 3:
                            mm.then_inc(v1_projected, 1)

                    def logit_products(p, j, a):
                        if a == 0:
                            pe.wait_ge(blocks_dve, p + 1)
                            pe.wait_ge(blocks_pool, p + 1)
                            pe.wait_ge(qk_copied, p + 1)
                            if later(p, 2):
                                pe.wait_ge(shifted_ready, p - 1)
                        for e in range(2):
                            nc.tensor.matmul(PS[PITCH * e:PITCH * e + PITCH, 2 * j + a, 0:HALF],
                                             qk_pair[:, j, PITCH * e:PITCH * e + PITCH],
                                             q_block[:, j, e, a * HALF:(a + 1) * HALF], start=True, stop=False)

                    def logit_squares(p, j, a):
                        for e in range(2):
                            last = nc.tensor.matmul(PS[PITCH * e:PITCH * e + PITCH, 2 * j + a, 0:HALF],
                                                    C["ones"][:, 0:PITCH],
                                                    q_square[:, j, e, a * HALF:(a + 1) * HALF], start=False, stop=True)
                        if a == 1:
                            last.then_inc(logits_done, 1)

                    def turn_probs(p, j, a):
                        for h in range(8):
                            last = nc.tensor.transpose(PS[0:N, 4 + h // 4, 128 * (h % 4):128 * (h % 4) + 128],
                                                       probs[:, j, (8 * a + h) * N:(8 * a + h + 1) * N], C["ident"])
                            if h % 4 == 3:
                                last.then_inc(turned, 1)

                    def attend(p, j):
                        pe.wait_ge(v_all_ready, 4)
                        pe.wait_ge(v_copied, p + 1)
                        pe.wait_ge(turned_copied[1], p + 1)
                        for e in range(2):
                            for k in range(4):
                                last = nc.tensor.matmul(
                                    PS[32 * k:32 * k + 32, 6, 256 * e:256 * e + 256], v_pair[:, j, e, 32 * k:32 * k + 32],
                                    probsT[:, j, 4 * k:4 * k + 4, PITCH * e:PITCH * e + PITCH], start=True, stop=True)
                        last.then_inc(pv1_done, 1)

                    def project_heads(p, j):
                        pe.wait_ge(pv1_copied, p + 1)
                        pe.wait_ge(out1_added, p + 1)
                        if not isinstance(p, int) or p + 1 < PAIRS:
                            pe.wait_ge(probs_ready, p + 2)
                        for k in range(4):
                            for e in range(2):
                                last = nc.tensor.matmul(PS[PITCH * e:PITCH * e + PITCH, 7, 0:D],
                                                        heads_out[:, j, e, PITCH * k:PITCH * k + PITCH], wo_quarter[:, k, :],
                                                        start=(k == 0), stop=(k == 3))
                        last.then_inc(out1_done, 1)

                    for p in range(2):
                        for a in range(2):
                            logit_products(p, p, a)
                            logit_squares(p, p, a)
                    pe.wait_ge(v_all_ready, 4)
                    pe.wait_ge(wo_ready, 1)
                    pe.wait_ge(probs_ready, 1)

                    def turn(p, j, u):
                        if later(p, 1):
                            project_heads(p - 1, 1 - j)
                        turn_probs(p, j, 0)
                        if exists(p + 2, PAIRS):
                            logit_products(p + 2, j, 0)
                        pe.wait_ge(turned_copied[0], p + 1)
                        if exists(p + 2, PAIRS):
                            logit_squares(p + 2, j, 0)
                        turn_probs(p, j, 1)
                        if exists(p + 2, PAIRS):
                            logit_products(p + 2, j, 1)
                        attend(p, j)
                        if exists(p + 2, PAIRS):
                            logit_squares(p + 2, j, 1)

                    pipelined(pe, turn, PAIRS)
                    project_heads(PAIRS - 1, 1)

                    pe.wait_ge(out1_added, PAIRS + 1)
                    first_keys(pe, 0)

                    turn_tokens(1)
                    pe.wait_ge(y_copied, 4)
                    for b in range(B):
                        twice = T2[:, b, :, :].rearrange("p a n -> p (a n)")
                        mm = nc.tensor.matmul(PS[:, 2 + b // 4, 128 * (b % 4):128 * (b % 4) + 128], twice, MAT["Wqk_c"],
                                              start=True, stop=True)
                        if b % 4 == 3:
                            mm.then_inc(qkc_projected, 1)
                    pe.wait_ge(k_ready, KC)
                    for c in range(2):
                        nc.tensor.matmul(PS[:, 6 + c, :], MAT["Wv_c"], T2[:, 8 * c:8 * c + 8, 0, :], start=True, stop=True
                                         ).then_inc(vc_projected, 1)
                    for b in range(B):
                        if b % 4 == 0:
                            pe.wait_ge(squares_ready, b // 4 + 1)
                            pe.wait_ge(upper_ready, b // 4 + 1)
                        r = slice(0, PITCH + N)
                        mm = nc.tensor.matmul(PS[:, b // 4, 128 * (b % 4):128 * (b % 4) + 128], gram_left[r, b, :],
                                              gram_right[r, b, :], start=True, stop=True)
                        if b % 8 == 7:
                            mm.then_inc(gram_done, 1)
                    pe.wait_ge(vc_ready, 2)
                    for c in range(2):
                        project_values(pe, 0, 0, 0, c, (SPARE, MISC)[c])
                    for c in range(2):
                        pe.wait_ge(gram_ready, c + 1)
                        for g in range(8 * c, 8 * c + 8):
                            last = nc.tensor.matmul(PS[:, g // 4, 128 * (g % 4):128 * (g % 4) + 128], gram[:, g, :],
                                                    wo_scaled[:, 1, :], start=True, stop=True)
                        last.then_inc(mixed, 1)
                    pe.wait_ge(mixed_copied, 2)
                    pe.wait_ge(vc_ready, 2)
                    for c in range(2):
                        for p in range(4 * c, 4 * c + 4):
                            for e in range(2):
                                last = nc.tensor.matmul(
                                    PS[PITCH * e:PITCH * e + PITCH, 4 + c, 128 * (p % 4):128 * (p % 4) + 128],
                                    qkT[:, 128 * p + PITCH * e:128 * p + PITCH * e + PITCH], gram[:, 2 * p + e, :],
                                    start=True, stop=True)
                        last.then_inc(outc_done, 1)
                    pe.wait_ge(v_ready, 1)
                    project_values(pe, 0, 0, 0, 2, SPARE)

        w_gate_up = sb("w_gate_up", [128, 2, 2 * I])
        w_down = sb("w_down", [128, 2, IT, D])
        gate_up_loaded = [sem("gate_up_loaded_0"), sem("gate_up_loaded_1")]
        down_loaded = [sem("down_loaded_0"), sem("down_loaded_1")]

        def load_gate_up(sp, e, j):
            sp.dma_start(w_gate_up[:, j, :], wgu_in[bass.ds(e, 1), :, :].rearrange("a p n -> p (a n)")
                         ).then_inc(gate_up_loaded[j], 16)

        def load_down(sp, e, j):
            sp.dma_start(w_down[:, j, :, :], wd_in[bass.ds(e, 1), :, :, :].rearrange("a p t n -> p (a t) n")
                         ).then_inc(down_loaded[j], 16)

        s2 = ExitStack()

        def sb2(name, shape, dt=F32):
            return s2.enter_context(nc.sbuf_tensor(name, shape, dt))

        with s2:
            MAX_SLOTS = [3, 2, 3, 2, 3, 2, 1, 2, 1, 2, 0, 0]
            KEY_SLOTS, VALUE_SLOTS, STACK_SLOTS, DEN_SLOT, OUT_SLOT = [0, 2, 4], [1, 3, 5], [8, 11], 6, 10
            HALF_TILES = [slice(0, -(-HALF // 128)), slice(-(-HALF // 128), QT7)]
            assert sum(MAX_SLOTS) == QT7 * KC

            def max_bank(b, j, n):
                return 4 + (j + n) % 2 if later(b, 1) else (n + 4) % 6

            def max_chunks(t):
                n = list(range(sum(MAX_SLOTS[:t]), sum(MAX_SLOTS[:t + 1])))
                return n[:1], n[1:]
            STACK_DMAS = 3 * GROUPS

            q_all = sb2("q_all", [128, B * PITCH])
            Y2 = q_all[:, :].rearrange("p (a d) -> p a d", a=PAIRS)
            q_hi = sb2("q_hi", [128, B * PITCH], F32R)
            q_lo = sb2("q_lo", [128, B * PITCH], F32R)
            k_stack = sb2("k_stack", [SHIFT_ROW + 1, 2, GROUPS, S], F32R)
            q_block_hi = sb2("q_block_hi", [128, 2, HQ], F32R)
            q_block_lo = sb2("q_block_lo", [128, 2, HQ], F32R)
            q_stack = sb2("q_stack", [128, 2, HQ], F32R)
            chunk_max = sb2("chunk_max", [128, QT7, KC])
            P = sb2("P", [KR, 3, HQ])
            ones_row = P[:, :, :].rearrange("p a n -> p (a n)")[0:1, 0:S]
            heads_sum = sb2("heads_sum", [128, 4 * N])
            heads_out2 = sb2("heads_out2", [128, 4 * N])

            y2_ready = sem("y2_ready")
            y2_turned = sem("y2_turned")
            y2_copied = sem("y2_copied")
            q_projected = sem("q_projected")
            q_split = sem("q_split")
            ones_ready = sem("ones_ready")
            ones_loaded = sem("ones_loaded")
            q_blocks = sem("q_blocks")
            q_selected = sem("q_selected")
            q_stacked = sem("q_stacked")
            max_taken = sem("max_taken")
            max_ready = sem("max_ready")
            s_done = sem("s_done")
            p_ready = sem("p_ready")
            o_copied = sem("o_copied")
            den_done = sem("den_done")
            den_inverted = sem("den_inverted")
            o_scaled = sem("o_scaled")
            out_done = sem("out_done")
            x2_ready = sem("x2_ready")

            OSUM = PS[:, 6, 0:4 * N]

            with nc.Block() as block:

                @block.sync
                def _(sp):
                    def load_stack(b, j):
                        if isinstance(b, int) and b < 2:
                            sp.wait_ge(k_lo_ready, KC * (b + 1))
                        else:
                            sp.wait_ge(s_done, KT * (b - 1))
                        for q, part in enumerate((k_hi, k_lo, k_hi)):
                            for g in range(GROUPS):
                                sp.dma_start(k_stack[32 * q:32 * q + 32, j, g, :].bitcast(F32),
                                             part[32 * g:32 * g + 32, j, :].bitcast(F32)).then_inc(stack_loaded[j], 16)

                    load_stack(0, 0)
                    sp.wait_ge(ones_ready, 1)
                    for j in range(2):
                        for g in range(GROUPS):
                            sp.dma_start(k_stack[SHIFT_ROW:SHIFT_ROW + 1, j, g, :].bitcast(F32), ones_row
                                         ).then_inc(ones_loaded, 16)

                    def period(b, j, u):
                        if exists(b + 2, B):
                            sp.wait_ge(cleared, 1)
                            sp.wait_ge(v_projected, KC * (b + 1))
                            load_ctx(sp, b + 2, j)
                        if exists(b + 1, B):
                            load_stack(b + 1, 1 - j)

                    pipelined(sp, period, B)
                    for e in range(2):
                        load_gate_up(sp, e, e)
                        load_down(sp, e, e)

                @block.gpsimd
                def _(pool):
                    nc.gpsimd.memset(ones_row, 1.0).then_inc(ones_ready, 1)
                    layernorm_power(pool, 3)
                    lower_keys(pool, 1, 1, 0)

                    def blocks(b, j):
                        for part, dst in ((q_hi, q_block_hi), (q_lo, q_block_lo)):
                            q = part[:, :].bitcast(F32).rearrange("p (b n) -> p b n", n=PITCH)[:, bass.ds(b, 1), 0:N]
                            nc.gpsimd.tensor_tensor(dst[:, j, :].rearrange("p (h n) -> p h n", h=H),
                                                    q.broadcast_to([128, H, N]),
                                                    C["head"].unsqueeze(2).broadcast_to([128, H, N]), ALU.mult
                                                    ).then_inc(q_blocks, 1)

                    pool.wait_ge(q_split, 1)
                    blocks(0, 0)
                    blocks(1, 1)
                    pool.wait_ge(q_split, 2)

                    def period(b, j, u):
                        if exists(b + 2, B):
                            pool.wait_ge(q_selected, 2 * (b + 1))
                            blocks(b + 2, j)
                            lower_keys(pool, b + 2, j, u + 1)

                    pipelined(pool, period, B)

                @block.scalar
                def _(act):
                    for c in range(KC):
                        read_keys(act, 1, 1, 0, c)
                    for c in range(2):
                        act.wait_ge(y2_turned, c + 1)
                        nc.scalar.copy(T[:, c * 512:(c + 1) * 512], PS[:, c, :]).then_inc(y2_copied, 1)

                    def stack_queries(b, j, a):
                        if a == 0 and later(b, 2):
                            act.wait_ge(s_done, KT * (b - 1))
                        act.wait_ge(q_selected, 2 * b + a + 1)
                        nc.scalar.copy(q_stack[:, j, a * HALF:(a + 1) * HALF], MISC[:, 0:HALF]).then_inc(q_stacked, 1)

                    def exps(b, t):
                        act.wait_ge(s_done, KT * b + t + 1)
                        if later(b, 1) or t >= 3:
                            act.wait_ge(pv_done, KT * b + t - 2)
                        nc.scalar.activation(P[:, t % 3, :].rearrange("p (a n) -> p a n", a=2),
                                             PS[0:KR, 2 * (t % 2):2 * (t % 2) + 2, 0:HALF], ACT.Exp).then_inc(p_ready, 1)

                    def copy_sums(b):
                        act.wait_ge(pv_done, KT * (b + 1))
                        act.wait_ge(o_scaled, b + 1)
                        nc.scalar.copy(heads_sum[:, :], OSUM).then_inc(o_copied, 1)

                    for a in range(2):
                        stack_queries(0, 0, a)

                    def period(b, j, u):
                        for t in range(KT):
                            exps(b, t)
                            if exists(b + 2, B) and t in KEY_SLOTS:
                                read_keys(act, b + 2, j, u + 1, KEY_SLOTS.index(t))
                            if exists(b + 1, B) and t in STACK_SLOTS:
                                stack_queries(b + 1, 1 - j, STACK_SLOTS.index(t))
                            if t == 0 and later(b, 1):
                                copy_sums(b - 1)

                    pipelined(act, period, B)
                    copy_sums(B - 1)

                @block.vector
                def _(dve):
                    step = steps_of["dve"].again(dve)
                    layernorm(dve, step, 3, X, Y2, y2_ready)
                    dve.wait_ge(y2_ready, 2)
                    nc.vector.tensor_tensor(X[:, :, :], X[:, :, :], ROW["bo"].unsqueeze(1).broadcast_to([128, PAIRS, D]),
                                            ALU.add).then_inc(o_scaled, 1)
                    projected = PS[:, 2:4, :].rearrange("p a n -> p (a n)")
                    for c, part in enumerate((slice(0, 2 * PITCH), slice(2 * PITCH, B * PITCH))):
                        dve.wait_ge(q_projected, c + 1)
                        step.mark(nc.vector.tensor_scalar(q_all[:, part], projected[:, part], COL["bq"], DH ** -0.5,
                                                          ALU.add, ALU.mult))
                        step.wait()
                        step.mark(nc.vector.tensor_copy(q_hi[:, part], q_all[:, part]))
                        step.wait()
                        nc.vector.tensor_tensor(q_lo[:, part], q_all[:, part], q_hi[:, part].bitcast(F32), ALU.subtract
                                                ).then_inc(q_split, 1)

                    def take_max(b, j, n):
                        dve.wait_ge(max_scored, QT7 * KC * b + n + 1)
                        nc.vector.tensor_reduce(out=chunk_max[:, n // KC, n % KC:n % KC + 1],
                                                in_=PS[:, max_bank(b, j, n), 0:KW], axis=AX.X, op=ALU.max
                                                ).then_inc(max_taken, 1)

                    def join_max(b, a):
                        tiles = HALF_TILES[a]
                        dve.wait_ge(max_taken, QT7 * KC * b + tiles.stop * KC)
                        if later(b, 1):
                            dve.wait_ge(q_selected, 2 * b)
                        nc.vector.tensor_reduce(out=max_col[:, tiles, SHIFT_ROW], in_=chunk_max[:, tiles, :], axis=AX.X,
                                                op=ALU.max).then_inc(max_ready, 1)

                    def take_chunks(b, j, chunks):
                        for n in chunks:
                            take_max(b, j, n)
                            for a in range(2):
                                if n == HALF_TILES[a].stop * KC - 1:
                                    join_max(b, a)

                    def invert(b, a):
                        half = slice(2 * N * a, 2 * N * a + 2 * N)
                        dve.wait_ge(den_done, b + 1)
                        nc.vector.reciprocal(heads_out2[:, half], MISC[:, half]).then_inc(den_inverted, 1)

                    def scale_heads(b):
                        dve.wait_ge(den_inverted, 2 * b + 2)
                        nc.vector.tensor_tensor(heads_out2[:, :], heads_out2[:, :], heads_sum[:, :], ALU.mult
                                                ).then_inc(o_scaled, 1)

                    def residual(b, j, u):
                        dve.wait_ge(out_done, b + 1)
                        r = slice(PITCH * j, PITCH * j + N)
                        nc.vector.tensor_tensor(X[r, bass.ds(u, 1), :], X[r, bass.ds(u, 1), :],
                                                MISC[r, 0:D].unsqueeze(1), ALU.add).then_inc(x2_ready, 1)

                    take_chunks(0, 0, range(QT7 * KC))

                    def period(b, j, u):
                        for t in range(KT):
                            first, rest = max_chunks(t)
                            if exists(b + 1, B):
                                take_chunks(b + 1, 1 - j, first)
                                if t in VALUE_SLOTS:
                                    read_values(dve, b + 1, 1 - j, VALUE_SLOTS.index(t))
                            if later(b, 1):
                                if DEN_SLOT <= t < DEN_SLOT + 2:
                                    invert(b - 1, t - DEN_SLOT)
                                if t == DEN_SLOT + 2:
                                    scale_heads(b - 1)
                                if t == OUT_SLOT:
                                    residual(b - 1, 1 - j, u if j == 1 else u - 1)
                            if exists(b + 1, B):
                                take_chunks(b + 1, 1 - j, rest)

                    pipelined(dve, period, B)
                    for a in range(2):
                        invert(B - 1, a)
                    scale_heads(B - 1)
                    residual(B - 1, 1, PAIRS - 1)

                @block.tensor
                def _(pe):
                    pe.wait_ge(v_ready, KC)
                    first_keys(pe, 1)
                    for c in range(2):
                        pe.wait_ge(y2_ready, c + 1)
                        for p in range(4):
                            last = nc.tensor.transpose(PS[:, c, 128 * p:128 * p + 128], Y2[:, 4 * c + p, :], C["ident"])
                        last.then_inc(y2_turned, 1)
                    for c in range(2):
                        pe.wait_ge(y2_copied, c + 1)
                        nc.tensor.matmul(PS[:, 2 + c, :], MAT["wq"], T[:, c * 512:(c + 1) * 512], start=True, stop=True
                                         ).then_inc(q_projected, 1)

                    released = [None]

                    def shared_bank(after):
                        if released[0]:
                            pe.wait_ge(*released[0])
                        released[0] = after

                    def max_scores(b, j, n):
                        if n == 0:
                            pe.wait_ge(q_blocks, 2 * b + 1)
                            pe.wait_ge(k_ready, KC * (b + 1))
                        if later(b, 1):
                            pe.wait_ge(max_taken, QT7 * KC * b + n - 1)
                        elif n == 4:
                            pe.wait_ge(q_split, 2)
                        elif n >= 6:
                            pe.wait_ge(max_taken, n - 5)
                        t, c = n // KC, n % KC
                        nc.tensor.matmul(PS[:, max_bank(b, j, n), 0:KW], q_block_hi[:, j, 128 * t:128 * t + 128],
                                         k_hi[:, j, KW * c:KW * c + KW], start=True, stop=True).then_inc(max_scored, 1)

                    def select_queries(b, j, a):
                        pe.wait_ge(q_blocks, 2 * b + 2)
                        pe.wait_ge(max_ready, 2 * b + a + 1)
                        shared_bank((q_stacked, 2 * b + a + 1))
                        cols_ = slice(a * HALF, (a + 1) * HALF)
                        nc.tensor.matmul(MISC[:, 0:HALF], sel[:, 0, :], q_block_hi[:, j, cols_], start=True, stop=False)
                        c0, c1 = a * HALF, (a + 1) * HALF
                        for t in range(QT7):
                            lo, hi = max(c0, 128 * t), min(c1, 128 * t + 128)
                            if lo < hi:
                                nc.tensor.matmul(MISC[:, lo - c0:hi - c0], max_col[:, t, :],
                                                 sel[:, 2, lo - 128 * t:hi - 128 * t], start=False, stop=False)
                        nc.tensor.matmul(MISC[:, 0:HALF], sel[:, 1, :], q_block_lo[:, j, cols_], start=False, stop=True
                                         ).then_inc(q_selected, 1)

                    def scores(b, j, u, t):
                        if t == 0:
                            pe.wait_ge(stack_loaded[j], 16 * STACK_DMAS * (u + 1))
                            pe.wait_ge(q_stacked, 2 * (b + 1))
                        if later(b, 1) or t >= 2:
                            pe.wait_ge(p_ready, KT * b + t - 1)
                        if t == KT - 1 and exists(b + 2, B):
                            pe.wait_ge(k_lo_ready, KC * (b + 3))
                        for g in range(GROUPS):
                            o = g % 2 * GH * N
                            last = nc.tensor.matmul(PS[0:KR, 2 * (t % 2) + g // 2, o:o + GH * N],
                                                    k_stack[:, j, g, KR * t:KR * t + KR],
                                                    q_stack[0:SHIFT_ROW + 1, j, g * GH * N:(g + 1) * GH * N],
                                                    start=True, stop=True)
                        last.then_inc(s_done, 1)

                    def weigh(b, j, t):
                        pe.wait_ge(p_ready, KT * b + t + 1)
                        if t == 0:
                            if later(b, 1):
                                pe.wait_ge(o_copied, b)
                            pe.wait_ge(v_ready, KC * (b + 1))
                        for r in range(2):
                            for k in range(4):
                                g = 4 * r + k
                                last = nc.tensor.matmul(PS[32 * k:32 * k + 32, 6, 2 * N * r:2 * N * r + 2 * N],
                                                        values[:, j, t, g, :], P[:, t % 3, 2 * N * g:2 * N * g + 2 * N],
                                                        start=(t == 0 and r == 0), stop=(t == KT - 1),
                                                        skip_group_check=True)
                        last.then_inc(pv_done, 1)

                    def denominators(b):
                        pe.wait_ge(o_copied, b + 1)
                        shared_bank((den_inverted, 2 * b + 2))
                        nc.tensor.matmul(MISC[:, 0:4 * N], C["den"], heads_sum[:, :], start=True, stop=True
                                         ).then_inc(den_done, 1)

                    def project_out(b, j):
                        pe.wait_ge(o_scaled, b + 2)
                        shared_bank((x2_ready, b + 1))
                        for n in range(4):
                            last = nc.tensor.matmul(MISC[PITCH * j:PITCH * j + N, 0:D], heads_out2[:, N * n:N * n + N],
                                                    MAT[f"wo{n}"], start=(n == 0), stop=(n == 3))
                        last.then_inc(out_done, 1)

                    pe.wait_ge(sel_ready, 1)
                    for n in range(QT7 * KC):
                        max_scores(0, 0, n)
                        if n == HALF_TILES[0].stop * KC + 5:
                            select_queries(0, 0, 0)
                    select_queries(0, 0, 1)
                    pe.wait_ge(ones_loaded, 16 * 2 * GROUPS)

                    def period(b, j, u):
                        released[0] = (q_stacked, 2 * (b + 1))
                        for t in range(KT):
                            first, rest = max_chunks(t)
                            scores(b, j, u, t)
                            if exists(b + 1, B):
                                for n in first:
                                    max_scores(b + 1, 1 - j, n)
                            if exists(b + 2, B) and t in KEY_SLOTS:
                                c = KEY_SLOTS.index(t)
                                shared_bank((k_ready, KC * (b + 2) + c + 1))
                                project_keys(pe, b + 2, j, u + 1, c)
                            if exists(b + 1, B) and t in VALUE_SLOTS:
                                c = VALUE_SLOTS.index(t)
                                shared_bank((v_ready, KC * (b + 1) + c + 1))
                                project_values(pe, b + 1, 1 - j, u if j == 0 else u + 1, c)
                            if later(b, 1):
                                if t == DEN_SLOT:
                                    denominators(b - 1)
                                if t == OUT_SLOT:
                                    project_out(b - 1, 1 - j)
                            if exists(b + 1, B):
                                if t in STACK_SLOTS:
                                    select_queries(b + 1, 1 - j, STACK_SLOTS.index(t))
                                for n in rest:
                                    max_scores(b + 1, 1 - j, n)
                            if t > 0:
                                weigh(b, j, t - 1)
                            elif later(b, 1):
                                weigh(b - 1, 1 - j, KT - 1)

                    pipelined(pe, period, B)
                    weigh(B - 1, 1, KT - 1)
                    denominators(B - 1)
                    project_out(B - 1, 1)


        s3 = ExitStack()

        def sb3(name, shape, dt=F32):
            return s3.enter_context(nc.sbuf_tensor(name, shape, dt))

        with s3:
            UNITS = 2 * IT
            Y3 = sb3("Y3", [128, PAIRS, D])
            w_hi = sb3("w_hi", [128, 2, 2 * I], F32R)
            w_lo = sb3("w_lo", [128, 2, 2 * I], F32R)
            X3 = sb3("X3", [128, TT, D])
            T3 = sb3("T3", [128, B * N])
            T_hi = sb3("T_hi", [128, B * N], F32R)
            T_lo = sb3("T_lo", [128, B * N], F32R)
            gated = sb3("gated", [128, 2, HALF])
            hidden = sb3("hidden", [128, 2, IT, B * N])
            logit = sb3("logit", [128, TT, E])
            beats = sb3("beats", [128, TT, E, E])
            ties = sb3("ties", [128, TT, E, E])
            rank = sb3("rank", [128, TT, E])
            best = sb3("best", [128, TT])
            weight = sb3("weight", [128, TT, E])
            weight_sum = sb3("weight_sum", [128, TT])
            weight_now = sb3("weight_now", [128, 2, TT])

            y3_ready = sem("y3_ready")
            y3_turned = sem("y3_turned")
            y3_copied = sem("y3_copied")
            t_split = sem("t_split")
            w_rounded = sem("w_rounded")
            w_split = sem("w_split")
            routed = sem("routed")
            route_shifted = sem("route_shifted")
            route_exp = sem("route_exp")
            moved = sem("moved")
            gate_done = sem("gate_done")
            up_done = sem("up_done")
            gated_ready = sem("gated_ready")
            hidden_ready = sem("hidden_ready")
            down_done = sem("down_done")
            weight_copied = sem("weight_copied")
            summed = sem("summed")
            FREE_BANKS = 4
            stored = sem("stored")

            def half_tiles(half):
                return range(4 * half, min(4 * half + 4, TT))

            moves = []
            for b in range(B):
                n = 0
                while n < N:
                    tile, row = divmod(N * b + n, 128)
                    size = min(N - n, 128 - row)
                    moves.append((b, n, tile, row, size))
                    n += size

            def experts(engine, body):
                body(0, 0, 0)
                with engine.Fori(0, (E - 2) // 2) as i:
                    body(2 * i + 1, 1, i)
                    body(2 * i + 2, 0, i + 1)
                body(E - 1, 1, E // 2 - 1)

            with nc.Block() as block:

                @block.sync
                def _(sp):
                    sp.wait_ge(y3_ready, 2)
                    for b, n, tile, row, size in moves:
                        r0 = PITCH * (b % 2) + n
                        sp.dma_start(X3[row:row + size, tile, :], X[r0:r0 + size, b // 2, :]).then_inc(moved, 16)

                    def period(e, j, u):
                        if not isinstance(e, int) or e + 1 < E:
                            if later(e, 1):
                                sp.wait_ge(y3_ready, 2)
                                sp.wait_ge(w_split, e)
                                load_gate_up(sp, e + 1, 1 - j)
                                sp.wait_ge(y3_ready, 2)
                                sp.wait_ge(down_done, 2 * e)
                                load_down(sp, e + 1, 1 - j)

                    experts(sp, period)
                    sp.wait_ge(summed, FREE_BANKS + 2 * E)
                    sp.dma_start(out, X3[:, :, :]).then_inc(stored, 16)
                    sp.wait_ge(stored, 16)

                @block.gpsimd
                def _(pool):

                    def split(e, j):
                        pool.wait_ge(w_rounded, e + 1)
                        nc.gpsimd.tensor_tensor(w_lo[:, j, :], w_gate_up[:, j, :], w_hi[:, j, :].bitcast(F32), ALU.subtract
                                                ).then_inc(w_split, 1)

                    layernorm_power(pool, 4)
                    split(0, 0)

                    def period(e, j, u):
                        if not isinstance(e, int) or e + 1 < E:
                            split(e + 1, 1 - j)

                    experts(pool, period)

                @block.scalar
                def _(act):
                    def round_weights(e, j, u):
                        if later(e, 2):
                            act.wait_ge(up_done, UNITS * (e - 1))
                        act.wait_ge(gate_up_loaded[j], 16 * (u + 1))
                        nc.scalar.copy(w_hi[:, j, :], w_gate_up[:, j, :]).then_inc(w_rounded, 1)

                    act.wait_ge(x2_ready, B)
                    round_weights(0, 0, 0)
                    for c in range(2):
                        act.wait_ge(y3_turned, c + 1)
                        rows_, part = slice(c * HALF, (c + 1) * HALF), PS[:, c, :].rearrange("p (b n) -> p b n", n=PITCH)
                        for dst in (T_hi, T3):
                            last = nc.scalar.copy(dst[:, rows_].rearrange("p (b n) -> p b n", n=N), part[:, :, 0:N])
                        last.then_inc(y3_copied, 1)

                    def period(e, j, u):
                        for k in range(UNITS):
                            act.wait_ge(gate_done, UNITS * e + k + 1)
                            if later(e, 1) or k >= 2:
                                act.wait_ge(hidden_ready, UNITS * e + k - 1)
                            nc.scalar.activation(gated[:, k % 2, :], PS[:, k % 2, 0:HALF], ACT.Silu
                                                 ).then_inc(gated_ready, 1)
                            if k == 3 and isinstance(e, int) and e == 0:
                                act.wait_ge(route_shifted, 1)
                                nc.scalar.activation(weight[:, :, :], weight[:, :, :], ACT.Exp).then_inc(route_exp, 1)
                            if k == 1 and (not isinstance(e, int) or e + 1 < E):
                                round_weights(e + 1, 1 - j, u if j == 0 else u + 1)

                    experts(act, period)

                @block.vector
                def _(dve):
                    step = steps_of["dve"].again(dve)
                    dve.wait_ge(x2_ready, B)
                    layernorm(dve, step, 4, X, Y3, y3_ready)

                    dve.wait_ge(y3_copied, 2)
                    for c in range(2):
                        part = slice(c * HALF, (c + 1) * HALF)
                        nc.vector.tensor_tensor(T_lo[:, part], T3[:, part], T_hi[:, part].bitcast(F32), ALU.subtract
                                                ).then_inc(*((summed, FREE_BANKS) if c == 0 else (t_split, 1)))

                    def route(k):
                        all_pairs = [128, TT, E, E]
                        if k == 0:
                            dve.wait_ge(routed, 1)
                            step.mark(nc.vector.tensor_copy(logit[:, :, :],
                                                            PS[:, 7, 0:TT * E].rearrange("p (a e) -> p a e", e=E)))
                            step.wait()
                            nc.vector.tensor_reduce(out=best[:, :], in_=logit[:, :, :], axis=AX.X, op=ALU.max)
                            other = logit[:, :, :].unsqueeze(2).broadcast_to(all_pairs)
                            own = logit[:, :, :].unsqueeze(3).broadcast_to(all_pairs)
                            nc.vector.tensor_tensor(beats[:, :, :, :], other, own, ALU.is_gt)
                            step.mark(nc.vector.tensor_tensor(ties[:, :, :, :], other, own, ALU.is_equal))
                        if k == 1:
                            step.wait()
                            nc.vector.tensor_tensor(weight[:, :, :], logit[:, :, :],
                                                    best[:, :].unsqueeze(2).broadcast_to([128, TT, E]), ALU.subtract
                                                    ).then_inc(route_shifted, 1)
                            before = C["before"].rearrange("p (e f) -> p e f", e=E).unsqueeze(1).broadcast_to(all_pairs)
                            step.mark(nc.vector.tensor_tensor(ties[:, :, :, :], ties[:, :, :, :], before, ALU.mult))
                        if k == 2:
                            step.wait()
                            step.mark(nc.vector.tensor_tensor(beats[:, :, :, :], beats[:, :, :, :], ties[:, :, :, :], ALU.add))
                        if k == 3:
                            step.wait()
                            step.mark(nc.vector.tensor_reduce(out=rank[:, :, :], in_=beats[:, :, :, :], axis=AX.X, op=ALU.add))
                        if k == 5:
                            step.wait()
                            dve.wait_ge(route_exp, 1)
                            step.mark(nc.vector.scalar_tensor_tensor(weight[:, :, :], rank[:, :, :], 2.0, weight[:, :, :],
                                                                     ALU.is_lt, ALU.mult))
                            step.wait()
                            step.mark(nc.vector.tensor_reduce(out=weight_sum[:, :], in_=weight[:, :, :], axis=AX.X, op=ALU.add))
                        if k == 6:
                            step.wait()
                            step.mark(nc.vector.reciprocal(weight_sum[:, :], weight_sum[:, :]))
                        if k == 7:
                            step.wait()
                            step.mark(nc.vector.tensor_tensor(weight[:, :, :], weight[:, :, :],
                                                              weight_sum[:, :].unsqueeze(2).broadcast_to([128, TT, E]), ALU.mult))
                            step.wait()
                            dve.wait_ge(moved, 16 * len(moves))

                    def add_outputs(e, j, half):
                        if half == 0:
                            dve.wait_ge(summed, FREE_BANKS + 2 * e)
                            nc.vector.tensor_copy(weight_now[:, j, :], weight[:, :, bass.ds(e, 1)].rearrange("p a e -> p (a e)")
                                                  ).then_inc(weight_copied, 1)
                            dve.wait_ge(weight_copied, e + 1)
                        dve.wait_ge(down_done, 2 * e + half + 1)
                        dve.wait_ge(summed, FREE_BANKS + 2 * e + half - 1)
                        for p in half_tiles(half):
                            last = nc.vector.scalar_tensor_tensor(
                                X3[:, p, :], PS[:, 4 + 2 * j + half, 128 * (p % 4):128 * (p % 4) + 128],
                                weight_now[:, j, p:p + 1], X3[:, p, :], ALU.mult, ALU.add)
                        last.then_inc(summed, 1)

                    def period(e, j, u):
                        for k in range(UNITS):
                            c, t = k // IT, k % IT
                            dve.wait_ge(gated_ready, UNITS * e + k + 1)
                            dve.wait_ge(up_done, UNITS * e + k + 1)
                            nc.vector.tensor_tensor(
                                hidden[:, j, t, c * HALF:(c + 1) * HALF], gated[:, k % 2, :], PS[:, 2 + k % 2, 0:HALF],
                                ALU.mult).then_inc(hidden_ready, 1)
                            if isinstance(e, int) and e == 0:
                                route(k)
                            if later(e, 1) and k % 4 == 3:
                                add_outputs(e - 1, 1 - j, k // 4)

                    experts(dve, period)
                    for half in range(2):
                        add_outputs(E - 1, 1, half)

                @block.tensor
                def _(pe):
                    for c in range(2):
                        pe.wait_ge(y3_ready, c + 1)
                        for p in range(4):
                            last = nc.tensor.transpose(PS[:, c, 128 * p:128 * p + 128], Y3[:, 4 * c + p, :], C["ident"])
                        last.then_inc(y3_turned, 1)
                    pe.wait_ge(y3_copied, 2)
                    for p in range(TT):
                        last = nc.tensor.matmul(PS[:, 7, E * p:E * p + E], T3[:, 128 * p:128 * p + 128], gate[:, :],
                                                start=True, stop=True)
                    last.then_inc(routed, 1)
                    pe.wait_ge(t_split, 1)

                    def down(e, j, p):
                        if p == 0:
                            pe.wait_ge(hidden_ready, UNITS * e + IT)
                            pe.wait_ge(down_loaded[j], 16 * (down_turn[0] + 1))
                        if p == 3:
                            pe.wait_ge(hidden_ready, UNITS * (e + 1))
                        if p % 4 == 0:
                            pe.wait_ge(summed, 2 * e + p // 4 + 1)
                        for t in range(IT):
                            last = nc.tensor.matmul(PS[:, 4 + 2 * j + p // 4, 128 * (p % 4):128 * (p % 4) + 128],
                                                    hidden[:, j, t, 128 * p:128 * p + 128], w_down[:, j, t, :],
                                                    start=(t == 0), stop=(t == IT - 1))
                        if p in (3, TT - 1):
                            last.then_inc(down_done, 1)

                    down_turn = [0]

                    def period(e, j, u):
                        down_turn[0] = u if j == 1 else u - 1
                        pe.wait_ge(w_split, e + 1)
                        for k in range(UNITS):
                            c, t = k // IT, k % IT
                            if later(e, 1) or k >= 2:
                                pe.wait_ge(hidden_ready, UNITS * e + k - 1)
                            for side, done in ((0, gate_done), (1, up_done)):
                                w = slice(I * side + 128 * t, I * side + 128 * t + 128)
                                bank = PS[:, 2 * side + k % 2, 0:HALF]
                                hi, lo = (part[:, c * HALF:(c + 1) * HALF] for part in (T_hi, T_lo))
                                nc.tensor.matmul(bank, w_hi[:, j, w], hi, start=True, stop=False)
                                nc.tensor.matmul(bank, w_hi[:, j, w], lo, start=False, stop=False)
                                nc.tensor.matmul(bank, w_lo[:, j, w], hi, start=False, stop=True).then_inc(done, 1)
                            if later(e, 1) and k < TT:
                                down(e - 1, 1 - j, k)

                    experts(pe, period)
                    down_turn[0] = E // 2 - 1
                    for p in range(TT):
                        down(E - 1, 1, p)


def lay_out(a):
    a = {k: np.asarray(v) for k, v in a.items()}
    f = np.float32
    x = np.zeros((128, PAIRS, D), f)
    for e in range(2):
        x[PITCH * e:PITCH * e + N] = a["x"][e::2].transpose(1, 0, 2)
    wo_t = a["L0_xattn_wo"].T.reshape(2, 4, 2, DH, D)
    wo = np.zeros((2, 2, 4, 32, D), f)
    for r in range(2):
        for e in range(2):
            wo[r, e, :, DH * e:DH * e + DH] = wo_t[r, :, e]
    wo = wo.reshape(4, 128, D)
    mats = [a["L0_attn_" + n] for n in MATS[:6]] + [a["L0_xattn_" + n].T for n in MATS[6:9]] + list(wo)
    mats = np.ascontiguousarray(np.stack(mats, axis=1))
    rows = np.stack([a["L0_attn_gamma1"], a["L0_attn_gamma2"], a["L0_xattn_bv"], a["L0_xattn_bo"]])
    rows = np.ascontiguousarray(np.broadcast_to(rows, (128, 4, D)))
    cols = np.stack([a["L0_attn_ln1_w"], a["L0_attn_ln1_b"], a["L0_attn_ln2_w"], a["L0_attn_ln2_b"],
                     a["L0_xattn_bq"], a["L0_xattn_bk"],
                     np.repeat(a["L0_attn_tau_t"].reshape(H), DH), np.repeat(a["L0_attn_tau_c"].reshape(CH), CD)], axis=1)
    wgu = np.concatenate([a["L0_ffn_wg"].transpose(0, 2, 1), a["L0_ffn_wu"].transpose(0, 2, 1)], axis=2)
    wd = a["L0_ffn_wd"].reshape(E, D, IT, 128).transpose(0, 3, 2, 1)
    return {"x_in": x, "ctx_in": np.ascontiguousarray(a["ctx_1024"].transpose(0, 2, 1)), "mats_in": mats, "rows_in": rows,
            "cols_in": np.ascontiguousarray(cols), "gate_in": np.ascontiguousarray(a["L0_ffn_gate_w"].T),
            "consts_in": shape_constants()[0], "wgu_in": np.ascontiguousarray(wgu), "wd_in": np.ascontiguousarray(wd)}


def program(nc, arrays):
    args = {k: nc.dram_tensor(k, v.shape, mybir.dt.from_np(v.dtype), kind="ExternalInput").ap() for k, v in arrays.items()}
    out = nc.dram_tensor("out", (128, TT, D), F32, kind="ExternalOutput").ap()
    build(nc, const_at=shape_constants()[1], out=out, **args)


def kernel(**inputs):
    import concourse.bacc as bacc
    from concourse.bass_utils import run_bass_kernel_spmd

    nc = bacc.Bacc("TRN2", target_bir_lowering=False, num_devices=1)
    arrays = lay_out(inputs)
    program(nc, arrays)
    got = run_bass_kernel_spmd(nc, [arrays], core_ids=[0]).results[0]["out"]
    return np.ascontiguousarray(got.transpose(1, 0, 2)).reshape(B, N, D)
```
